# Optimizing a Trainium2 kernel written in Bass

```python
import numpy as np
import jax
import jax.numpy as jnp

def _softmax(x, axis=-1):
    return jax.nn.softmax(x, axis=axis)

def _gelu(x):
    return jax.nn.gelu(x, approximate=True)

def _silu(x):
    return jax.nn.silu(x)

def _sigmoid(x):
    return jax.nn.sigmoid(x)

def _layernorm(x, axis=-1, eps=1e-05):
    m = jnp.mean(x, axis=axis, keepdims=True)
    v = jnp.var(x, axis=axis, keepdims=True)
    return (x - m) / jnp.sqrt(v + eps)

def _scatter_add(tgt, idx, src, axis=0):
    return tgt.at[idx].add(src)

def _segment_sum(src, seg, n):
    return jax.ops.segment_sum(src, seg, n)
kernel_name = 'mk_hybrid_d1_jaxref_r8_05103f'

def setup_inputs(seed: int=0):
    np.random.seed(seed)
    _w = jnp.asarray

    def _L0_attn_a_setup():
        import jax, jax.numpy as jnp
        import numpy as np
        HIDDEN = 128
        N_HEADS = 16
        WINDOW = 64
        ROPE_BASE = 10000.0
        BATCH = 1
        SEQ = 1024

        def _rope(x, base=ROPE_BASE):
            B, S, D = x.shape
            half = D // 2
            inv_freq = 1.0 / base ** (jnp.arange(half, dtype=jnp.float32) / half)
            ang = jnp.arange(S, dtype=jnp.float32)[:, None] * inv_freq[None, :]
            cos, sin = (jnp.cos(ang), jnp.sin(ang))
            x1, x2 = (x[..., :half], x[..., half:])
            return jnp.concatenate([x1 * cos - x2 * sin, x1 * sin + x2 * cos], axis=-1)

        def _banded_attention(q, k, v, window):
            B, H, S, Dh = q.shape
            Wb = window
            nb = S // Wb
            scale = 1.0 / jnp.sqrt(jnp.asarray(Dh, q.dtype))
            qb = q.reshape(B, H, nb, Wb, Dh)
            kb = k.reshape(B, H, nb, Wb, Dh)
            vb = v.reshape(B, H, nb, Wb, Dh)
            zpad = [(0, 0), (0, 0), (1, 0), (0, 0), (0, 0)]
            k_prev = jnp.pad(kb, zpad)[:, :, :nb]
            v_prev = jnp.pad(vb, zpad)[:, :, :nb]
            k_ctx = jnp.concatenate([k_prev, kb], axis=3)
            v_ctx = jnp.concatenate([v_prev, vb], axis=3)
            scores = jnp.einsum('bhnqd,bhnkd->bhnqk', qb, k_ctx) * scale
            i = jnp.arange(Wb)[:, None]
            j = jnp.arange(2 * Wb)[None, :]
            band = (j >= i) & (j <= i + Wb)
            kv_glob = (jnp.arange(nb)[:, None, None] - 1) * Wb + j[None]
            mask = band[None] & (kv_glob >= 0)
            scores = jnp.where(mask[None, None], scores, jnp.finfo(scores.dtype).min)
            probs = jax.nn.softmax(scores, axis=-1)
            out = jnp.einsum('bhnqk,bhnkd->bhnqd', probs, v_ctx)
            return out.reshape(B, H, S, Dh)
        key = jax.random.key(seed)
        ks = jax.random.split(key, 9)
        s = 1.0 / np.sqrt(HIDDEN)
        return {'hidden_state': jax.random.normal(ks[0], (BATCH, SEQ, HIDDEN), jnp.float32), 'Wq': jax.random.uniform(ks[1], (HIDDEN, HIDDEN), jnp.float32, -s, s), 'bq': jnp.zeros((HIDDEN,), jnp.float32), 'Wk': jax.random.uniform(ks[2], (HIDDEN, HIDDEN), jnp.float32, -s, s), 'bk': jnp.zeros((HIDDEN,), jnp.float32), 'Wv': jax.random.uniform(ks[3], (HIDDEN, HIDDEN), jnp.float32, -s, s), 'bv': jnp.zeros((HIDDEN,), jnp.float32), 'Wo': jax.random.uniform(ks[4], (HIDDEN, HIDDEN), jnp.float32, -s, s), 'bo': jnp.zeros((HIDDEN,), jnp.float32)}
    _L0_attn_a_in = _L0_attn_a_setup()

    def _L0_attn_b_setup():
        import jax, jax.numpy as jnp
        import numpy as np
        RSQRT2 = 2 ** (-0.5)
        B, S, D_IN = (2, 512, 128)
        H, D_HEAD = (8, 64)
        QK_DIM = H * D_HEAD
        V_DIM = H * D_HEAD
        OUT_DIM = D_IN
        LN_EPS = 1e-05

        def _layernorm(y, gamma, beta):
            mu = jnp.mean(y, axis=-1, keepdims=True)
            var = jnp.mean(jnp.square(y - mu), axis=-1, keepdims=True)
            return (y - mu) * jax.lax.rsqrt(var + LN_EPS) * gamma + beta
        key = jax.random.key(seed)
        ks = jax.random.split(key, 8)

        def lecun(k, fan_in, shape):
            return jax.random.normal(k, shape, dtype=jnp.float32) * (1.0 / np.sqrt(fan_in))
        return {'x': jax.random.normal(ks[0], (B, S, D_IN), dtype=jnp.float32), 'W_qk': lecun(ks[1], D_IN, (D_IN, 2 * QK_DIM)), 'b_qk': jnp.zeros((2 * QK_DIM,), jnp.float32), 'W_v': lecun(ks[2], D_IN, (D_IN, V_DIM)), 'b_v': jnp.zeros((V_DIM,), jnp.float32), 'W_out': lecun(ks[3], V_DIM, (V_DIM, OUT_DIM)), 'b_out': jnp.zeros((OUT_DIM,), jnp.float32), 'ln_gamma': jnp.ones((OUT_DIM,), jnp.float32), 'ln_beta': jnp.zeros((OUT_DIM,), jnp.float32)}
    _L0_attn_b_in = _L0_attn_b_setup()

    def _L0_ffn_setup():
        import jax, jax.numpy as jnp
        import numpy as np
        B, S, H, F, E, K = (4, 512, 128, 512, 8, 2)
        LN_EPS = 1e-05
        key = jax.random.key(seed)
        kx, kr, k1, k2 = jax.random.split(key, 4)
        x = jax.random.normal(kx, (B, S, H), dtype=jnp.float32)
        gamma = jnp.ones((H,), jnp.float32)
        beta = jnp.zeros((H,), jnp.float32)
        Wr = jax.random.normal(kr, (H, E), jnp.float32) * 0.02
        br = jnp.zeros((E,), jnp.float32)
        W1 = jax.random.normal(k1, (E, H, F), jnp.float32) * (1.0 / np.sqrt(H))
        b1 = jnp.zeros((E, F), jnp.float32)
        W2 = jax.random.normal(k2, (E, F, H), jnp.float32) * (1.0 / np.sqrt(F))
        b2 = jnp.zeros((E, H), jnp.float32)
        return {'x': x, 'gamma': gamma, 'beta': beta, 'Wr': Wr, 'br': br, 'W1': W1, 'b1': b1, 'W2': W2, 'b2': b2}
    _L0_ffn_in = _L0_ffn_setup()
    _d = {'L0_attn_a_hidden_state': _L0_attn_a_in['hidden_state'], 'L0_attn_a_Wq': _L0_attn_a_in['Wq'], 'L0_attn_a_bq': _L0_attn_a_in['bq'], 'L0_attn_a_Wk': _L0_attn_a_in['Wk'], 'L0_attn_a_bk': _L0_attn_a_in['bk'], 'L0_attn_a_Wv': _L0_attn_a_in['Wv'], 'L0_attn_a_bv': _L0_attn_a_in['bv'], 'L0_attn_a_Wo': _L0_attn_a_in['Wo'], 'L0_attn_a_bo': _L0_attn_a_in['bo'], 'L0_attn_b_W_qk': _L0_attn_b_in['W_qk'], 'L0_attn_b_b_qk': _L0_attn_b_in['b_qk'], 'L0_attn_b_W_v': _L0_attn_b_in['W_v'], 'L0_attn_b_b_v': _L0_attn_b_in['b_v'], 'L0_attn_b_W_out': _L0_attn_b_in['W_out'], 'L0_attn_b_b_out': _L0_attn_b_in['b_out'], 'L0_attn_b_ln_gamma': _L0_attn_b_in['ln_gamma'], 'L0_attn_b_ln_beta': _L0_attn_b_in['ln_beta'], 'L0_ffn_gamma': _L0_ffn_in['gamma'], 'L0_ffn_beta': _L0_ffn_in['beta'], 'L0_ffn_Wr': _L0_ffn_in['Wr'], 'L0_ffn_br': _L0_ffn_in['br'], 'L0_ffn_W1': _L0_ffn_in['W1'], 'L0_ffn_b1': _L0_ffn_in['b1'], 'L0_ffn_W2': _L0_ffn_in['W2'], 'L0_ffn_b2': _L0_ffn_in['b2']}
    _x0 = _d['L0_attn_a_hidden_state']
    _d['L0_attn_a_hidden_state'] = jax.random.normal(jax.random.fold_in(jax.random.key(seed), 1), (4, 1024, 128), dtype=_x0.dtype)
    del _x0
    return _d

def reference(L0_attn_a_hidden_state, L0_attn_a_Wq, L0_attn_a_bq, L0_attn_a_Wk, L0_attn_a_bk, L0_attn_a_Wv, L0_attn_a_bv, L0_attn_a_Wo, L0_attn_a_bo, L0_attn_b_W_qk, L0_attn_b_b_qk, L0_attn_b_W_v, L0_attn_b_b_v, L0_attn_b_W_out, L0_attn_b_b_out, L0_attn_b_ln_gamma, L0_attn_b_ln_beta, L0_ffn_gamma, L0_ffn_beta, L0_ffn_Wr, L0_ffn_br, L0_ffn_W1, L0_ffn_b1, L0_ffn_W2, L0_ffn_b2):

    def _L0_attn_a_ref(hidden_state, Wq, bq, Wk, bk, Wv, bv, Wo, bo):
        import jax, jax.numpy as jnp
        import numpy as np
        HIDDEN = 128
        N_HEADS = 16
        WINDOW = 64
        ROPE_BASE = 10000.0
        BATCH = 1
        SEQ = 1024

        def _rope(x, base=ROPE_BASE):
            B, S, D = x.shape
            half = D // 2
            inv_freq = 1.0 / base ** (jnp.arange(half, dtype=jnp.float32) / half)
            ang = jnp.arange(S, dtype=jnp.float32)[:, None] * inv_freq[None, :]
            cos, sin = (jnp.cos(ang), jnp.sin(ang))
            x1, x2 = (x[..., :half], x[..., half:])
            return jnp.concatenate([x1 * cos - x2 * sin, x1 * sin + x2 * cos], axis=-1)

        def _banded_attention(q, k, v, window):
            B, H, S, Dh = q.shape
            Wb = window
            nb = S // Wb
            scale = 1.0 / jnp.sqrt(jnp.asarray(Dh, q.dtype))
            qb = q.reshape(B, H, nb, Wb, Dh)
            kb = k.reshape(B, H, nb, Wb, Dh)
            vb = v.reshape(B, H, nb, Wb, Dh)
            zpad = [(0, 0), (0, 0), (1, 0), (0, 0), (0, 0)]
            k_prev = jnp.pad(kb, zpad)[:, :, :nb]
            v_prev = jnp.pad(vb, zpad)[:, :, :nb]
            k_ctx = jnp.concatenate([k_prev, kb], axis=3)
            v_ctx = jnp.concatenate([v_prev, vb], axis=3)
            scores = jnp.einsum('bhnqd,bhnkd->bhnqk', qb, k_ctx) * scale
            i = jnp.arange(Wb)[:, None]
            j = jnp.arange(2 * Wb)[None, :]
            band = (j >= i) & (j <= i + Wb)
            kv_glob = (jnp.arange(nb)[:, None, None] - 1) * Wb + j[None]
            mask = band[None] & (kv_glob >= 0)
            scores = jnp.where(mask[None, None], scores, jnp.finfo(scores.dtype).min)
            probs = jax.nn.softmax(scores, axis=-1)
            out = jnp.einsum('bhnqk,bhnkd->bhnqd', probs, v_ctx)
            return out.reshape(B, H, S, Dh)
        B, S, D = hidden_state.shape
        Dh = D // N_HEADS
        q = hidden_state @ Wq.T + bq
        k = hidden_state @ Wk.T + bk
        v = hidden_state @ Wv.T + bv
        q = _rope(q)
        k = _rope(k)
        split = lambda x: x.reshape(B, S, N_HEADS, Dh).transpose(0, 2, 1, 3)
        out = _banded_attention(split(q), split(k), split(v), WINDOW)
        out = out.transpose(0, 2, 1, 3).reshape(B, S, D)
        return out @ Wo.T + bo

    def _L0_attn_b_ref(x, W_qk, b_qk, W_v, b_v, W_out, b_out, ln_gamma, ln_beta):
        import jax, jax.numpy as jnp
        import numpy as np
        RSQRT2 = 2 ** (-0.5)
        B, S, D_IN = (2, 512, 128)
        H, D_HEAD = (8, 64)
        QK_DIM = H * D_HEAD
        V_DIM = H * D_HEAD
        OUT_DIM = D_IN
        LN_EPS = 1e-05

        def _layernorm(y, gamma, beta):
            mu = jnp.mean(y, axis=-1, keepdims=True)
            var = jnp.mean(jnp.square(y - mu), axis=-1, keepdims=True)
            return (y - mu) * jax.lax.rsqrt(var + LN_EPS) * gamma + beta
        b, s, _ = x.shape
        scale = D_HEAD ** (-0.5)
        qk = x @ W_qk + b_qk
        qk = qk.reshape(b, s, H, D_HEAD, 2)
        q, k = (qk[..., 0], qk[..., 1])
        v = (x @ W_v + b_v).reshape(b, s, H, D_HEAD)
        sim = jnp.einsum('bihd,bjhd->bhij', q, k) * scale
        attn = jax.nn.softmax(sim, axis=-1)
        o = jnp.einsum('bhij,bjhd->bihd', attn, v)
        o = o.reshape(b, s, V_DIM)
        y = _layernorm(o @ W_out + b_out, ln_gamma, ln_beta)
        return (y + x) * RSQRT2

    def _L0_ffn_ref(x, gamma, beta, Wr, br, W1, b1, W2, b2):
        import jax, jax.numpy as jnp
        import numpy as np
        B, S, H, F, E, K = (4, 512, 128, 512, 8, 2)
        LN_EPS = 1e-05
        residual = x
        mu = jnp.mean(x, axis=-1, keepdims=True)
        var = jnp.var(x, axis=-1, keepdims=True)
        xn = (x - mu) * jax.lax.rsqrt(var + LN_EPS) * gamma + beta
        probs = jax.nn.softmax(xn @ Wr + br, axis=-1)
        scores, idx = jax.lax.top_k(probs, K)

        def expert_fn(w):
            W1_e, b1_e, W2_e, b2_e = w
            return jax.nn.relu(xn @ W1_e + b1_e) @ W2_e + b2_e
        full = jax.lax.map(expert_fn, (W1, b1, W2, b2))
        full = jnp.moveaxis(full, 0, 2)
        c = jnp.einsum('ef,efh->eh', jax.nn.relu(b1), W2) + b2
        c_total = c.sum(axis=0)
        sel_full = jnp.take_along_axis(full, idx[..., None], axis=2)
        c_sel = c[idx]
        output = jnp.sum(scores[..., None] * (sel_full - c_sel + c_total), axis=2)
        return residual + output
    x = L0_attn_a_hidden_state
    x = x + _L0_attn_a_ref(_layernorm(x, axis=-1), L0_attn_a_Wq, L0_attn_a_bq, L0_attn_a_Wk, L0_attn_a_bk, L0_attn_a_Wv, L0_attn_a_bv, L0_attn_a_Wo, L0_attn_a_bo)
    x = x + _L0_ffn_ref(_layernorm(x, axis=-1), L0_ffn_gamma, L0_ffn_beta, L0_ffn_Wr, L0_ffn_br, L0_ffn_W1, L0_ffn_b1, L0_ffn_W2, L0_ffn_b2)
    x = x + _L0_attn_b_ref(_layernorm(x, axis=-1), L0_attn_b_W_qk, L0_attn_b_b_qk, L0_attn_b_W_v, L0_attn_b_b_v, L0_attn_b_W_out, L0_attn_b_b_out, L0_attn_b_ln_gamma, L0_attn_b_ln_beta)
    x = x + _L0_ffn_ref(_layernorm(x, axis=-1), L0_ffn_gamma, L0_ffn_beta, L0_ffn_Wr, L0_ffn_br, L0_ffn_W1, L0_ffn_b1, L0_ffn_W2, L0_ffn_b2)
    return x

_drawn_inputs = setup_inputs


def setup_inputs(seed=0):
    import zlib

    import numpy as np

    out = dict(_drawn_inputs(seed))
    spreads = {'L0_attn_a_bq': (0.0, 0.8),
     'L0_attn_a_bk': (0.0, 0.8),
     'L0_attn_a_bv': (0.0, 0.1),
     'L0_attn_a_bo': (0.0, 0.1),
     'L0_attn_b_b_qk': (0.0, 0.638),
     'L0_attn_b_b_v': (0.0, 0.1),
     'L0_attn_b_b_out': (0.0, 0.1),
     'L0_attn_b_ln_gamma': (1.0, 0.2),
     'L0_attn_b_ln_beta': (0.0, 0.284),
     'L0_ffn_gamma': (1.0, 0.2),
     'L0_ffn_beta': (0.0, 0.1),
     'L0_ffn_br': (0.0, 0.1),
     'L0_ffn_b1': (0.0, 0.1),
     'L0_ffn_b2': (0.0, 0.1)}
    factors = {'L0_attn_a_Wq': 2.903, 'L0_attn_a_Wk': 2.872}
    for name, (base, spread) in spreads.items():
        noise = np.random.default_rng([zlib.crc32(name.encode()), seed]).standard_normal(out[name].shape)
        drawn = base * np.exp(spread * noise) if base else spread * noise
        out[name] = jnp.asarray(drawn.astype(out[name].dtype))
    for name, factor in factors.items():
        out[name] = (out[name] * factor).astype(out[name].dtype)
    return out
```

```python
from contextlib import ExitStack

import numpy as np

import concourse.bass as bass
from concourse import mybir

F32 = mybir.dt.float32
F16 = mybir.dt.float16
BF16 = mybir.dt.bfloat16
ALU = mybir.AluOpType
ACT = mybir.ActivationFunctionType
AX_X = mybir.AxisListType.X
ds = bass.ds

P = 128
D = 128
B, S = 4, 1024
T = B * S
NT = T // P
CH = 512
NCH = T // CH
TPC = CH // P
EPS = 1e-5

HA, DA = 16, 8
WIN = 64
NB = T // WIN
SCALE_A = 1.0 / float(np.sqrt(np.float32(DA)))
VW = DA + 1

HB, DB = 8, 64
SCALE_B = DB ** -0.5
KT = S // P
RSQRT2 = 2 ** -0.5

NE, FF = 8, 512
FC = FF // P
WS = 64.0



class Stage:

    def __init__(self, nc, tag):
        self.nc, self.tag, self.ctx, self.sems = nc, tag, ExitStack(), []

    def __enter__(self):
        self.ctx.__enter__()
        return self

    def __exit__(self, *e):
        if self.sems:
            self.nc.clear_and_free_semaphores(self.sems)
            self.nc.all_engine_barrier()
        return self.ctx.__exit__(*e)

    def sb(self, name, shape, dt=F32):
        return self.ctx.enter_context(self.nc.sbuf_tensor(f"{self.tag}_{name}", shape, dt))

    def ps(self, name, shape, dt=F32):
        return self.ctx.enter_context(self.nc.psum_tensor(f"{self.tag}_{name}", shape, dt))

    def sem(self, name):
        self.sems.append(self.nc.alloc_semaphore(name=f"{self.tag}_{name}"))
        return self.sems[-1]

    def block(self):
        return self.nc.Block()


def band_project(nc, X, Q4, K4, Vhi, Vlo, io):
    with Stage(nc, "a1") as st:
        sb, ps, sem = st.sb, st.ps, st.sem
        w32, whi, wlo = sb("w32", [P, 5, D]), sb("whi", [P, 5, D], F16), sb("wlo", [P, 5, D], F16)
        bias = sb("bias", [P, 4])
        bvb = sb("bvb", [P, D])
        cos, sin = sb("cos", [P, S]), sb("sin", [P, S])
        ident = sb("ident", [P, P])
        seen = sb("seen", [P, 1])
        halfneg, epsc = sb("halfneg", [P, TPC]), sb("epsc", [P, TPC])
        stats, mv = sb("stats", [P, 2, TPC, 6]), sb("mv", [P, 2, TPC, 2])
        vare, rstd = sb("vare", [P, 2, TPC]), sb("rstd", [P, 2, TPC])
        xh = sb("xh", [P, TPC, D])
        xTh, xTl = sb("xTh", [P, WIN + S], F16), sb("xTl", [P, WIN + S], F16)
        t1, t2, rot = sb("t1", [P, CH]), sb("t2", [P, CH]), sb("rot", [P, 2, CH])
        v32 = sb("v32", [P, 8, D])
        qk = {(n, part): sb(f"{n}{part}", [P, T], F16) for n in "qk" for part in "hl"}
        psX = ps("psX", [P, CH])
        psP = [ps(f"psP{i}", [P, CH]) for i in range(4)]
        psV = ps("psV", [P, 8, D])

        const_loaded, x_loaded = sem("const_loaded"), sem("x_loaded")
        weights_scaled, weights_hi, weights_lo = sem("weights_scaled"), sem("weights_hi"), sem("weights_lo")
        zeroed = sem("zeroed")
        bn_done, stats_ready, eps_added, rstd_ready = sem("bn"), sem("stats_ready"), sem("eps_added"), sem("rstd_ready")
        xhat_ready, xhat_transposed = sem("xhat_ready"), sem("xhat_transposed")
        xT_hi, xT_lo = sem("xT_hi"), sem("xT_lo")
        proj_done, v_done = sem("proj_done"), sem("v_done")
        cos_part, rope_parts, rotated = sem("cos_part"), sem("rope_parts"), sem("rotated")
        qk_hi, qk_lo = sem("qk_hi"), sem("qk_lo")
        v_biased, v_hi, v_lo = sem("v_biased"), sem("v_hi"), sem("v_lo")
        stacked = sem("stacked")

        xt = io["x"].rearrange("b (t p) d -> p (b t) d", p=P)
        chunks_of_batch = S // CH

        with st.block() as block:

            @block.sync
            def _(sp):
                for c in range(NCH):
                    sp.dma_start(X[:, c * TPC:(c + 1) * TPC, :], xt[:, c * TPC:(c + 1) * TPC, :]).then_inc(x_loaded, 16)
                with sp.Fori(0, B) as b:
                    sp.wait_ge(qk_hi, 1 + (b + 1) * 2 * chunks_of_batch)
                    sp.wait_ge(qk_lo, 1 + (b + 1) * 2 * chunks_of_batch)
                    for g in range(4):
                        for j in range(4):
                            rows, src = slice(32 * j, 32 * j + 32), slice(32 * g, 32 * g + 32)
                            sp.dma_start(Q4[rows, g, ds(b * S, S)], qk["q", "hhll"[j]][src, ds(b * S, S)]).then_inc(stacked, 16)
                            sp.dma_start(K4[rows, g, ds(b * S + WIN, S)], qk["k", "hlhl"[j]][src, ds(b * S, S)]).then_inc(stacked, 16)
                sp.wait_ge(stacked, B * 32 * 16)

            @block.gpsimd
            def _(pool):
                pool.sem_inc(v_lo, 1)
                pool.sem_inc(qk_lo, 1)
                nc.gpsimd.memset(halfneg[:], -0.5).then_inc(zeroed, 1)
                nc.gpsimd.memset(epsc[:], EPS).then_inc(zeroed, 1)
                nc.gpsimd.memset(Vhi[:], 1.0).then_inc(zeroed, 1)
                nc.gpsimd.memset(Vlo[:], 0.0).then_inc(zeroed, 1)
                nc.gpsimd.memset(K4[:, :, 0:WIN], 0.0).then_inc(zeroed, 1)
                nc.gpsimd.memset(xTh[:, 0:WIN], 0.0).then_inc(zeroed, 1)
                nc.gpsimd.memset(xTl[:, 0:WIN], 0.0).then_inc(zeroed, 1)
                pool.wait_ge(zeroed, 7)

                def rstd_of(c, h):
                    pool.wait_ge(stats_ready, c + 1)
                    nc.gpsimd.tensor_tensor(vare[:, h], mv[:, h, :, 1], epsc[:], ALU.add).then_inc(eps_added, 1)
                    pool.wait_ge(eps_added, c + 1)
                    nc.gpsimd.tensor_tensor(rstd[:, h], vare[:, h], halfneg[:], ALU.pow).then_inc(rstd_ready, 1)

                def lows(b, h):
                    c = chunks_of_batch * b + h
                    for n, name in enumerate("qk"):
                        pool.wait_ge(qk_hi, 1 + 2 * c + n + 1)
                        nc.gpsimd.tensor_tensor(qk[name, "l"][:, ds(c * CH, CH)], rot[:, n, :],
                                                qk[name, "h"][:, ds(c * CH, CH)], ALU.subtract).then_inc(qk_lo, 1)
                    pool.wait_ge(v_hi, c + 1)
                    nc.gpsimd.tensor_tensor(
                        Vlo[:, ds(c * 8, 8), :, 0:DA], v32[:].rearrange("p w (h d) -> p w h d", d=DA),
                        Vhi[:, ds(c * 8, 8), :, 0:DA], ALU.subtract).then_inc(v_lo, 1)

                rstd_of(0, 0)
                rstd_of(1, 1)
                with pool.Fori(0, B - 1) as b:
                    for h in range(chunks_of_batch):
                        rstd_of(2 * b + h + 2, h)
                        lows(b, h)
                for h in range(chunks_of_batch):
                    lows(B - 1, h)

            @block.scalar
            def _(act):
                act.sem_inc(qk_hi, 1)
                act.dma_start(w32[:], io["wA"]).then_inc(const_loaded, 16)
                act.dma_start(ident[:], io["ident"]).then_inc(const_loaded, 16)
                act.dma_start(bias[:], io["biasA"]).then_inc(const_loaded, 16)
                act.dma_start(bvb[:], io["bv"].rearrange("(a n) -> a n", a=1).broadcast_to([P, D])).then_inc(const_loaded, 16)
                act.dma_start(cos[:], io["cos"]).then_inc(const_loaded, 16)
                act.dma_start(sin[:], io["sin"]).then_inc(const_loaded, 16)
                act.wait_ge(const_loaded, 96)
                nc.scalar.activation(whi[:], w32[:], ACT.Copy).then_inc(weights_hi, 1)

                def chunk(b, h):
                    c = chunks_of_batch * b + h
                    act.wait_ge(xhat_transposed, c + 1)
                    act.wait_ge(v_done, 1 + chunks_of_batch * b)
                    nc.scalar.activation(xTh[:, WIN + h * CH:WIN + (h + 1) * CH], psX[:], ACT.Copy).then_inc(xT_hi, 1)
                    for n, name in enumerate("qk"):
                        act.wait_ge(rotated, 2 * c + n + 1)
                        nc.scalar.activation(qk[name, "h"][:, ds(c * CH, CH)], rot[:, n, :], ACT.Copy).then_inc(qk_hi, 1)
                    act.wait_ge(v_biased, 1 + c + 1)
                    nc.scalar.activation(Vhi[:, ds(c * 8, 8), :, 0:DA], v32[:].rearrange("p w (h d) -> p w h d", d=DA),
                                         ACT.Copy).then_inc(v_hi, 1)

                act.wait_ge(zeroed, 7)
                with act.Fori(0, B) as b:
                    for h in range(chunks_of_batch):
                        chunk(b, h)

            @block.vector
            def _(dve):
                dve.sem_inc(v_biased, 1)
                dve.sem_inc(rope_parts, 1)
                def stats_of(c, h):
                    for j in range(TPC):
                        nc.vector.bn_stats(stats[:, h, j, :], X[:, TPC * c + j, :]).then_inc(bn_done, 1)
                    for j in range(TPC):
                        if j == 0:
                            dve.wait_ge(bn_done, TPC * c + TPC)
                            nc.vector.tensor_copy(seen[:], stats[:, h, TPC - 1, 0:1])
                        ins = nc.vector.bn_aggr(mv[:, h, j, :], stats[:, h, j, :])
                    ins.then_inc(stats_ready, 1)

                def normalise(c, h):
                    dve.wait_ge(rstd_ready, c + 1)
                    dve.wait_ge(xhat_transposed, c)
                    for j in range(TPC):
                        ins = nc.vector.tensor_scalar(xh[:, j, :], X[:, TPC * c + j, :], mv[:, h, j, 0:1],
                                                      rstd[:, h, j:j + 1], ALU.subtract, ALU.mult)
                    ins.then_inc(xhat_ready, 1)

                def chunk(b, h, more):
                    c = chunks_of_batch * b + h
                    dve.wait_ge(xT_hi, c + 1)
                    cols = slice(WIN + h * CH, WIN + (h + 1) * CH)
                    nc.vector.tensor_tensor(xTl[:, cols], psX[:], xTh[:, cols], ALU.subtract).then_inc(xT_lo, 1)
                    if more:
                        stats_of(c + 2, h)
                    if more or h == 0:
                        normalise(c + 1, 1 - h)
                    for n in range(2):
                        dve.wait_ge(proj_done, 4 * c + 2 * n + 1)
                        nc.vector.scalar_tensor_tensor(t1[:], psP[2 * n][:], bias[:, 2 * n:2 * n + 1],
                                                       cos[:, h * CH:(h + 1) * CH], ALU.add, ALU.mult).then_inc(cos_part, 1)
                        dve.wait_ge(proj_done, 4 * c + 2 * n + 2)
                        nc.vector.scalar_tensor_tensor(t2[:], psP[2 * n + 1][:], bias[:, 2 * n + 1:2 * n + 2],
                                                       sin[:, h * CH:(h + 1) * CH], ALU.add, ALU.mult).then_inc(rope_parts, 1)
                        dve.wait_ge(cos_part, 2 * c + n + 1)
                        dve.wait_ge(rope_parts, 1 + 2 * c + n + 1)
                        dve.wait_ge(qk_lo, 1 + 2 * c)
                        nc.vector.tensor_tensor(rot[:, n, :], t1[:], t2[:], ALU.add).then_inc(rotated, 1)
                        dve.wait_ge(rotated, 2 * c + n + 1)
                    dve.wait_ge(v_done, 1 + c + 1)
                    dve.wait_ge(v_lo, 1 + c)
                    nc.vector.tensor_tensor(v32[:], psV[:], bvb[:, None, :].broadcast_to([P, 8, D]),
                                            ALU.add).then_inc(v_biased, 1)

                dve.wait_ge(const_loaded, 96)
                dve.wait_ge(weights_hi, 1)
                nc.vector.tensor_tensor(wlo[:], w32[:], whi[:], ALU.subtract).then_inc(weights_lo, 1)
                dve.wait_ge(x_loaded, NCH * 16)
                stats_of(0, 0)
                stats_of(1, 1)
                normalise(0, 0)
                with dve.Fori(0, B - 1) as b:
                    for h in range(chunks_of_batch):
                        chunk(b, h, True)
                for h in range(chunks_of_batch):
                    chunk(B - 1, h, False)

            @block.tensor
            def _(pe):
                pe.sem_inc(v_done, 1)
                def transposes(c):
                    pe.wait_ge(xhat_ready, c + 1)
                    pe.wait_ge(xT_lo, c)
                    for j in range(TPC):
                        ins = nc.tensor.transpose(psX[:, j * P:(j + 1) * P], xh[:, j, :], ident[:])
                    ins.then_inc(xhat_transposed, 1)

                def project(b, h):
                    c = chunks_of_batch * b + h
                    pe.wait_ge(xT_hi, c + 1)
                    pe.wait_ge(xT_lo, c + 1)
                    for i in range(4):
                        pe.wait_ge(rope_parts, 1 + 2 * c)
                        cols = slice(WIN + h * CH, WIN + (h + 1) * CH)
                        nc.tensor.matmul(psP[i][:], whi[:, i, :], xTh[:, cols], start=True, stop=False)
                        nc.tensor.matmul(psP[i][:], whi[:, i, :], xTl[:, cols], start=False, stop=False)
                        nc.tensor.matmul(psP[i][:], wlo[:, i, :], xTh[:, cols], start=False, stop=True).then_inc(proj_done, 1)
                    pe.wait_ge(v_biased, 1 + c)
                    for w in range(8):
                        cols = slice((8 * h + w) * WIN, (8 * h + w) * WIN + P)
                        nc.tensor.matmul(psV[:, w, :], xTh[:, cols], whi[:, 4, :], start=True, stop=False)
                        nc.tensor.matmul(psV[:, w, :], xTl[:, cols], whi[:, 4, :], start=False, stop=False)
                        ins = nc.tensor.matmul(psV[:, w, :], xTh[:, cols], wlo[:, 4, :], start=False, stop=True)
                    ins.then_inc(v_done, 1)

                pe.wait_ge(const_loaded, 96)
                pe.wait_ge(weights_lo, 1)
                pe.wait_ge(zeroed, 7)
                transposes(0)
                with pe.Fori(0, B - 1) as b:
                    for h in range(chunks_of_batch):
                        project(b, h)
                        transposes(2 * b + h + 1)
                project(B - 1, 0)
                transposes(NCH - 1)
                project(B - 1, 1)


def band_attend(nc, X, Q4, K4, Vhi, Vlo, io):
    with Stage(nc, "a2") as st:
        sb, ps, sem = st.sb, st.ps, st.sem
        NP_ = HA // 2
        ident, identb = sb("ident", [P, P]), sb("identb", [P, P], BF16)
        bandm32, bandm = sb("bandm32", [P, 2, P]), sb("bandm", [P, 2, P], BF16)
        masks = sb("masks", [P, NT, P], BF16)
        headm = sb("headm", [P, 4], F16)
        parm = sb("parm", [P, 2])
        fold = sb("fold", [P, 2, P])
        wo32, woh, wol = sb("wo32", [P, D]), sb("woh", [P, D], F16), sb("wol", [P, D], F16)
        bob = sb("bob", [P, D])
        Qx = sb("Qx", [P, 2, HA, WIN], F16)
        mx, nb = sb("mx", [P, NP_]), sb("nb", [P, NP_])
        E = sb("E", [P, 2, NP_, P])
        Th, Tl = sb("Th", [P, 2, NP_, P], F16), sb("Tl", [P, 2, NP_, P], F16)
        rd, rm = sb("rd", [P, NP_, 2]), sb("rm", [P, NP_, 2])
        On = sb("On", [P, 2, NP_ * 2, DA])
        oTh, oTl = sb("oTh", [P, P], F16), sb("oTl", [P, P], F16)
        psS = [[ps(f"psS{j}{a}", [P, 4, P]) for a in range(2)] for j in range(2)]
        psT = [ps(f"psT{a}", [P, 4, P]) for a in range(2)]
        psO = ps("psO", [P, 512])
        psY = ps("psY", [P, 512])
        pv = psO[:, 0:NP_ * 2 * VW].rearrange("p (m r w) -> p m r w", r=2, w=VW)

        loaded, wo_hi, wo_lo, masks_ready = sem("loaded"), sem("wo_hi"), sem("wo_lo"), sem("masks_ready")
        band_cast, q_masked = sem("band_cast"), sem("q_masked")
        scores_done = sem("scores_done")
        max_done, bias_done, shifted, exps_done = sem("max_done"), sem("bias_done"), sem("shifted"), sem("exps_done")
        exp_transposed, T_hi, T_lo = sem("exp_transposed"), sem("T_hi"), sem("T_lo")
        values_done = sem("values_done")
        recip_done, recip_masked, normed = sem("recip_done"), sem("recip_masked"), sem("normed")
        folded, oT_hi, oT_lo, projected, bias_added, added = (
            sem("folded"), sem("oT_hi"), sem("oT_lo"), sem("projected"), sem("bias_added"), sem("added"))

        with st.block() as block:

            @block.sync
            def _(sp):
                sp.dma_start(ident[:], io["ident"]).then_inc(loaded, 16)
                sp.dma_start(bandm32[:], io["bandm"]).then_inc(loaded, 16)
                sp.dma_start(headm[:], io["headm"]).then_inc(loaded, 16)
                sp.dma_start(parm[:], io["parm"]).then_inc(loaded, 16)
                sp.dma_start(fold[:], io["fold"]).then_inc(loaded, 16)
                sp.dma_start(wo32[:], io["woT"]).then_inc(loaded, 16)
                sp.dma_start(bob[:], io["bo"].rearrange("(a n) -> a n", a=1).broadcast_to([P, D])).then_inc(loaded, 16)

            LOADED = 7 * 16

            @block.gpsimd
            def _(pool):
                def mask_q(n, j, first=False):
                    if not first:
                        pool.wait_ge(scores_done, 2 * n - 2)
                    nc.gpsimd.tensor_tensor(
                        Qx[:, j].rearrange("p (g h) q -> p g h q", h=4),
                        Q4[:, :, None, ds(WIN * n, WIN)].broadcast_to([P, 4, 4, WIN]),
                        headm[:, None, :, None].broadcast_to([P, 4, 4, WIN]), ALU.mult).then_inc(q_masked, 1)

                pool.wait_ge(loaded, LOADED)
                mask_q(0, 0, True)
                mask_q(1, 1, True)
                with pool.Fori(1, NT) as t:
                    for j in range(2):
                        mask_q(2 * t + j, j)

            @block.scalar
            def _(act):
                def exps(n, j):
                    act.wait_ge(bias_done, n + 1)
                    for p in range(4, NP_):
                        ins = nc.scalar.activation(E[:, j, p, :], psS[j][1][:, p - 4, :], ACT.Exp,
                                                   bias=nb[:, p:p + 1], scale=SCALE_A)
                    ins.then_inc(exps_done, 1)
                    act.wait_ge(shifted, n + 1)
                    nc.scalar.activation(E[:, j, 0:4, :], E[:, j, 0:4, :], ACT.Exp, scale=SCALE_A).then_inc(exps_done, 1)

                def tile(t, first, last):
                    for j in range(2):
                        n = 2 * t + j
                        if not first:
                            act.wait_ge(values_done, n - 1)
                        for a in range(2):
                            act.wait_ge(exp_transposed, 2 * n + a + 1)
                            nc.scalar.activation(Th[:, j, 4 * a:4 * a + 4, :], psT[a][:], ACT.Copy).then_inc(T_hi, 1)
                        if j == 0 and not first:
                            act.wait_ge(folded, t)
                            nc.scalar.activation(oTh[:], psY[:, 0:P], ACT.Copy).then_inc(oT_hi, 1)
                        if not (last and j == 1):
                            exps(n + 1, 1 - j)

                act.wait_ge(loaded, LOADED)
                nc.scalar.activation(woh[:], wo32[:], ACT.Copy).then_inc(wo_hi, 1)
                nc.scalar.activation(bandm[:], bandm32[:], ACT.Copy).then_inc(band_cast, 1)
                nc.scalar.activation(identb[:], ident[:], ACT.Copy).then_inc(band_cast, 1)
                exps(0, 0)
                tile(0, True, False)
                with act.Fori(1, NT - 1) as t:
                    tile(t, False, False)
                tile(NT - 1, False, True)
                act.wait_ge(folded, NT)
                nc.scalar.activation(oTh[:], psY[:, 0:P], ACT.Copy).then_inc(oT_hi, 1)

            @block.vector
            def _(dve):
                dve.sem_inc(added, 1)
                def shift(n, j, first=False):
                    if not first:
                        dve.wait_ge(exps_done, 2 * n)
                    for a in range(2):
                        dve.wait_ge(scores_done, 2 * n + a + 1)
                        nc.vector.tensor_reduce(mx[:, 4 * a:4 * a + 4], psS[j][a][:], AX_X, ALU.max).then_inc(max_done, 1)
                    dve.wait_ge(max_done, 2 * n + 2)
                    nc.vector.tensor_scalar(nb[:, 4:8], mx[:, 4:8], -SCALE_A, None, ALU.mult).then_inc(bias_done, 1)
                    if not first:
                        dve.wait_ge(exp_transposed, 2 * n - 2)
                    nc.vector.tensor_tensor(E[:, j, 0:4, :], psS[j][0][:], mx[:, 0:4, None].broadcast_to([P, 4, P]),
                                            ALU.subtract).then_inc(shifted, 1)

                def norm(n, j):
                    dve.wait_ge(values_done, n + 1)
                    nc.vector.reciprocal(rd[:], pv[:, :, :, DA]).then_inc(recip_done, 1)
                    dve.wait_ge(recip_done, n + 1)
                    nc.vector.tensor_tensor(rm[:], rd[:], parm[:, None, :].broadcast_to([P, NP_, 2]),
                                            ALU.mult).then_inc(recip_masked, 1)
                    dve.wait_ge(recip_masked, n + 1)
                    nc.vector.tensor_tensor(
                        On[:, j].rearrange("p (m r) d -> p m r d", r=2), pv[:, :, :, 0:DA],
                        rm[:, :, :, None].broadcast_to([P, NP_, 2, DA]), ALU.mult).then_inc(normed, 1)

                def add(t):
                    dve.wait_ge(projected, t + 1)
                    nc.vector.tensor_tensor(X[:, ds(t, 1), :], psY[:, None, P:2 * P], X[:, ds(t, 1), :], ALU.add).then_inc(added, 1)

                def split_o(t):
                    dve.wait_ge(oT_hi, t + 1)
                    nc.vector.tensor_tensor(oTl[:], psY[:, 0:P], oTh[:], ALU.subtract).then_inc(oT_lo, 1)

                def tile(t, first, last):
                    for j in range(2):
                        n = 2 * t + j
                        if not (last and j == 1):
                            shift(n + 1, 1 - j)
                        if j == 1 and not first:
                            add(t - 1)
                        if not (first and j == 0):
                            if j == 1 and not first:
                                dve.wait_ge(folded, t)
                            norm(n - 1, 1 - j)
                        for a in range(2):
                            dve.wait_ge(T_hi, 2 * n + a + 1)
                            nc.vector.tensor_tensor(Tl[:, j, 4 * a:4 * a + 4, :], psT[a][:], Th[:, j, 4 * a:4 * a + 4, :],
                                                    ALU.subtract).then_inc(T_lo, 1)
                        if j == 0 and not first:
                            split_o(t - 1)

                dve.wait_ge(loaded, LOADED)
                dve.wait_ge(wo_hi, 1)
                nc.vector.tensor_tensor(wol[:], wo32[:], woh[:], ALU.subtract).then_inc(wo_lo, 1)
                dve.wait_ge(band_cast, 1)
                nc.vector.tensor_copy(masks[:], bandm[:, 1:2, :].broadcast_to([P, NT, P])).then_inc(masks_ready, 1)
                dve.wait_ge(masks_ready, 1)
                nc.vector.tensor_copy(masks[:].rearrange("p (b i) k -> p b i k", b=B)[:, :, 0, :],
                                      bandm[:, 0:1, :].broadcast_to([P, B, P])).then_inc(masks_ready, 1)
                nc.vector.tensor_tensor(X[:], X[:], bob[:, None, :].broadcast_to([P, NT, D]), ALU.add).then_inc(bias_added, 1)
                dve.wait_ge(bias_added, 1)
                shift(0, 0, True)
                tile(0, True, False)
                with dve.Fori(1, NT - 1) as t:
                    tile(t, False, False)
                tile(NT - 1, False, True)
                dve.wait_ge(folded, NT - 1)
                norm(NB - 1, 1)
                split_o(NT - 1)
                add(NT - 1)

            @block.tensor
            def _(pe):
                def scores(n, j, first=False):
                    pe.wait_ge(q_masked, n + 1)
                    if not first:
                        pe.wait_ge(exps_done, 2 * n - 2)
                        pe.wait_ge(shifted, n - 1)
                    for a in range(2):
                        m = masks[:, ds(n // 2, 1), :] if j == 0 else bandm[:, 1:2, :]
                        nc.tensor.matmul(psS[j][a][:], identb[:], m.broadcast_to([P, 4, P]), start=True, stop=False)
                        for p in range(4):
                            q = Qx[:, j, 8 * a + 2 * p:8 * a + 2 * p + 2, :]
                            ins = nc.tensor.matmul(psS[j][a][:, p, :], q, K4[:, 2 * a + p // 2, ds(WIN * n, P)],
                                                   start=False, stop=(p == 3))
                        ins.then_inc(scores_done, 1)

                def transposes(n, j, first=False):
                    for a in range(2):
                        pe.wait_ge(exps_done, 2 * n + 2)
                        if not first:
                            pe.wait_ge(T_lo, 2 * n - 1 + a)
                        for p in range(4):
                            ins = nc.tensor.transpose(psT[a][:, p, :], E[:, j, 4 * a + p, :], ident[:])
                        ins.then_inc(exp_transposed, 1)

                def values(n, j, first=False):
                    if not first:
                        pe.wait_ge(normed, n)
                    for a in range(2):
                        pe.wait_ge(T_lo, 2 * n + a + 1)
                        for p in range(4 * a, 4 * a + 4):
                            o = pv[:, p, :, :]
                            vh, vl = Vhi[:, ds(n, 1), 2 * p:2 * p + 2, :], Vlo[:, ds(n, 1), 2 * p:2 * p + 2, :]
                            nc.tensor.matmul(o, Th[:, j, p, :], vh, start=True, stop=False)
                            nc.tensor.matmul(o, Th[:, j, p, :], vl, start=False, stop=False)
                            ins = nc.tensor.matmul(o, Tl[:, j, p, :], vh, start=False, stop=True)
                    ins.then_inc(values_done, 1)

                def fold_o(t):
                    pe.wait_ge(normed, 2 * t + 2)
                    pe.wait_ge(added, 1 + t)
                    for j in range(2):
                        ins = nc.tensor.matmul(psY[:, 0:P], On[:, j], fold[:, j, :], start=(j == 0), stop=(j == 1))
                    ins.then_inc(folded, 1)

                def project(t):
                    pe.wait_ge(oT_lo, t + 1)
                    nc.tensor.matmul(psY[:, P:2 * P], oTh[:], woh[:], start=True, stop=False)
                    nc.tensor.matmul(psY[:, P:2 * P], oTh[:], wol[:], start=False, stop=False)
                    nc.tensor.matmul(psY[:, P:2 * P], oTl[:], woh[:], start=False, stop=True).then_inc(projected, 1)

                def tile(t, first, last):
                    for j in range(2):
                        n = 2 * t + j
                        if not (last and j == 1):
                            scores(n + 1, 1 - j, first and j == 0)
                        if j == 1 and not first:
                            project(t - 1)
                        transposes(n, j, first and j == 0)
                        if j == 0 and not first:
                            fold_o(t - 1)
                        values(n, j, first and j == 0)

                pe.wait_ge(loaded, LOADED)
                pe.wait_ge(wo_lo, 1)
                pe.wait_ge(masks_ready, 2)
                pe.wait_ge(band_cast, 2)
                scores(0, 0, True)
                tile(0, True, False)
                with pe.Fori(1, NT - 1) as t:
                    tile(t, False, False)
                tile(NT - 1, False, True)
                fold_o(NT - 1)
                project(NT - 1)


def experts(nc, X, io, tag):
    with Stage(nc, tag) as outer:
        sb = outer.sb
        xnh, xnl = sb("xnh", [P, T], F16), sb("xnl", [P, T], F16)
        w1h, w1l = sb("w1h", [P, NE, FF], F16), sb("w1l", [P, NE, FF], F16)
        w2h, w2l = sb("w2h", [P, NE, FC, D], F16), sb("w2l", [P, NE, FC, D], F16)
        b1 = sb("b1", [P, NE, FC])
        K = sb("K", [P, NE])
        Gh, Gl = sb("Gh", [P, NT, NE], F16), sb("Gl", [P, NT, NE], F16)
        identh, ident = sb("identh", [P, P], F16), sb("ident", [P, P])
        route(nc, X, xnh, xnl, w1h, w1l, w2h, w2l, b1, K, Gh, Gl, identh, ident, io, tag + "r")
        mixture(nc, X, xnh, xnl, w1h, w1l, w2h, w2l, b1, K, Gh, Gl, identh, ident, tag + "m")


def route(nc, X, xnh, xnl, w1h, w1l, w2h, w2l, b1, K, Gh, Gl, identh, ident, io, tag):
    with Stage(nc, tag) as st:
        sb, ps, sem = st.sb, st.ps, st.sem
        w32 = sb("w32", [P, NE * FF])
        wr32, wrh, wrl = sb("wr32", [P, NE]), sb("wrh", [P, NE], F16), sb("wrl", [P, NE], F16)
        gamma, beta = sb("gamma", [P, 1]), sb("beta", [P, 1])
        brb = sb("brb", [P, NE])
        b2 = sb("b2", [P, NE])
        a32, ah, al = sb("a32", [P, NE, FC]), sb("ah", [P, NE, FC], F16), sb("al", [P, NE, FC], F16)
        ctot, csum = sb("ctot", [P, 1]), sb("csum", [P, NE])
        seen = sb("seen", [P, 2])
        halfneg, epsc = sb("halfneg", [P, TPC]), sb("epsc", [P, TPC])
        stats, mv = sb("stats", [P, 2, 2, TPC, 6]), sb("mv", [P, 2, 2, TPC, 2])
        vare, rstd = sb("vare", [P, 2, 2, TPC]), sb("rstd", [P, 2, 2, TPC])
        u = sb("u", [P, 2, TPC, D])
        xh = sb("xh", [P, 2, TPC, D])
        xn = sb("xn", [P, 2, CH])
        rank = sb("rank", [P, NE])
        L, eq, oh1, oh2, pr = (sb(n, [P, NT, NE]) for n in ("L", "eq", "oh1", "oh2", "pr"))
        m = sb("m", [P, 6, NT])
        psX = [ps(f"psX{h}", [P, CH]) for h in range(2)]
        psL = ps("psL", [P, 512])
        psK = ps("psK", [P, 512])
        lg = psL[:, 0:NT * NE].rearrange("p (t e) -> p t e", e=NE)

        loaded, w1_loaded, w2_loaded, set_up = sem("loaded"), sem("w1_loaded"), sem("w2_loaded"), sem("set_up")
        w_hi, w_lo = sem("w_hi"), sem("w_lo")
        bn_done = [sem("bnX_done"), sem("bnu_done")]
        stats_ready = [sem("statsX_ready"), sem("statsu_ready")]
        eps_added = [sem("epsX_added"), sem("epsu_added")]
        rstd_ready = [sem("rstdX_ready"), sem("rstdu_ready")]
        u_ready, u_added, xhat_ready, transposed = sem("u_ready"), sem("u_added"), sem("xhat_ready"), sem("transposed")
        xn_hi, xn_ready, xn_lo, logits_done = sem("xn_hi"), sem("xn_ready"), sem("xn_lo"), sem("logits_done")
        wr_hi, wr_lo = sem("wr_hi"), sem("wr_lo")
        b1_relu, b1_hi, b1_lo, k_done, k_step = sem("b1_relu"), sem("b1_hi"), sem("b1_lo"), sem("k_done"), sem("k_step")
        rt, exp_ready = sem("router_step"), sem("exp_ready")

        with st.block() as block:

            @block.sync
            def _(sp):
                for dst, src in ((identh[:], io["identh"]), (ident[:], io["ident"]), (gamma[:], io["gammaF"]),
                                 (beta[:], io["betaF"]), (wr32[:], io["wrF"]), (b1[:], io["b1F"]), (b2[:], io["b2F"]),
                                 (rank[:], io["rank"]),
                                 (brb[:], io["brF"].rearrange("(a n) -> a n", a=1).broadcast_to([P, NE]))):
                    sp.dma_start(dst, src).then_inc(loaded, 16)
                sp.dma_start(w32[:], io["w1F"].rearrange("p e f -> p (e f)")).then_inc(w1_loaded, 16)
                sp.wait_ge(w_lo, 1)
                sp.dma_start(w32[:], io["w2F"].rearrange("p e f d -> p (e f d)")).then_inc(w2_loaded, 16)

            LOADED = 9 * 16

            @block.gpsimd
            def _(pool):
                pool.sem_inc(u_added, 1)
                nc.gpsimd.memset(halfneg[:], -0.5).then_inc(set_up, 1)
                nc.gpsimd.memset(epsc[:], EPS).then_inc(set_up, 1)
                pool.wait_ge(set_up, 2)

                def rstd_of(k, c, h):
                    pool.wait_ge(stats_ready[k], c + 1)
                    nc.gpsimd.tensor_tensor(vare[:, k, h], mv[:, k, h, :, 1], epsc[:], ALU.add).then_inc(eps_added[k], 1)
                    pool.wait_ge(eps_added[k], c + 1)
                    nc.gpsimd.tensor_tensor(rstd[:, k, h], vare[:, k, h], halfneg[:], ALU.pow).then_inc(rstd_ready[k], 1)

                def add_u(c, h):
                    pool.wait_ge(u_ready, c + 1)
                    nc.gpsimd.tensor_tensor(X[:, ds(TPC * c, TPC), :], X[:, ds(TPC * c, TPC), :], u[:, h], ALU.add).then_inc(u_added, 1)

                rstd_of(0, 0, 0)
                rstd_of(0, 1, 1)
                rstd_of(1, 0, 0)
                with pool.Fori(0, NCH // 2 - 1) as b:
                    for h in range(2):
                        c = 2 * b + h
                        rstd_of(0, c + 2, h)
                        rstd_of(1, c + 1, 1 - h)
                        add_u(c, h)
                rstd_of(1, NCH - 1, 1)
                add_u(NCH - 2, 0)
                add_u(NCH - 1, 1)

            @block.scalar
            def _(act):
                act.wait_ge(loaded, LOADED)
                nc.scalar.activation(wrh[:], wr32[:], ACT.Copy).then_inc(wr_hi, 1)
                nc.scalar.activation(a32[:], b1[:], ACT.Relu).then_inc(b1_relu, 1)
                act.wait_ge(b1_relu, 1)
                nc.scalar.activation(ah[:], a32[:], ACT.Copy).then_inc(b1_hi, 1)
                act.wait_ge(w1_loaded, 16)
                nc.scalar.activation(w1h[:].rearrange("p e f -> p (e f)"), w32[:], ACT.Copy, scale=WS).then_inc(w_hi, 1)
                act.wait_ge(w2_loaded, 16)
                nc.scalar.activation(w2h[:].rearrange("p e f d -> p (e f d)"), w32[:], ACT.Copy, scale=WS).then_inc(w_hi, 1)

                with act.Fori(0, NCH // 2) as b:
                    for h in range(2):
                        act.wait_ge(transposed, 2 * b + h + 1)
                        act.wait_ge(xn_lo, 1 + 2 * b)
                        nc.scalar.activation(xnh[:, ds((2 * b + h) * CH, CH)], psX[h][:], ACT.Identity,
                                             bias=beta[:], scale=gamma[:]).then_inc(xn_hi, 1)
                        nc.scalar.activation(xn[:, h], psX[h][:], ACT.Identity, bias=beta[:], scale=gamma[:]).then_inc(xn_ready, 1)
                act.wait_ge(rt, 3)
                nc.scalar.activation(pr[:], L[:], ACT.Exp).then_inc(exp_ready, 1)

            @block.vector
            def _(dve):
                dve.sem_inc(xn_lo, 1)
                def stats_of(k, src, c, h):
                    for j in range(TPC):
                        nc.vector.bn_stats(stats[:, k, h, j, :], src(j)).then_inc(bn_done[k], 1)
                    for j in range(TPC):
                        if j == 0:
                            dve.wait_ge(bn_done[k], TPC * c + TPC)
                            nc.vector.tensor_copy(seen[:, k:k + 1], stats[:, k, h, TPC - 1, 0:1])
                        ins = nc.vector.bn_aggr(mv[:, k, h, j, :], stats[:, k, h, j, :])
                    ins.then_inc(stats_ready[k], 1)

                def norm_x(c, h):
                    dve.wait_ge(rstd_ready[0], c + 1)
                    for j in range(TPC):
                        ins = nc.vector.tensor_scalar(u[:, h, j, :], X[:, TPC * c + j, :], mv[:, 0, h, j, 0:1],
                                                      rstd[:, 0, h, j:j + 1], ALU.subtract, ALU.mult)
                    ins.then_inc(u_ready, 1)
                    dve.wait_ge(u_ready, c + 1)
                    stats_of(1, lambda j: u[:, h, j, :], c, h)

                def norm_u(c, h):
                    dve.wait_ge(rstd_ready[1], c + 1)
                    for j in range(TPC):
                        ins = nc.vector.tensor_scalar(xh[:, h, j, :], u[:, h, j, :], mv[:, 1, h, j, 0:1],
                                                      rstd[:, 1, h, j:j + 1], ALU.subtract, ALU.mult)
                    ins.then_inc(xhat_ready, 1)

                def chunk(c, h, more):
                    norm_u(c, h)
                    if more:
                        stats_of(0, lambda j: X[:, TPC * (c + 2) + j, :], c + 2, h)
                    if more or h == 0:
                        dve.wait_ge(u_added, 1 + c)
                        norm_x(c + 1, 1 - h)
                    dve.wait_ge(xn_ready, c + 1)
                    dve.wait_ge(xn_hi, c + 1)
                    nc.vector.tensor_tensor(xnl[:, ds(c * CH, CH)], xn[:, h], xnh[:, ds(c * CH, CH)], ALU.subtract).then_inc(xn_lo, 1)

                dve.wait_ge(loaded, LOADED)
                dve.wait_ge(wr_hi, 1)
                nc.vector.tensor_tensor(wrl[:], wr32[:], wrh[:], ALU.subtract).then_inc(wr_lo, 1)
                dve.wait_ge(b1_hi, 1)
                nc.vector.tensor_tensor(al[:], a32[:], ah[:], ALU.subtract).then_inc(b1_lo, 1)
                stats_of(0, lambda j: X[:, j, :], 0, 0)
                stats_of(0, lambda j: X[:, TPC + j, :], 1, 1)
                norm_x(0, 0)
                dve.wait_ge(w_hi, 1)
                nc.vector.scalar_tensor_tensor(w1l[:].rearrange("p e f -> p (e f)"), w32[:], WS, w1h[:].rearrange("p e f -> p (e f)"),
                                               ALU.mult, ALU.subtract).then_inc(w_lo, 1)
                with dve.Fori(0, NCH // 2 - 1) as b:
                    for h in range(2):
                        chunk(2 * b + h, h, True)
                for h in range(2):
                    chunk(NCH - 2 + h, h, False)
                dve.wait_ge(w_hi, 2)
                nc.vector.scalar_tensor_tensor(w2l[:].rearrange("p e f d -> p (e f d)"), w32[:], WS,
                                               w2h[:].rearrange("p e f d -> p (e f d)"), ALU.mult, ALU.subtract).then_inc(w_lo, 1)

                step = [0]

                def then(ins):
                    step[0] += 1
                    ins.then_inc(rt, 1)
                    dve.wait_ge(rt, step[0])

                bc = lambda a: a[:, :, None].broadcast_to([P, NT, NE])
                rk = rank[:, None, :].broadcast_to([P, NT, NE])
                V = nc.vector
                dve.wait_ge(logits_done, NCH)
                then(V.tensor_tensor(L[:], lg, brb[:, None, :].broadcast_to([P, NT, NE]), ALU.add))
                then(V.tensor_reduce(m[:, 0], L[:], AX_X, ALU.max))
                then(V.tensor_tensor(L[:], L[:], bc(m[:, 0]), ALU.subtract))
                then(V.tensor_scalar(eq[:], L[:], 0.0, None, ALU.is_equal))
                then(V.tensor_tensor(eq[:], eq[:], rk, ALU.mult))
                then(V.tensor_reduce(m[:, 1], eq[:], AX_X, ALU.max))
                then(V.tensor_tensor(oh1[:], rk, bc(m[:, 1]), ALU.is_equal))
                then(V.scalar_tensor_tensor(oh2[:], oh1[:], -1e30, L[:], ALU.mult, ALU.add))
                then(V.tensor_reduce(m[:, 2], oh2[:], AX_X, ALU.max))
                then(V.tensor_tensor(eq[:], oh2[:], bc(m[:, 2]), ALU.is_equal))
                then(V.tensor_tensor(eq[:], eq[:], rk, ALU.mult))
                then(V.tensor_reduce(m[:, 3], eq[:], AX_X, ALU.max))
                then(V.tensor_tensor(oh2[:], rk, bc(m[:, 3]), ALU.is_equal))
                then(V.tensor_tensor(oh1[:], oh1[:], oh2[:], ALU.add))
                dve.wait_ge(exp_ready, 1)
                then(V.tensor_reduce(m[:, 4], pr[:], AX_X, ALU.add))
                then(V.reciprocal(m[:, 5], m[:, 4]))
                then(V.tensor_tensor(pr[:], pr[:], bc(m[:, 5]), ALU.mult))
                then(V.tensor_tensor(pr[:], pr[:], oh1[:], ALU.mult))
                then(V.tensor_copy(Gh[:], pr[:]))
                then(V.tensor_tensor(Gl[:], pr[:], Gh[:], ALU.subtract))
                dve.wait_ge(k_done, 1)
                V.scalar_tensor_tensor(csum[:], b2[:], WS, psK[:, 0:NE], ALU.mult, ALU.add).then_inc(k_step, 1)
                dve.wait_ge(k_step, 1)
                V.tensor_reduce(ctot[:], csum[:], AX_X, ALU.add).then_inc(k_step, 1)
                dve.wait_ge(k_step, 2)
                V.tensor_scalar(K[:], psK[:, 0:NE], -1.0, ctot[:], ALU.mult, ALU.add).then_inc(k_step, 1)
                dve.wait_ge(k_step, 3)

            @block.tensor
            def _(pe):
                def transposes(c, h):
                    pe.wait_ge(xhat_ready, c + 1)
                    for j in range(TPC):
                        ins = nc.tensor.transpose(psX[h][:, j * P:(j + 1) * P], xh[:, h, j, :], ident[:])
                    ins.then_inc(transposed, 1)

                def logits(c):
                    pe.wait_ge(xn_lo, 1 + c + 1)
                    for j in range(TPC):
                        t = TPC * c + j
                        o = psL[:, ds(t * NE, NE)]
                        nc.tensor.matmul(o, xnh[:, ds(t * P, P)], wrh[:], start=True, stop=False)
                        nc.tensor.matmul(o, xnh[:, ds(t * P, P)], wrl[:], start=False, stop=False)
                        ins = nc.tensor.matmul(o, xnl[:, ds(t * P, P)], wrh[:], start=False, stop=True)
                    ins.then_inc(logits_done, 1)

                pe.wait_ge(loaded, LOADED)
                pe.wait_ge(wr_lo, 1)
                transposes(0, 0)
                with pe.Fori(0, NCH // 2 - 1) as b:
                    for h in range(2):
                        pe.wait_ge(xn_lo, 1 + 2 * b + h)
                        transposes(2 * b + h + 1, 1 - h)
                        logits(2 * b + h)
                pe.wait_ge(xn_lo, 1 + NCH - 2)
                transposes(NCH - 1, 1)
                logits(NCH - 2)
                logits(NCH - 1)
                pe.wait_ge(w_lo, 2)
                pe.wait_ge(b1_lo, 1)
                for e in range(NE):
                    for f in range(FC):
                        w, wl = w2h[:, e, f, :], w2l[:, e, f, :]
                        nc.tensor.matmul(psK[:, e:e + 1], w, ah[:, e, f:f + 1], start=(f == 0), stop=False)
                        nc.tensor.matmul(psK[:, e:e + 1], w, al[:, e, f:f + 1], start=False, stop=False)
                        ins = nc.tensor.matmul(psK[:, e:e + 1], wl, ah[:, e, f:f + 1], start=False, stop=(f == FC - 1))
                ins.then_inc(k_done, 1)


def mixture(nc, X, xnh, xnl, w1h, w1l, w2h, w2l, b1, K, Gh, Gl, identh, ident, tag):
    with Stage(nc, tag) as st:
        sb, ps, sem = st.sb, st.ps, st.sem
        R = sb("R", [P, 2, FC, CH])
        Hh, Hl = sb("Hh", [P, 2, FC, CH], F16), sb("Hl", [P, 2, FC, CH], F16)
        gb = sb("gb", [P, 2, CH])
        Y = sb("Y", [P, 2, CH])
        acc, accf = sb("acc", [P, CH]), sb("accf", [P, CH])
        psZ = [ps(f"psZ{f}", [P, CH]) for f in range(FC)]
        psY = [ps(f"psY{j}", [P, CH]) for j in range(2)]
        psG, psT = ps("psG", [P, CH]), ps("psT", [P, CH])

        up_done, gates_spread, gates_read = sem("up_done"), sem("gates_spread"), sem("gates_read")
        relu_done = sem("relu_done")
        H_hi = sem("H_hi")
        H_lo = sem("H_lo")
        down_done = sem("down_done")
        y_done = sem("y_done")
        y_added = sem("y_added")
        summed, sum_transposed, x_added = sem("summed"), sem("sum_transposed"), sem("x_added")
        chunk_step = sem("chunk_step")

        with st.block() as block:

            @block.tensor
            def _(pe):
                pe.sem_inc(sum_transposed, 1)
                pe.sem_inc(down_done, 2)

                def up(u, c, e):
                    for f in range(FC):
                        pe.wait_ge(relu_done, FC * u + f + 1)
                        x, xl = xnh[:, ds(c * CH, CH)], xnl[:, ds(c * CH, CH)]
                        w, wl = w1h[:, ds(e, 1), f * P:(f + 1) * P], w1l[:, ds(e, 1), f * P:(f + 1) * P]
                        nc.tensor.matmul(psZ[f][:], w, x, start=True, stop=False)
                        nc.tensor.matmul(psZ[f][:], w, xl, start=False, stop=False)
                        nc.tensor.matmul(psZ[f][:], wl, x, start=False, stop=True).then_inc(up_done, 1)

                def spread(u, c, e):
                    pe.wait_ge(gates_read, u)
                    for j in range(TPC):
                        t = TPC * c + j
                        o = psG[:, j * P:(j + 1) * P]
                        nc.tensor.matmul(o, Gh[:].rearrange("p t e -> p (t e)")[:, ds(NE * t + e, 1)].broadcast_to([P, P]), identh[:], start=True, stop=False)
                        ins = nc.tensor.matmul(o, Gl[:].rearrange("p t e -> p (t e)")[:, ds(NE * t + e, 1)].broadcast_to([P, P]), identh[:], start=False, stop=True)
                    ins.then_inc(gates_spread, 1)

                def down(u, e, j):
                    pe.wait_ge(y_done, u + 1)
                    for f in range(FC):
                        pe.wait_ge(H_lo, 2 * FC + FC * u + f + 1)
                        w, wl = w2h[:, ds(e, 1), f, :], w2l[:, ds(e, 1), f, :]
                        nc.tensor.matmul(psY[j][:], w, Hh[:, j, f, :], start=(f == 0), stop=False)
                        nc.tensor.matmul(psY[j][:], w, Hl[:, j, f, :], start=False, stop=False)
                        ins = nc.tensor.matmul(psY[j][:], wl, Hh[:, j, f, :], start=False, stop=(f == FC - 1))
                    ins.then_inc(down_done, 1)

                def pair(c, ep):
                    for j in range(2):
                        u = NE * c + 2 * ep + j
                        q = (NE // 2) * c + ep + j
                        up(u + 1, (q // (NE // 2)) % NCH, 2 * (q % (NE // 2)) + (1 - j))
                        spread(u, c, 2 * ep + j)
                        down(u, 2 * ep + j, j)

                def transposes(c):
                    pe.wait_ge(summed, c + 1)
                    pe.wait_ge(x_added, 1 + c)
                    for j in range(TPC):
                        ins = nc.tensor.transpose(psT[:, j * P:(j + 1) * P], accf[:, j * P:(j + 1) * P], ident[:])
                    ins.then_inc(sum_transposed, 1)

                up(0, 0, 0)
                pair(0, 0)
                with pe.Fori(1, NE // 2) as ep:
                    pair(0, ep)
                with pe.Fori(1, NCH) as c:
                    pair(c, 0)
                    transposes(c - 1)
                    with pe.Fori(1, NE // 2) as ep:
                        pair(c, ep)
                transposes(NCH - 1)

            @block.scalar
            def _(act):
                act.sem_inc(relu_done, FC)

                def relu(u, e, j):
                    for f in range(FC):
                        act.wait_ge(up_done, FC * u + f + 1)
                        act.wait_ge(H_lo, FC * u + f + 1)
                        nc.scalar.activation(R[:, j, f, :], psZ[f][:], ACT.Relu, bias=b1[:, ds(e, 1), f], scale=1.0 / WS).then_inc(relu_done, 1)

                relu(0, 0, 0)
                with act.Fori(0, NCH * NE // 2) as q:
                    for j in range(2):
                        u = 2 * q + j
                        relu(u + 1, 2 * ((q + j) % (NE // 2)) + (1 - j), 1 - j)
                        act.wait_ge(gates_spread, u + 1)
                        act.wait_ge(y_done, u + 1)
                        nc.scalar.activation(gb[:, j, :], psG[:], ACT.Copy, scale=1.0 / WS).then_inc(gates_read, 1)

            @block.vector
            def _(dve):
                dve.sem_inc(x_added, 1)
                dve.sem_inc(H_lo, 2 * FC)
                dve.sem_inc(y_done, 2)

                def split(u, j):
                    dve.wait_ge(down_done, u + 1)
                    for f in range(FC):
                        dve.wait_ge(relu_done, FC + FC * u + f + 1)
                        nc.vector.tensor_copy(Hh[:, j, f, :], R[:, j, f, :]).then_inc(H_hi, 1)
                        dve.wait_ge(H_hi, FC * u + f + 1)
                        nc.vector.tensor_tensor(Hl[:, j, f, :], R[:, j, f, :], Hh[:, j, f, :], ALU.subtract).then_inc(H_lo, 1)

                def gate(u, e, j):
                    dve.wait_ge(down_done, 2 + u + 1)
                    dve.wait_ge(gates_read, u + 1)
                    dve.wait_ge(y_added, u + 1)
                    nc.vector.scalar_tensor_tensor(Y[:, j, :], psY[j][:], K[:, ds(e, 1)], gb[:, j, :], ALU.add, ALU.mult).then_inc(y_done, 1)

                def pair(c, ep):
                    for j in range(2):
                        u = NE * c + 2 * ep + j
                        split(u + 1, 1 - j)
                        gate(u, 2 * ep + j, j)

                def add(c):
                    dve.wait_ge(sum_transposed, 1 + c + 1)
                    nc.vector.tensor_tensor(X[:, ds(TPC * c, TPC), :], psT[:].rearrange("p (t d) -> p t d", d=D),
                                            X[:, ds(TPC * c, TPC), :], ALU.add).then_inc(x_added, 1)

                split(0, 0)
                pair(0, 0)
                with dve.Fori(1, NE // 2) as ep:
                    pair(0, ep)
                with dve.Fori(1, NCH) as c:
                    pair(c, 0)
                    add(c - 1)
                    with dve.Fori(1, NE // 2) as ep:
                        pair(c, ep)
                add(NCH - 1)

            @block.gpsimd
            def _(pool):
                pool.sem_inc(y_added, 2)

                def more(u, j):
                    pool.wait_ge(y_done, 2 + u + 1)
                    pool.wait_ge(y_added, 2 + u)
                    nc.gpsimd.tensor_tensor(acc[:], acc[:], Y[:, j, :], ALU.add).then_inc(y_added, 1)

                with pool.Fori(0, NCH) as c:
                    pool.wait_ge(y_done, 2 + NE * c + 2)
                    nc.gpsimd.tensor_tensor(acc[:], Y[:, 0, :], Y[:, 1, :], ALU.add).then_inc(y_added, 2)
                    with pool.Fori(1, NE // 2 - 1) as ep:
                        for j in range(2):
                            more(NE * c + 2 * ep + j, j)
                    more(NE * c + NE - 2, 0)
                    pool.wait_ge(y_done, 2 + NE * c + NE)
                    pool.wait_ge(y_added, 2 + NE * c + NE - 1)
                    pool.wait_ge(sum_transposed, 1 + c)
                    nc.gpsimd.tensor_tensor(accf[:], acc[:], Y[:, 1, :], ALU.add).then_inc(chunk_step, 1)
                    pool.wait_ge(chunk_step, c + 1)
                    pool.sem_inc(y_added, 1)
                    pool.sem_inc(summed, 1)


def full_attention(nc, X, io):
    with Stage(nc, "full") as st:
        sb = st.sb
        woh, wol = sb("woh", [P, HB // 2, D], F16), sb("wol", [P, HB // 2, D], F16)
        OTh, OTl = sb("OTh", [P, HB // 2, T], F16), sb("OTl", [P, HB // 2, T], F16)
        with Stage(nc, "fullw") as st2:
            sb = st2.sb
            wTh, wTl = sb("wTh", [P, T], F16), sb("wTl", [P, T], F16)
            wq = sb("wqh", [P, HB, P], F16), sb("wql", [P, HB, P], F16)
            wk = sb("wkh", [P, HB, P], F16), sb("wkl", [P, HB, P], F16)
            wv = sb("wvh", [P, HB, DB], F16), sb("wvl", [P, HB, DB], F16)
            full_prepare(nc, X, wTh, wTl, wq, wk, wv, (woh, wol), io)
            full_heads(nc, wTh, wTl, wq, wk, wv, OTh, OTl, io)
        full_output(nc, X, OTh, OTl, woh, wol, io)


def full_prepare(nc, X, wTh, wTl, wq, wk, wv, wo, io):
    with Stage(nc, "bp") as st:
        sb, ps, sem = st.sb, st.ps, st.sem
        names = [("wqB", wq, HB * P), ("wkB", wk, HB * P), ("wvB", wv, HB * DB), ("woutB", wo, HB // 2 * D)]
        w32 = [sb(n, [P, size]) for n, _, size in names]
        ident = sb("ident", [P, P])
        seen = sb("seen", [P, 1])
        halfneg, epsc = sb("halfneg", [P, TPC]), sb("epsc", [P, TPC])
        stats, mv = sb("stats", [P, 2, TPC, 6]), sb("mv", [P, 2, TPC, 2])
        vare, rstd = sb("vare", [P, 2, TPC]), sb("rstd", [P, 2, TPC])
        w = sb("w", [P, 2, TPC, D])
        psX = [ps(f"psX{h}", [P, CH]) for h in range(2)]

        loaded, set_up, w_hi, w_lo = sem("loaded"), sem("set_up"), sem("w_hi"), sem("w_lo")
        bn_done, stats_ready, eps_added, rstd_ready = sem("bn_done"), sem("stats_ready"), sem("eps_added"), sem("rstd_ready")
        w_ready, transposed, wT_hi, wT_lo, added = sem("w_ready"), sem("transposed"), sem("wT_hi"), sem("wT_lo"), sem("added")
        LOADED = 5 * 16

        with st.block() as block:

            @block.sync
            def _(sp):
                sp.dma_start(ident[:], io["ident"]).then_inc(loaded, 16)
                for (n, _, _), dst in zip(names, w32):
                    src = io[n]
                    if n == "wvB":
                        sp.dma_start(dst[:], src).then_inc(loaded, 16)
                    else:
                        sp.dma_start(dst[:], src.rearrange("p a b -> p (a b)")).then_inc(loaded, 16)

            @block.gpsimd
            def _(pool):
                nc.gpsimd.memset(halfneg[:], -0.5).then_inc(set_up, 1)
                nc.gpsimd.memset(epsc[:], EPS).then_inc(set_up, 1)
                pool.wait_ge(set_up, 2)
                with pool.Fori(0, NCH // 2) as b:
                    for h in range(2):
                        c = 2 * b + h
                        pool.wait_ge(stats_ready, c + 1)
                        nc.gpsimd.tensor_tensor(vare[:, h], mv[:, h, :, 1], epsc[:], ALU.add).then_inc(eps_added, 1)
                        pool.wait_ge(eps_added, c + 1)
                        nc.gpsimd.tensor_tensor(rstd[:, h], vare[:, h], halfneg[:], ALU.pow).then_inc(rstd_ready, 1)

            @block.scalar
            def _(act):
                act.wait_ge(loaded, LOADED)
                for i, (_, (hi, _), _) in enumerate(names):
                    nc.scalar.activation(hi[:].rearrange("p a b -> p (a b)"), w32[i][:], ACT.Copy).then_inc(w_hi, 1)
                with act.Fori(0, NCH // 2) as b:
                    for h in range(2):
                        c = 2 * b + h
                        act.wait_ge(transposed, c + 1)
                        nc.scalar.activation(wTh[:, ds(c * CH, CH)], psX[h][:], ACT.Copy).then_inc(wT_hi, 1)

            @block.vector
            def _(dve):
                dve.sem_inc(wT_lo, 1)
                def stats_of(c, h):
                    for j in range(TPC):
                        nc.vector.bn_stats(stats[:, h, j, :], X[:, TPC * c + j, :]).then_inc(bn_done, 1)
                    dve.wait_ge(bn_done, TPC * c + TPC)
                    nc.vector.tensor_copy(seen[:], stats[:, h, TPC - 1, 0:1])
                    for j in range(TPC):
                        ins = nc.vector.bn_aggr(mv[:, h, j, :], stats[:, h, j, :])
                    ins.then_inc(stats_ready, 1)

                def normalise(c, h):
                    dve.wait_ge(rstd_ready, c + 1)
                    for j in range(TPC):
                        ins = nc.vector.tensor_scalar(w[:, h, j, :], X[:, TPC * c + j, :], mv[:, h, j, 0:1],
                                                      rstd[:, h, j:j + 1], ALU.subtract, ALU.mult)
                    ins.then_inc(w_ready, 1)

                def chunk(c, h, more):
                    if more:
                        stats_of(c + 2, h)
                    dve.wait_ge(w_ready, c + 1)
                    nc.vector.scalar_tensor_tensor(
                        X[:, ds(TPC * c, TPC), :], w[:, h], RSQRT2, X[:, ds(TPC * c, TPC), :],
                        ALU.mult, ALU.add).then_inc(added, 1)
                    if more or h == 0:
                        normalise(c + 1, 1 - h)
                    dve.wait_ge(wT_hi, c + 1)
                    nc.vector.tensor_tensor(wTl[:, ds(c * CH, CH)], psX[h][:], wTh[:, ds(c * CH, CH)], ALU.subtract).then_inc(wT_lo, 1)

                stats_of(0, 0)
                stats_of(1, 1)
                normalise(0, 0)
                with dve.Fori(0, NCH // 2 - 1) as b:
                    for h in range(2):
                        chunk(2 * b + h, h, True)
                for h in range(2):
                    chunk(NCH - 2 + h, h, False)
                for i, (_, (hi, lo), _) in enumerate(names):
                    dve.wait_ge(w_hi, i + 1)
                    nc.vector.tensor_tensor(lo[:].rearrange("p a b -> p (a b)"), w32[i][:],
                                            hi[:].rearrange("p a b -> p (a b)"), ALU.subtract).then_inc(w_lo, 1)

            @block.tensor
            def _(pe):
                pe.wait_ge(loaded, LOADED)
                with pe.Fori(0, NCH // 2) as b:
                    for h in range(2):
                        pe.wait_ge(w_ready, 2 * b + h + 1)
                        pe.wait_ge(wT_lo, 1 + 2 * b)
                        for j in range(TPC):
                            ins = nc.tensor.transpose(psX[h][:, j * P:(j + 1) * P], w[:, h, j, :], ident[:])
                        ins.then_inc(transposed, 1)


def full_heads(nc, wTh, wTl, wq, wk, wv, OTh, OTl, io):
    with Stage(nc, "bh") as st:
        sb, ps, sem = st.sb, st.ps, st.sem
        HALF = S // 2
        U = B * HB
        MROW = DB
        identh = sb("identh", [P, P], F16)
        ones = sb("ones", [P, DB])
        bq, bk, bvb = sb("bq", [P, HB]), sb("bk", [P, HB]), sb("bvb", [P, HB, DB])
        KH = sb("KH", [P, 2, S], F16)
        K1 = sb("K1", [P, 2, S], F16)
        QH = sb("QH", [P, 2, S], F16)
        QL = sb("QL", [P, 2, S], F16)
        V = sb("V", [P, 2, KT, DB])
        Mn, Ml = sb("Mn", [P, KT]), sb("Ml", [P, KT, 2], F16)
        E = sb("E", [P, KT, S])
        E1, E2 = sb("E1", [P, S]), sb("E2", [P, S])
        rden = sb("rden", [P, HALF])
        O = sb("O", [P, S])
        psA = ps("psA", [P, 2, HALF])
        psS = [ps(f"psS{i}", [P, 2, HALF]) for i in range(2)]
        psO = [ps(f"psO{i}", [P, HALF]) for i in range(2)]

        loaded, set_up = sem("loaded"), sem("set_up")
        k_done, v_done, q_done = sem("k_done"), sem("v_done"), sem("q_done")
        k_hi, k_split, k_copied, v_ready, q_hi, q_split = (
            sem("k_hi"), sem("k_split"), sem("k_copied"), sem("v_ready"), sem("q_hi"), sem("q_split"))
        rows_done, max_done, max_hi, max_split, max_row_done, max_row = (
            sem("rows_done"), sem("max_done"), sem("max_hi"), sem("max_split"), sem("max_row_done"), sem("max_row"))
        scores_done = sem("scores_done")
        exp_done = sem("exp_done")
        value_done = sem("value_done")
        sum1 = sem("sum1")
        sum2 = sem("sum2")
        den_done, recip_done = sem("den_done"), sem("recip_done")
        normed = sem("normed")
        o_hi = sem("o_hi")
        o_lo = sem("o_lo")
        half_normed = sem("half_normed")

        batch = lambda u: u // HB
        head = lambda u: u % HB

        with st.block() as block:

            @block.sync
            def _(sp):
                sp.dma_start(identh[:], io["identh"]).then_inc(loaded, 16)
                sp.dma_start(bq[:], io["bqB"]).then_inc(loaded, 16)
                sp.dma_start(bk[:], io["bkB"]).then_inc(loaded, 16)
                sp.dma_start(bvb[:].rearrange("p a b -> p (a b)"),
                             io["bvB"].rearrange("(a n) -> a n", a=1).broadcast_to([P, HB * DB])).then_inc(loaded, 16)

            LOADED = 4 * 16

            @block.tensor
            def _(pe):
                def three(out, a, b, first=True, last=True):
                    nc.tensor.matmul(out, a[0], b[0], start=first, stop=False)
                    nc.tensor.matmul(out, a[0], b[1], start=False, stop=False)
                    return nc.tensor.matmul(out, a[1], b[0], start=False, stop=last)

                def tokens(u, at, n):
                    return wTh[:, ds(batch(u) * S + at, n)], wTl[:, ds(batch(u) * S + at, n)]

                def make_k(u):
                    for a in range(2):
                        ins = three(psA[:, a], [x[:, ds(head(u), 1), :] for x in wk], tokens(u, a * HALF, HALF))
                    ins.then_inc(k_done, 1)

                def make_v(u):
                    pe.wait_ge(k_split, u + 1)
                    for t in range(KT):
                        ins = three(psA[:, 0, t * DB:(t + 1) * DB], tokens(u, t * P, P), [x[:, ds(head(u), 1), :] for x in wv])
                    ins.then_inc(v_done, 1)

                def make_q(u):
                    pe.wait_ge(v_ready, u + 1)
                    for a in range(2):
                        ins = three(psA[:, a], [x[:, ds(head(u), 1), :] for x in wq], tokens(u, a * HALF, HALF))
                    ins.then_inc(q_done, 1)

                def rows(u, s, t):
                    pe.wait_ge(q_split, u + 1)
                    pe.wait_ge(max_done, KT * u + t)
                    for a in range(2):
                        ins = nc.tensor.matmul(psA[:, a], QH[:, s, t * P:(t + 1) * P], KH[:, s, a * HALF:(a + 1) * HALF],
                                               start=True, stop=True)
                    ins.then_inc(rows_done, 1)

                def max_rows(u):
                    pe.wait_ge(max_split, u + 1)
                    for t in range(KT):
                        ins = nc.tensor.matmul(psA[MROW:MROW + 2, t // 4, t % 4 * P:(t % 4 + 1) * P], Ml[:, t, :], identh[:],
                                               start=True, stop=True)
                    ins.then_inc(max_row_done, 1)

                def scores(u, s, t):
                    pe.wait_ge(exp_done, KT * u + t + 1)
                    if t == 0:
                        pe.wait_ge(k_copied, u + 1)
                        pe.wait_ge(max_row, u + 1)
                    keys = slice(t * P, (t + 1) * P)
                    for a in range(2):
                        q = slice(a * HALF, (a + 1) * HALF)
                        nc.tensor.matmul(psS[t % 2][:, a], KH[:, s, keys], QH[:, s, q], start=True, stop=False)
                        ins = nc.tensor.matmul(psS[t % 2][:, a], K1[:, s, keys], QL[:, s, q], start=False, stop=True)
                    ins.then_inc(scores_done, 1)

                def values(u, s, t):
                    pe.wait_ge(exp_done, 2 + KT * u + t + 1)
                    if t == 0:
                        pe.wait_ge(normed, u + 1)
                        pe.wait_ge(v_ready, u + 1)
                    for a in range(2):
                        ins = nc.tensor.matmul(psO[s][DB * a:DB * (a + 1), :], V[:, s, t, :], E[:, t, a * HALF:(a + 1) * HALF],
                                               start=(t == 0), stop=(t == KT - 1))
                    ins.then_inc(value_done, 1)

                def denominators(u):
                    pe.wait_ge(sum1, 2 + 2 * u + 2)
                    pe.wait_ge(sum2, 4 + 4 * u + 4)
                    for a in range(2):
                        q = slice(a * HALF, (a + 1) * HALF)
                        nc.tensor.matmul(psA[DB * a:DB * (a + 1), 0], ones[:], E1[:, q], start=True, stop=False)
                        ins = nc.tensor.matmul(psA[DB * a:DB * (a + 1), 0], ones[:], E2[:, q], start=False, stop=True)
                    ins.then_inc(den_done, 1)

                def unit(u, s, first=False, last=False):
                    n, o = u + 1, 1 - s
                    if not last:
                        pe.wait_ge(max_row, u + 1)
                        make_k(n)
                    scores(u, s, 1)
                    values(u, s, 0)
                    if not last:
                        make_v(n)
                    scores(u, s, 2)
                    if not last:
                        make_q(n)
                    values(u, s, 1)
                    if not first:
                        if not last:
                            pe.wait_ge(q_split, u + 2)
                        denominators(u - 1)
                    scores(u, s, 3)
                    if not last:
                        if not first:
                            pe.wait_ge(recip_done, u)
                        rows(n, o, 0)
                    values(u, s, 2)
                    for t in range(3, 6):
                        if not last:
                            rows(n, o, 2 * t - 5)
                        scores(u, s, t + 1)
                        if not last:
                            rows(n, o, 2 * t - 4)
                        values(u, s, t)
                    if not last:
                        rows(n, o, 7)
                    scores(u, s, 7)
                    values(u, s, 6)
                    if not last:
                        max_rows(n)
                    values(u, s, 7)
                    if not last:
                        scores(n, o, 0)

                pe.wait_ge(loaded, LOADED)
                pe.wait_ge(set_up, 4)
                make_k(0)
                make_v(0)
                make_q(0)
                for t in range(KT):
                    rows(0, 0, t)
                max_rows(0)
                scores(0, 0, 0)
                unit(0, 0, first=True)
                unit(1, 1)
                with pe.Fori(1, U // 2 - 1) as pr:
                    for s in range(2):
                        unit(2 * pr + s, s)
                unit(U - 2, 0)
                unit(U - 1, 1, last=True)
                pe.wait_ge(recip_done, U - 1)
                denominators(U - 1)

            @block.scalar
            def _(act):
                act.sem_inc(exp_done, 2)

                def hi(u, s, dst, bias, done, signal):
                    act.wait_ge(done, u + 1)
                    nc.scalar.activation(dst[:, s, :], psA[:].rearrange("p a q -> p (a q)"), ACT.Identity,
                                         bias=bias[:, ds(head(u), 1)]).then_inc(signal, 1)

                def row(u, s):
                    act.wait_ge(max_row_done, u + 1)
                    nc.scalar.activation(QL[MROW:MROW + 2, s, :], psA[MROW:MROW + 2].rearrange("p a q -> p (a q)"),
                                         ACT.Copy).then_inc(max_row, 1)

                def exp(u, s, t):
                    act.wait_ge(scores_done, KT * u + t + 1)
                    act.wait_ge(value_done, KT * u + t + 1)
                    if t in (0, 2, 4):
                        act.wait_ge(sum1, 2 * u + (1 if t < 4 else 2))
                    else:
                        act.wait_ge(sum2, 4 * u + {1: 1, 3: 1, 5: 2, 6: 3, 7: 4}[t])
                    nc.scalar.activation(E[:, t, :], psS[t % 2][:].rearrange("p a q -> p (a q)"), ACT.Exp,
                                         scale=SCALE_B).then_inc(exp_done, 1)

                def out_hi(u, s):
                    act.wait_ge(half_normed, 2 * u + 2)
                    rows_ = slice(DB * s, DB * (s + 1))
                    nc.scalar.activation(OTh[rows_, ds(head(u) // 2, 1), ds(batch(u) * S, S)], O[rows_, None, :],
                                         ACT.Copy).then_inc(o_hi, 1)

                def unit(u, s, first=False, last=False):
                    n, o = u + 1, 1 - s
                    exp(u, s, 0)
                    if not last:
                        hi(n, o, KH, bk, k_done, k_hi)
                    exp(u, s, 1)
                    exp(u, s, 2)
                    if not last:
                        hi(n, o, QH, bq, q_done, q_hi)
                    exp(u, s, 3)
                    exp(u, s, 4)
                    if not first:
                        out_hi(u - 1, o)
                    for t in range(5, KT):
                        exp(u, s, t)
                    if not last:
                        row(n, o)

                act.wait_ge(loaded, LOADED)
                hi(0, 0, KH, bk, k_done, k_hi)
                hi(0, 0, QH, bq, q_done, q_hi)
                act.wait_ge(set_up, 4)
                row(0, 0)
                unit(0, 0, first=True)
                unit(1, 1)
                with act.Fori(1, U // 2 - 1) as pr:
                    for s in range(2):
                        unit(2 * pr + s, s)
                unit(U - 2, 0)
                unit(U - 1, 1, last=True)
                out_hi(U - 1, 1)

            @block.vector
            def _(dve):
                dve.sem_inc(sum1, 2)
                dve.sem_inc(normed, 2)
                flat = lambda x: x.rearrange("p a q -> p (a q)")

                def k_low(u, s):
                    dve.wait_ge(k_hi, u + 1)
                    nc.vector.scalar_tensor_tensor(KH[DB:P, s, :], flat(psA[DB:P]), bk[DB:P, ds(head(u), 1)], KH[DB:P, s, :],
                                                   ALU.add, ALU.subtract).then_inc(k_split, 1)
                    nc.vector.tensor_copy(K1[0:DB, s, :], KH[0:DB, s, :]).then_inc(k_copied, 1)

                def v_bias(u, s):
                    dve.wait_ge(v_done, u + 1)
                    nc.vector.tensor_tensor(V[:, s], psA[:, 0].rearrange("p (t d) -> p t d", d=DB),
                                            bvb[:, ds(head(u), 1), :].broadcast_to([P, KT, DB]), ALU.add).then_inc(v_ready, 1)

                def q_low(u, s):
                    dve.wait_ge(q_hi, u + 1)
                    nc.vector.scalar_tensor_tensor(QL[0:DB, s, :], flat(psA[0:DB]), bq[0:DB, ds(head(u), 1)], QH[0:DB, s, :],
                                                   ALU.add, ALU.subtract).then_inc(q_split, 1)

                def row_max(u, t):
                    dve.wait_ge(rows_done, KT * u + t + 1)
                    nc.vector.tensor_reduce(Mn[:, t:t + 1], flat(psA[:]), AX_X, ALU.max, negate=True).then_inc(max_done, 1)

                def max_halves(u):
                    dve.wait_ge(max_done, KT * u + KT)
                    nc.vector.tensor_copy(Ml[:, :, 0], Mn[:]).then_inc(max_hi, 1)
                    dve.wait_ge(max_hi, u + 1)
                    nc.vector.tensor_tensor(Ml[:, :, 1], Mn[:], Ml[:, :, 0], ALU.subtract).then_inc(max_split, 1)

                def sum_even(u):
                    dve.wait_ge(exp_done, 2 + KT * u + 3)
                    dve.wait_ge(den_done, u)
                    nc.vector.tensor_tensor(E1[:], E[:, 0, :], E[:, 2, :], ALU.add).then_inc(sum1, 1)

                def sum_more(u):
                    dve.wait_ge(exp_done, 2 + KT * u + 5)
                    dve.wait_ge(sum1, 2 + 2 * u + 1)
                    nc.vector.tensor_tensor(E1[:], E1[:], E[:, 4, :], ALU.add).then_inc(sum1, 1)

                def norm(u, s):
                    dve.wait_ge(den_done, u + 1)
                    nc.vector.reciprocal(rden[:], psA[:, 0]).then_inc(recip_done, 1)
                    dve.wait_ge(recip_done, u + 1)
                    dve.wait_ge(value_done, KT + KT * u + KT)
                    dve.wait_ge(o_lo, u + 1)
                    for a in range(2):
                        src = slice(DB * a, DB * (a + 1))
                        nc.vector.tensor_tensor(O[DB * s:DB * (s + 1), a * HALF:(a + 1) * HALF], psO[s][src, :], rden[src, :],
                                                ALU.mult).then_inc(half_normed, 1)
                    dve.wait_ge(half_normed, 2 * u + 2)
                    dve.sem_inc(normed, 1)

                def unit(u, s, first=False, last=False):
                    n, o = u + 1, 1 - s
                    if not last:
                        k_low(n, o)
                        v_bias(n, o)
                        q_low(n, o)
                    if not first:
                        norm(u - 1, o)
                    if not last:
                        row_max(n, 0)
                    sum_even(u)
                    if not last:
                        for t in range(1, 5):
                            row_max(n, t)
                    sum_more(u)
                    if not last:
                        for t in range(5, KT):
                            row_max(n, t)
                        max_halves(n)

                nc.vector.memset(ones[:], 1.0).then_inc(set_up, 1)
                nc.vector.memset(K1[DB:P, :, :], 0.0).then_inc(set_up, 1)
                nc.vector.memset(QL[DB:P, :, :], 0.0).then_inc(set_up, 1)
                dve.wait_ge(set_up, 3)
                nc.vector.memset(K1[DB:DB + 2, :, :], 1.0).then_inc(set_up, 1)
                dve.wait_ge(loaded, LOADED)
                k_low(0, 0)
                v_bias(0, 0)
                q_low(0, 0)
                for t in range(KT):
                    row_max(0, t)
                max_halves(0)
                unit(0, 0, first=True)
                unit(1, 1)
                with dve.Fori(1, U // 2 - 1) as pr:
                    for s in range(2):
                        unit(2 * pr + s, s)
                unit(U - 2, 0)
                unit(U - 1, 1, last=True)
                norm(U - 1, 1)

            @block.gpsimd
            def _(pool):
                pool.sem_inc(sum2, 4)
                pool.sem_inc(value_done, KT)
                pool.sem_inc(o_lo, 2)
                def sums(u, steps):
                    for i in steps:
                        t = (3, 5, 6, 7)[i]
                        pool.wait_ge(exp_done, 2 + KT * u + t + 1)
                        if i == 0:
                            pool.wait_ge(den_done, u)
                            nc.gpsimd.tensor_tensor(E2[:], E[:, 1, :], E[:, 3, :], ALU.add).then_inc(sum2, 1)
                        else:
                            pool.wait_ge(sum2, 4 + 4 * u + i)
                            nc.gpsimd.tensor_tensor(E2[:], E2[:], E[:, t, :], ALU.add).then_inc(sum2, 1)

                def out_lo(u, s, sums_so_far):
                    pool.wait_ge(sum2, 4 + sums_so_far)
                    pool.wait_ge(o_hi, u + 1)
                    rows_ = slice(DB * s, DB * (s + 1))
                    nc.gpsimd.tensor_tensor(OTl[rows_, ds(head(u) // 2, 1), ds(batch(u) * S, S)], O[rows_, None, :],
                                            OTh[rows_, ds(head(u) // 2, 1), ds(batch(u) * S, S)], ALU.subtract).then_inc(o_lo, 1)

                def unit(u, s, first=False, last=False):
                    sums(u, (0,))
                    if not first:
                        out_lo(u - 1, 1 - s, 4 * u + 1)
                        pool.wait_ge(o_lo, 2 + u)
                    sums(u, (1, 2, 3))

                unit(0, 0, first=True)
                unit(1, 1)
                with pool.Fori(1, U // 2 - 1) as pr:
                    for s in range(2):
                        unit(2 * pr + s, s)
                unit(U - 2, 0)
                unit(U - 1, 1, last=True)
                out_lo(U - 1, 1, 4 * U)
                pool.wait_ge(o_lo, 2 + U)


def full_output(nc, X, OTh, OTl, woh, wol, io):
    with Stage(nc, "bo") as st:
        sb, ps, sem = st.sb, st.ps, st.sem
        bob, gb, bb = sb("bob", [P, D]), sb("gb", [P, D]), sb("bb", [P, D])
        g2, b2 = sb("g2", [P, D]), sb("b2", [P, D])
        seen = sb("seen", [P, 1])
        halfneg, epsc = sb("halfneg", [P, TPC]), sb("epsc", [P, TPC])
        stats, mv = sb("stats", [P, 2, TPC, 6]), sb("mv", [P, 2, TPC, 2])
        vare, rstd = sb("vare", [P, 2, TPC]), sb("rstd", [P, 2, TPC])
        y, yn = sb("y", [P, 2, TPC, D]), sb("yn", [P, 2, TPC, D])
        psY = [ps(f"psY{h}", [P, TPC, D]) for h in range(2)]

        loaded, set_up, scaled = sem("loaded"), sem("set_up"), sem("scaled")
        projected, biased = sem("projected"), sem("biased")
        bn_done, stats_ready, eps_added, rstd_ready = sem("bn_done"), sem("stats_ready"), sem("eps_added"), sem("rstd_ready")
        normed, gained, shifted, added = sem("normed"), sem("gained"), sem("shifted"), sem("added")

        with st.block() as block:

            @block.sync
            def _(sp):
                for dst, n in ((bob, "boutB"), (gb, "lngB"), (bb, "lnbB")):
                    sp.dma_start(dst[:], io[n].rearrange("(a n) -> a n", a=1).broadcast_to([P, D])).then_inc(loaded, 16)

            @block.tensor
            def _(pe):
                with pe.Fori(0, NCH // 2) as b:
                    for h in range(2):
                        c = 2 * b + h
                        pe.wait_ge(biased, 1 + 2 * b)
                        for j in range(TPC):
                            for m in range(HB // 2):
                                o = psY[h][:, j, :]
                                oh, ol = OTh[:, m, ds(c * CH + j * P, P)], OTl[:, m, ds(c * CH + j * P, P)]
                                nc.tensor.matmul(o, oh, woh[:, m, :], start=(m == 0), stop=False)
                                nc.tensor.matmul(o, oh, wol[:, m, :], start=False, stop=False)
                                ins = nc.tensor.matmul(o, ol, woh[:, m, :], start=False, stop=(m == HB // 2 - 1))
                        ins.then_inc(projected, 1)

            @block.vector
            def _(dve):
                dve.sem_inc(added, 1)
                dve.sem_inc(biased, 1)
                wide = lambda a: a[:, None, :].broadcast_to([P, TPC, D])

                def stats_of(c, h):
                    dve.wait_ge(projected, c + 1)
                    nc.vector.tensor_tensor(y[:, h], psY[h][:], wide(bob), ALU.add).then_inc(biased, 1)
                    dve.wait_ge(biased, 1 + c + 1)
                    for j in range(TPC):
                        nc.vector.bn_stats(stats[:, h, j, :], y[:, h, j, :]).then_inc(bn_done, 1)
                    dve.wait_ge(bn_done, TPC * c + TPC)
                    nc.vector.tensor_copy(seen[:], stats[:, h, TPC - 1, 0:1])
                    for j in range(TPC):
                        ins = nc.vector.bn_aggr(mv[:, h, j, :], stats[:, h, j, :])
                    ins.then_inc(stats_ready, 1)

                def normalise(c, h):
                    dve.wait_ge(rstd_ready, c + 1)
                    dve.wait_ge(added, 1 + 2 * (c // 2))
                    for j in range(TPC):
                        ins = nc.vector.tensor_scalar(yn[:, h, j, :], y[:, h, j, :], mv[:, h, j, 0:1],
                                                      rstd[:, h, j:j + 1], ALU.subtract, ALU.mult)
                    ins.then_inc(normed, 1)
                    dve.wait_ge(normed, c + 1)
                    nc.vector.tensor_tensor(yn[:, h], yn[:, h], wide(g2), ALU.mult).then_inc(gained, 1)
                    dve.wait_ge(gained, c + 1)
                    nc.vector.tensor_tensor(X[:, ds(TPC * c, TPC), :], yn[:, h], X[:, ds(TPC * c, TPC), :], ALU.add).then_inc(added, 1)

                dve.wait_ge(loaded, 48)
                nc.vector.tensor_scalar(g2[:], gb[:], RSQRT2, None, ALU.mult).then_inc(scaled, 1)
                nc.vector.tensor_scalar(b2[:], bb[:], RSQRT2, None, ALU.mult).then_inc(scaled, 1)
                dve.wait_ge(scaled, 2)
                nc.vector.tensor_tensor(X[:], X[:], b2[:, None, :].broadcast_to([P, NT, D]), ALU.add).then_inc(shifted, 1)
                dve.wait_ge(shifted, 1)
                stats_of(0, 0)
                with dve.Fori(0, NCH // 2 - 1) as b:
                    for h in range(2):
                        stats_of(2 * b + h + 1, 1 - h)
                        normalise(2 * b + h, h)
                stats_of(NCH - 1, 1)
                normalise(NCH - 2, 0)
                normalise(NCH - 1, 1)
                dve.wait_ge(added, 1 + NCH)

            @block.gpsimd
            def _(pool):
                nc.gpsimd.memset(halfneg[:], -0.5).then_inc(set_up, 1)
                nc.gpsimd.memset(epsc[:], EPS).then_inc(set_up, 1)
                pool.wait_ge(set_up, 2)
                with pool.Fori(0, NCH // 2) as b:
                    for h in range(2):
                        c = 2 * b + h
                        pool.wait_ge(stats_ready, c + 1)
                        nc.gpsimd.tensor_tensor(vare[:, h], mv[:, h, :, 1], epsc[:], ALU.add).then_inc(eps_added, 1)
                        pool.wait_ge(eps_added, c + 1)
                        nc.gpsimd.tensor_tensor(rstd[:, h], vare[:, h], halfneg[:], ALU.pow).then_inc(rstd_ready, 1)


def transformer_layer(nc, io, out):
    X_ctx = ExitStack()
    with X_ctx:
        X = X_ctx.enter_context(nc.sbuf_tensor("X", [P, NT, D], F32))
        with Stage(nc, "band") as st:
            Q4 = st.sb("Q4", [P, 4, T], F16)
            K4 = st.sb("K4", [P, 4, WIN + T], F16)
            Vhi, Vlo = st.sb("Vhi", [P, NB, HA, VW], F16), st.sb("Vlo", [P, NB, HA, VW], F16)
            band_project(nc, X, Q4, K4, Vhi, Vlo, io)
            band_attend(nc, X, Q4, K4, Vhi, Vlo, io)
        experts(nc, X, io, "f1")
        full_attention(nc, X, io)
        experts(nc, X, io, "f2")
        with Stage(nc, "out") as st:
            stored = st.sem("stored")
            with st.block() as block:
                @block.sync
                def _(sp):
                    sp.dma_start(out.rearrange("b (t p) d -> p (b t) d", p=P), X[:]).then_inc(stored, 16)
                    sp.wait_ge(stored, 16)


def shape_constants():
    half = D // 2
    inv = (np.float32(1.0) / np.power(10000.0, np.arange(half) / half).astype(np.float32)).astype(np.float32)
    ang = (np.arange(S, dtype=np.float32)[:, None] * inv[None, :]).T
    c, s = np.cos(ang), np.sin(ang)
    q, k = np.arange(P)[:, None] % WIN, np.arange(P)[None, :]
    band = (k >= q) & (k <= q + WIN)
    row = np.arange(P)
    fold = np.zeros((P, 2, P), np.float32)
    for j in range(2):
        fold[row, j, WIN * j + row % WIN] = 1.0
    return {
        "cos": np.concatenate([c, c]).astype(np.float32),
        "sin": np.concatenate([-s, s]).astype(np.float32),
        "ident": np.eye(P, dtype=np.float32),
        "identh": np.eye(P, dtype=np.float16),
        "bandm": np.where(np.stack([band & (k >= WIN), band], 1), 0.0, -1e30).astype(np.float32),
        "headm": ((row[:, None] % 32) // DA == np.arange(4)[None, :]).astype(np.float16),
        "parm": (row[:, None] // WIN == np.arange(2)[None, :]).astype(np.float32),
        "fold": fold,
        "rank": np.broadcast_to((NE - np.arange(NE)).astype(np.float32), (P, NE)).copy(),
    }


def laid_out(a):
    f = {k: np.asarray(v) for k, v in a.items()}
    wq, wk, wv = f["L0_attn_a_Wq"], f["L0_attn_a_Wk"], f["L0_attn_a_Wv"]
    bq, bk = f["L0_attn_a_bq"], f["L0_attn_a_bk"]
    half = D // 2
    roll = lambda x: np.concatenate([x[half:], x[:half]])
    wqk = f["L0_attn_b_W_qk"].reshape(D, HB, DB, 2)
    bqk = f["L0_attn_b_b_qk"].reshape(HB, DB, 2)
    dup = lambda x: np.concatenate([x, x], axis=-1)
    c = np.ascontiguousarray
    return {
        "x": f["L0_attn_a_hidden_state"],
        "wA": c(np.stack([wq.T, roll(wq).T, wk.T, roll(wk).T, wv.T], axis=1)),
        "biasA": c(np.stack([bq, roll(bq), bk, roll(bk)], axis=1)),
        "bv": f["L0_attn_a_bv"],
        "woT": c(f["L0_attn_a_Wo"].T),
        "bo": f["L0_attn_a_bo"],
        "wqB": c(dup(wqk[..., 0])), "wkB": c(dup(wqk[..., 1])),
        "bqB": c(dup(bqk[..., 0]).T), "bkB": c(dup(bqk[..., 1]).T),
        "wvB": f["L0_attn_b_W_v"], "bvB": f["L0_attn_b_b_v"],
        "woutB": c(f["L0_attn_b_W_out"].reshape(HB // 2, 2 * DB, D).transpose(1, 0, 2)),
        "boutB": f["L0_attn_b_b_out"],
        "lngB": f["L0_attn_b_ln_gamma"], "lnbB": f["L0_attn_b_ln_beta"],
        "gammaF": c(f["L0_ffn_gamma"][:, None]), "betaF": c(f["L0_ffn_beta"][:, None]),
        "wrF": f["L0_ffn_Wr"], "brF": f["L0_ffn_br"],
        "w1F": c(f["L0_ffn_W1"].transpose(1, 0, 2)),
        "b1F": c(f["L0_ffn_b1"].reshape(NE, FC, P).transpose(2, 0, 1)),
        "w2F": c(f["L0_ffn_W2"].reshape(NE, FC, P, D).transpose(2, 0, 1, 3)),
        "b2F": c(f["L0_ffn_b2"].T),
        **shape_constants(),
    }


def kernel(**inputs):
    import concourse.bacc as bacc
    from concourse.bass_utils import run_bass_kernel_spmd

    nc = bacc.Bacc("TRN2", target_bir_lowering=False, num_devices=1)
    arrays = laid_out(inputs)
    io = {n: nc.dram_tensor(f"in_{n}", a.shape, mybir.dt.from_np(a.dtype), kind="ExternalInput").ap()
          for n, a in arrays.items()}
    out = nc.dram_tensor("out", (B, S, D), F32, kind="ExternalOutput").ap()
    transformer_layer(nc, io, out)
    r = run_bass_kernel_spmd(nc, [{f"in_{n}": a for n, a in arrays.items()}], core_ids=[0])
    return r.results[0]["out"]
```

```python
from contextlib import ExitStack

import numpy as np

import concourse.bass as bass
from concourse import mybir

F32 = mybir.dt.float32
F16 = mybir.dt.float16
BF16 = mybir.dt.bfloat16
ALU = mybir.AluOpType
ACT = mybir.ActivationFunctionType
AX_X = mybir.AxisListType.X
ds = bass.ds

P = 128
D = 128
B, S = 4, 1024
T = B * S
NT = T // P
CH = 512
NCH = T // CH
TPC = CH // P
EPS = 1e-5

HA, DA = 16, 8
WIN = 64
NB = T // WIN
SCALE_A = 1.0 / float(np.sqrt(np.float32(DA)))
VW = DA + 1

HB, DB = 8, 64
SCALE_B = DB ** -0.5
KT = S // P
RSQRT2 = 2 ** -0.5

NE, FF = 8, 512
FC = FF // P
WS = 64.0



class Stage:

    def __init__(self, nc, tag):
        self.nc, self.tag, self.ctx, self.sems = nc, tag, ExitStack(), []

    def __enter__(self):
        self.ctx.__enter__()
        return self

    def __exit__(self, *e):
        if self.sems:
            self.nc.clear_and_free_semaphores(self.sems)
            self.nc.all_engine_barrier()
        return self.ctx.__exit__(*e)

    def sb(self, name, shape, dt=F32):
        return self.ctx.enter_context(self.nc.sbuf_tensor(f"{self.tag}_{name}", shape, dt))

    def ps(self, name, shape, dt=F32):
        return self.ctx.enter_context(self.nc.psum_tensor(f"{self.tag}_{name}", shape, dt))

    def sem(self, name):
        self.sems.append(self.nc.alloc_semaphore(name=f"{self.tag}_{name}"))
        return self.sems[-1]

    def block(self):
        return self.nc.Block()


def stack(sp, batches, Q4, K4, qk, qk_hi, qk_lo, stacked, batch_stacked):
    with sp.Fori(*batches) as b:
        sp.wait_ge(qk_hi, 1 + (b + 1) * 2 * (S // CH))
        sp.wait_ge(qk_lo, 1 + (b + 1) * 2 * (S // CH))
        for g in range(4):
            for j in range(4):
                rows, src = slice(32 * j, 32 * j + 32), slice(32 * g, 32 * g + 32)
                sp.dma_start(Q4[rows, g, ds(b * S, S)], qk["q", "hhll"[j]][src, ds(b * S, S)]).then_inc(stacked, 16)
                sp.dma_start(K4[rows, g, ds(b * S + WIN, S)], qk["k", "hlhl"[j]][src, ds(b * S, S)]).then_inc(stacked, 16)
        sp.wait_ge(stacked, STACKS * (b + 1))
        sp.sem_inc(batch_stacked, 1)


STACKED_FIRST = B // 2
STACKS = 32 * 16


def band_project(nc, X, Q4, K4, V, qk, qk_hi, qk_lo, stacked, batch_stacked, io):
    with Stage(nc, "a1") as st:
        sb, ps, sem = st.sb, st.ps, st.sem
        w32, whi, wlo = sb("w32", [P, 5, D]), sb("whi", [P, 5, D], F16), sb("wlo", [P, 5, D], F16)
        bias = sb("bias", [P, 4])
        bvb = sb("bvb", [P, D])
        cos, sin = sb("cos", [P, S]), sb("sin", [P, S])
        ident = sb("ident", [P, P])
        seen = sb("seen", [P, 1])
        halfneg, epsc = sb("halfneg", [P, TPC]), sb("epsc", [P, TPC])
        stats, mv = sb("stats", [P, 2, TPC, 6]), sb("mv", [P, 2, TPC, 2])
        vare, rstd = sb("vare", [P, 2, TPC]), sb("rstd", [P, 2, TPC])
        xh = sb("xh", [P, TPC, D])
        xTh, xTl = sb("xTh", [P, WIN + S], F16), sb("xTl", [P, WIN + S], F16)
        t1, t2, rot = sb("t1", [P, CH]), sb("t2", [P, CH]), sb("rot", [P, 2, CH])
        v32 = sb("v32", [P, 8, D])
        psX = ps("psX", [P, CH])
        psP = [ps(f"psP{i}", [P, CH]) for i in range(4)]
        psV = ps("psV", [P, 8, D])

        const_loaded, x_first, x_loaded = sem("const_loaded"), sem("x_first"), sem("x_loaded")
        weights_scaled, weights_hi, weights_lo = sem("weights_scaled"), sem("weights_hi"), sem("weights_lo")
        zeroed = sem("zeroed")
        bn_done, stats_ready, eps_added, rstd_ready = sem("bn"), sem("stats_ready"), sem("eps_added"), sem("rstd_ready")
        xhat_ready, xhat_transposed = sem("xhat_ready"), sem("xhat_transposed")
        xT_hi, xT_lo = sem("xT_hi"), sem("xT_lo")
        proj_done, v_done = sem("proj_done"), sem("v_done")
        cos_part, rope_parts, rotated = sem("cos_part"), sem("rope_parts"), sem("rotated")
        v_biased, v_hi, v_lo = sem("v_biased"), sem("v_hi"), sem("v_lo")

        xt = io["x"].rearrange("b (t p) d -> p (b t) d", p=P)
        chunks_of_batch = S // CH

        with st.block() as block:

            @block.sync
            def _(sp):
                for a, b, loaded in ((0, 2, x_first), (2, NCH // 2, x_loaded), (NCH // 2, NCH, x_loaded)):
                    sp.dma_start(X[:, a * TPC:b * TPC, :], xt[:, a * TPC:b * TPC, :]).then_inc(loaded, 16)
                stack(sp, (0, STACKED_FIRST), Q4, K4, qk, qk_hi, qk_lo, stacked, batch_stacked)

            @block.gpsimd
            def _(pool):
                pool.sem_inc(v_lo, 1)
                pool.sem_inc(qk_lo, 1)
                nc.gpsimd.memset(halfneg[:], -0.5).then_inc(zeroed, 1)
                nc.gpsimd.memset(epsc[:], EPS).then_inc(zeroed, 1)
                nc.gpsimd.memset(V[:, :, 0], 1.0).then_inc(zeroed, 1)
                nc.gpsimd.memset(V[:, :, 1], 0.0).then_inc(zeroed, 1)
                nc.gpsimd.memset(K4[:, :, 0:WIN], 0.0).then_inc(zeroed, 1)
                nc.gpsimd.memset(xTh[:, 0:WIN], 0.0).then_inc(zeroed, 1)
                nc.gpsimd.memset(xTl[:, 0:WIN], 0.0).then_inc(zeroed, 1)
                pool.wait_ge(zeroed, 7)

                def rstd_of(c, h):
                    pool.wait_ge(stats_ready, c + 1)
                    nc.gpsimd.tensor_tensor(vare[:, h], mv[:, h, :, 1], epsc[:], ALU.add).then_inc(eps_added, 1)
                    pool.wait_ge(eps_added, c + 1)
                    nc.gpsimd.tensor_tensor(rstd[:, h], vare[:, h], halfneg[:], ALU.pow).then_inc(rstd_ready, 1)

                def lows(b, h):
                    c = chunks_of_batch * b + h
                    for n, name in enumerate("qk"):
                        pool.wait_ge(qk_hi, 1 + 2 * c + n + 1)
                        nc.gpsimd.tensor_tensor(qk[name, "l"][:, ds(c * CH, CH)], rot[:, n, :],
                                                qk[name, "h"][:, ds(c * CH, CH)], ALU.subtract).then_inc(qk_lo, 1)
                    pool.wait_ge(v_hi, c + 1)
                    nc.gpsimd.tensor_tensor(
                        V[:, ds(c * 8, 8), 1, :, 0:DA], v32[:].rearrange("p w (h d) -> p w h d", d=DA),
                        V[:, ds(c * 8, 8), 0, :, 0:DA], ALU.subtract).then_inc(v_lo, 1)

                rstd_of(0, 0)
                rstd_of(1, 1)
                with pool.Fori(0, B - 1) as b:
                    for h in range(chunks_of_batch):
                        rstd_of(2 * b + h + 2, h)
                        lows(b, h)
                for h in range(chunks_of_batch):
                    lows(B - 1, h)

            @block.scalar
            def _(act):
                act.sem_inc(qk_hi, 1)
                act.dma_start(w32[:], io["wA"]).then_inc(const_loaded, 16)
                act.dma_start(ident[:], io["ident"]).then_inc(const_loaded, 16)
                act.dma_start(bias[:], io["biasA"]).then_inc(const_loaded, 16)
                act.dma_start(bvb[:], io["bv"].rearrange("(a n) -> a n", a=1).broadcast_to([P, D])).then_inc(const_loaded, 16)
                act.dma_start(cos[:], io["cos"]).then_inc(const_loaded, 16)
                act.dma_start(sin[:], io["sin"]).then_inc(const_loaded, 16)
                act.wait_ge(const_loaded, 96)
                nc.scalar.activation(whi[:], w32[:], ACT.Copy).then_inc(weights_hi, 1)

                def xT_high(b, h):
                    c = chunks_of_batch * b + h
                    act.wait_ge(xhat_transposed, c + 1)
                    act.wait_ge(v_done, 1 + chunks_of_batch * b)
                    nc.scalar.activation(xTh[:, WIN + h * CH:WIN + (h + 1) * CH], psX[:], ACT.Copy).then_inc(xT_hi, 1)

                def chunk(b, h, last=False):
                    c = chunks_of_batch * b + h
                    for n, name in enumerate("qk"):
                        act.wait_ge(rotated, 2 * c + n + 1)
                        nc.scalar.activation(qk[name, "h"][:, ds(c * CH, CH)], rot[:, n, :], ACT.Copy).then_inc(qk_hi, 1)
                        if n == 0 and not last:
                            xT_high(b + h, 1 - h)
                    act.wait_ge(v_biased, 1 + c + 1)
                    nc.scalar.activation(V[:, ds(c * 8, 8), 0, :, 0:DA], v32[:].rearrange("p w (h d) -> p w h d", d=DA),
                                         ACT.Copy).then_inc(v_hi, 1)

                act.wait_ge(zeroed, 7)
                xT_high(0, 0)
                with act.Fori(0, B - 1) as b:
                    for h in range(chunks_of_batch):
                        chunk(b, h)
                chunk(B - 1, 0)
                chunk(B - 1, 1, last=True)

            @block.vector
            def _(dve):
                dve.sem_inc(v_biased, 1)
                dve.sem_inc(rope_parts, 2)
                def stats_of(c, h):
                    for j in range(TPC):
                        nc.vector.bn_stats(stats[:, h, j, :], X[:, TPC * c + j, :]).then_inc(bn_done, 1)
                    for j in range(TPC):
                        if j == 0:
                            dve.wait_ge(bn_done, TPC * c + TPC)
                            nc.vector.tensor_copy(seen[:], stats[:, h, TPC - 1, 0:1])
                        ins = nc.vector.bn_aggr(mv[:, h, j, :], stats[:, h, j, :])
                    ins.then_inc(stats_ready, 1)

                def normalise(c, h):
                    dve.wait_ge(rstd_ready, c + 1)
                    dve.wait_ge(xhat_transposed, c)
                    for j in range(TPC):
                        ins = nc.vector.tensor_scalar(xh[:, j, :], X[:, TPC * c + j, :], mv[:, h, j, 0:1],
                                                      rstd[:, h, j:j + 1], ALU.subtract, ALU.mult)
                    ins.then_inc(xhat_ready, 1)

                def xT_low(c, h):
                    dve.wait_ge(xT_hi, c + 1)
                    cols = slice(WIN + h * CH, WIN + (h + 1) * CH)
                    nc.vector.tensor_tensor(xTl[:, cols], psX[:], xTh[:, cols], ALU.subtract).then_inc(xT_lo, 1)

                def chunk(b, h, more):
                    c = chunks_of_batch * b + h
                    if more:
                        stats_of(c + 2, h)
                    if more or h == 0:
                        normalise(c + 1, 1 - h)
                    for n in range(2):
                        dve.wait_ge(proj_done, 4 * c + 2 * n + 1)
                        nc.vector.scalar_tensor_tensor(t1[:], psP[2 * n][:], bias[:, 2 * n:2 * n + 1],
                                                       cos[:, h * CH:(h + 1) * CH], ALU.add, ALU.mult).then_inc(cos_part, 1)
                        dve.wait_ge(proj_done, 4 * c + 2 * n + 2)
                        nc.vector.scalar_tensor_tensor(t2[:], psP[2 * n + 1][:], bias[:, 2 * n + 1:2 * n + 2],
                                                       sin[:, h * CH:(h + 1) * CH], ALU.add, ALU.mult).then_inc(rope_parts, 1)
                        dve.wait_ge(cos_part, 2 * c + n + 1)
                        dve.wait_ge(rope_parts, 2 + 2 * c + n + 1)
                        dve.wait_ge(qk_lo, 1 + 2 * c)
                        nc.vector.tensor_tensor(rot[:, n, :], t1[:], t2[:], ALU.add).then_inc(rotated, 1)
                        dve.wait_ge(rotated, 2 * c + n + 1)
                        if n == 0 and (more or h == 0):
                            xT_low(c + 1, 1 - h)
                    dve.wait_ge(v_done, 1 + c + 1)
                    dve.wait_ge(v_lo, 1 + c)
                    nc.vector.tensor_tensor(v32[:], psV[:], bvb[:, None, :].broadcast_to([P, 8, D]),
                                            ALU.add).then_inc(v_biased, 1)

                dve.wait_ge(x_first, 16)
                stats_of(0, 0)
                stats_of(1, 1)
                normalise(0, 0)
                dve.wait_ge(weights_hi, 1)
                nc.vector.tensor_tensor(wlo[:], w32[:], whi[:], ALU.subtract).then_inc(weights_lo, 1)
                dve.wait_ge(const_loaded, 96)
                dve.wait_ge(x_loaded, 2 * 16)
                xT_low(0, 0)
                with dve.Fori(0, B - 1) as b:
                    for h in range(chunks_of_batch):
                        chunk(b, h, True)
                for h in range(chunks_of_batch):
                    chunk(B - 1, h, False)

            @block.tensor
            def _(pe):
                pe.sem_inc(v_done, 1)
                def transposes(c):
                    pe.wait_ge(xhat_ready, c + 1)
                    pe.wait_ge(xT_lo, c)
                    for j in range(TPC):
                        ins = nc.tensor.transpose(psX[:, j * P:(j + 1) * P], xh[:, j, :], ident[:])
                    ins.then_inc(xhat_transposed, 1)

                def project(b, h, last=False):
                    c = chunks_of_batch * b + h
                    pe.wait_ge(xT_hi, c + 1)
                    pe.wait_ge(xT_lo, c + 1)
                    for i in range(4):
                        pe.wait_ge(rope_parts, 2 * c + i // 2 + 1)
                        cols = slice(WIN + h * CH, WIN + (h + 1) * CH)
                        nc.tensor.matmul(psP[i][:], whi[:, i, :], xTh[:, cols], start=True, stop=False)
                        nc.tensor.matmul(psP[i][:], whi[:, i, :], xTl[:, cols], start=False, stop=False)
                        nc.tensor.matmul(psP[i][:], wlo[:, i, :], xTh[:, cols], start=False, stop=True).then_inc(proj_done, 1)
                    if not last:
                        transposes(c + 1)
                    pe.wait_ge(v_biased, 1 + c)
                    for w in range(8):
                        cols = slice((8 * h + w) * WIN, (8 * h + w) * WIN + P)
                        nc.tensor.matmul(psV[:, w, :], xTh[:, cols], whi[:, 4, :], start=True, stop=False)
                        nc.tensor.matmul(psV[:, w, :], xTl[:, cols], whi[:, 4, :], start=False, stop=False)
                        ins = nc.tensor.matmul(psV[:, w, :], xTh[:, cols], wlo[:, 4, :], start=False, stop=True)
                    ins.then_inc(v_done, 1)

                pe.wait_ge(const_loaded, 96)
                pe.wait_ge(weights_lo, 1)
                pe.wait_ge(zeroed, 7)
                transposes(0)
                with pe.Fori(0, B - 1) as b:
                    for h in range(chunks_of_batch):
                        project(b, h)
                project(B - 1, 0)
                project(B - 1, 1, last=True)


def band_attend(nc, X, Q4, K4, V, qk, qk_hi, qk_lo, stacked, batch_stacked, io):
    with Stage(nc, "a2") as st:
        sb, ps, sem = st.sb, st.ps, st.sem
        NP_ = HA // 2
        ident, identb = sb("ident", [P, P]), sb("identb", [P, P], BF16)
        bandm32, bandm = sb("bandm32", [P, 2, P]), sb("bandm", [P, 2, P], BF16)
        masks = sb("masks", [P, NT, P], BF16)
        headm = sb("headm", [P, 4], F16)
        parm = sb("parm", [P, 2])
        fold = sb("fold", [P, 2, P])
        wo32, woh, wol = sb("wo32", [P, D]), sb("woh", [P, D], F16), sb("wol", [P, D], F16)
        bob = sb("bob", [P, D])
        Qx = sb("Qx", [P, 2, HA, WIN], F16)
        mx, nb = sb("mx", [P, 2, NP_]), sb("nb", [P, 2, NP_])
        E = sb("E", [P, 2, NP_, P])
        Th, Tl = sb("Th", [P, 2, NP_, P], F16), sb("Tl", [P, 2, NP_, P], F16)
        Vn = sb("Vn", [P, 2, 2, HA * VW], F16)
        rd, rm = sb("rd", [P, NP_, 2]), sb("rm", [P, NP_, 2])
        On = sb("On", [P, 2, NP_ * 2, DA])
        oTh, oTl = sb("oTh", [P, P], F16), sb("oTl", [P, P], F16)
        psS = [[ps(f"psS{j}{a}", [P, 4, P]) for a in range(2)] for j in range(2)]
        psT = [ps(f"psT{a}", [P, 4, P]) for a in range(2)]
        psO = ps("psO", [P, 512])
        psY = ps("psY", [P, 512])
        pv = psO[:, 0:NP_ * 2 * VW].rearrange("p (m r w) -> p m r w", r=2, w=VW)

        loaded, wo_hi, wo_lo, masks_ready = sem("loaded"), sem("wo_hi"), sem("wo_lo"), sem("masks_ready")
        band_cast, q_masked = sem("band_cast"), sem("q_masked")
        scores_done = sem("scores_done")
        max_done, bias_done, exps_done = sem("max_done"), sem("bias_done"), sem("exps_done")
        exp_transposed, T_hi, T_lo = sem("exp_transposed"), sem("T_hi"), sem("T_lo")
        v_copied, values_done = sem("v_copied"), sem("values_done")
        recip_done, recip_masked, normed = sem("recip_done"), sem("recip_masked"), sem("normed")
        folded, oT_hi, oT_lo, projected, bias_added, added = (
            sem("folded"), sem("oT_hi"), sem("oT_lo"), sem("projected"), sem("bias_added"), sem("added"))

        with st.block() as block:

            @block.sync
            def _(sp):
                sp.dma_start(ident[:], io["ident"]).then_inc(loaded, 16)
                sp.dma_start(bandm32[:], io["bandm"]).then_inc(loaded, 16)
                sp.dma_start(headm[:], io["headm"]).then_inc(loaded, 16)
                sp.dma_start(parm[:], io["parm"]).then_inc(loaded, 16)
                sp.dma_start(fold[:], io["fold"]).then_inc(loaded, 16)
                sp.dma_start(wo32[:], io["woT"]).then_inc(loaded, 16)
                sp.dma_start(bob[:], io["bo"].rearrange("(a n) -> a n", a=1).broadcast_to([P, D])).then_inc(loaded, 16)

                stack(sp, (STACKED_FIRST, B), Q4, K4, qk, qk_hi, qk_lo, stacked, batch_stacked)

            LOADED = 7 * 16

            @block.gpsimd
            def _(pool):
                def mask_q(n, j, first=False):
                    pool.wait_ge(batch_stacked, n // (S // WIN) + 1)
                    if not first:
                        pool.wait_ge(scores_done, 2 * n - 2)
                    nc.gpsimd.tensor_tensor(
                        Qx[:, j].rearrange("p (g h) q -> p g h q", h=4),
                        Q4[:, :, None, ds(WIN * n, WIN)].broadcast_to([P, 4, 4, WIN]),
                        headm[:, None, :, None].broadcast_to([P, 4, 4, WIN]), ALU.mult).then_inc(q_masked, 1)

                pool.wait_ge(loaded, LOADED)
                mask_q(0, 0, True)
                mask_q(1, 1, True)
                with pool.Fori(1, NT) as t:
                    for j in range(2):
                        mask_q(2 * t + j, j)

            @block.scalar
            def _(act):
                def exps(n, j, a):
                    act.wait_ge(bias_done, 2 * n + a + 1)
                    for p in range(4):
                        ins = nc.scalar.activation(E[:, j, 4 * a + p, :], psS[j][a][:, p, :], ACT.Exp,
                                                   bias=nb[:, j, 4 * a + p:4 * a + p + 1], scale=SCALE_A)
                    ins.then_inc(exps_done, 1)

                def T_high(n, j, a):
                    act.wait_ge(exp_transposed, 2 * n + a + 1)
                    nc.scalar.activation(Th[:, j, 4 * a:4 * a + 4, :], psT[a][:], ACT.Copy).then_inc(T_hi, 1)

                def o_high(t):
                    act.wait_ge(folded, t + 1)
                    nc.scalar.activation(oTh[:], psY[:, 0:P], ACT.Copy).then_inc(oT_hi, 1)

                def tile(t, first=False, second=False, last=False):
                    for j in range(2):
                        n = 2 * t + j
                        if not first:
                            act.wait_ge(values_done, n - 1)
                        for a in range(2):
                            T_high(n, j, a)
                            if a == 0 and j == 0 and not (first or second):
                                o_high(t - 2)
                            if not (last and j == 1):
                                exps(n + 1, 1 - j, a)

                act.wait_ge(loaded, LOADED)
                nc.scalar.activation(woh[:], wo32[:], ACT.Copy).then_inc(wo_hi, 1)
                nc.scalar.activation(bandm[:], bandm32[:], ACT.Copy).then_inc(band_cast, 1)
                nc.scalar.activation(identb[:], ident[:], ACT.Copy).then_inc(band_cast, 1)
                for a in range(2):
                    exps(0, 0, a)
                tile(0, first=True)
                tile(1, second=True)
                with act.Fori(2, NT - 1) as t:
                    tile(t)
                tile(NT - 1, last=True)
                o_high(NT - 2)
                o_high(NT - 1)

            @block.vector
            def _(dve):
                dve.sem_inc(added, 1)
                def maximum(n, j, a):
                    dve.wait_ge(scores_done, 2 * n + a + 1)
                    nc.vector.tensor_reduce(mx[:, j, 4 * a:4 * a + 4], psS[j][a][:], AX_X, ALU.max).then_inc(max_done, 1)

                def exp_bias(n, j, a):
                    dve.wait_ge(max_done, 2 * n + a + 1)
                    nc.vector.tensor_scalar(nb[:, j, 4 * a:4 * a + 4], mx[:, j, 4 * a:4 * a + 4], -SCALE_A, None,
                                            ALU.mult).then_inc(bias_done, 1)

                def recip(n):
                    dve.wait_ge(values_done, n + 1)
                    nc.vector.reciprocal(rd[:], pv[:, :, :, DA]).then_inc(recip_done, 1)

                def mask_recip(n):
                    dve.wait_ge(recip_done, n + 1)
                    nc.vector.tensor_tensor(rm[:], rd[:], parm[:, None, :].broadcast_to([P, NP_, 2]),
                                            ALU.mult).then_inc(recip_masked, 1)

                def norm(n, j):
                    dve.wait_ge(recip_masked, n + 1)
                    nc.vector.tensor_tensor(
                        On[:, j].rearrange("p (m r) d -> p m r d", r=2), pv[:, :, :, 0:DA],
                        rm[:, :, :, None].broadcast_to([P, NP_, 2, DA]), ALU.mult).then_inc(normed, 1)

                def shift_and_norm(n, j, shift=True, first=False, normalise=True, after_fold=None):
                    if shift and not first:
                        dve.wait_ge(exps_done, 2 * n - 2)
                        dve.wait_ge(bias_done, 2 * n - 2)
                    if shift:
                        maximum(n, j, 0)
                    if normalise:
                        recip(n - 3)
                    if shift:
                        exp_bias(n, j, 0)
                    if normalise:
                        mask_recip(n - 3)
                    if shift:
                        maximum(n, j, 1)
                    if normalise:
                        if after_fold is not None:
                            dve.wait_ge(folded, after_fold)
                        norm(n - 3, 1 - j)
                    if shift:
                        exp_bias(n, j, 1)

                def add(t):
                    dve.wait_ge(projected, t + 1)
                    nc.vector.tensor_tensor(X[:, ds(t, 1), :], psY[:, None, P:2 * P], X[:, ds(t, 1), :], ALU.add).then_inc(added, 1)

                def split_o(t):
                    dve.wait_ge(oT_hi, t + 1)
                    nc.vector.tensor_tensor(oTl[:], psY[:, 0:P], oTh[:], ALU.subtract).then_inc(oT_lo, 1)

                def copy_v(n, j, first=False):
                    if not first:
                        dve.wait_ge(values_done, n - 1)
                    nc.vector.tensor_copy(Vn[:, j, None], V[:, ds(n, 1)].rearrange("p n c h w -> p n c (h w)")).then_inc(v_copied, 1)

                def T_low(n, j, a):
                    dve.wait_ge(T_hi, 2 * n + a + 1)
                    nc.vector.tensor_tensor(Tl[:, j, 4 * a:4 * a + 4, :], psT[a][:], Th[:, j, 4 * a:4 * a + 4, :],
                                            ALU.subtract).then_inc(T_lo, 1)

                def tile(t, first=False, second=False, last=False):
                    for j in range(2):
                        n = 2 * t + j
                        shift_and_norm(n + 1, 1 - j, shift=not (last and j == 1), first=first and j == 0,
                                       normalise=not first, after_fold=None if first or second or j == 1 else t - 1)
                        if j == 1 and not (first or second):
                            add(t - 2)
                        copy_v(n, j, first)
                        T_low(n, j, 0)
                        if j == 0 and not (first or second):
                            split_o(t - 2)
                        T_low(n, j, 1)

                dve.wait_ge(loaded, LOADED)
                dve.wait_ge(wo_hi, 1)
                nc.vector.tensor_tensor(wol[:], wo32[:], woh[:], ALU.subtract).then_inc(wo_lo, 1)
                dve.wait_ge(band_cast, 1)
                nc.vector.tensor_copy(masks[:], bandm[:, 1:2, :].broadcast_to([P, NT, P])).then_inc(masks_ready, 1)
                dve.wait_ge(masks_ready, 1)
                nc.vector.tensor_copy(masks[:].rearrange("p (b i) k -> p b i k", b=B)[:, :, 0, :],
                                      bandm[:, 0:1, :].broadcast_to([P, B, P])).then_inc(masks_ready, 1)
                nc.vector.tensor_tensor(X[:], X[:], bob[:, None, :].broadcast_to([P, NT, D]), ALU.add).then_inc(bias_added, 1)
                dve.wait_ge(bias_added, 1)
                shift_and_norm(0, 0, first=True, normalise=False)
                tile(0, first=True)
                tile(1, second=True)
                with dve.Fori(2, NT - 1) as t:
                    tile(t)
                tile(NT - 1, last=True)
                shift_and_norm(NB + 1, 1, shift=False, after_fold=NT - 1)
                shift_and_norm(NB + 2, 0, shift=False)
                split_o(NT - 2)
                add(NT - 2)
                split_o(NT - 1)
                add(NT - 1)

            @block.tensor
            def _(pe):
                def scores(n, j, first=False):
                    pe.wait_ge(q_masked, n + 1)
                    if not first:
                        pe.wait_ge(exps_done, 2 * n - 2)
                    for a in range(2):
                        m = masks[:, ds(n // 2, 1), :] if j == 0 else bandm[:, 1:2, :]
                        nc.tensor.matmul(psS[j][a][:], identb[:], m.broadcast_to([P, 4, P]), start=True, stop=False)
                        for p in range(4):
                            q = Qx[:, j, 8 * a + 2 * p:8 * a + 2 * p + 2, :]
                            ins = nc.tensor.matmul(psS[j][a][:, p, :], q, K4[:, 2 * a + p // 2, ds(WIN * n, P)],
                                                   start=False, stop=(p == 3))
                        ins.then_inc(scores_done, 1)

                def transposes(n, j, first=False):
                    for a in range(2):
                        pe.wait_ge(exps_done, 2 * n + a + 1)
                        if not first:
                            pe.wait_ge(T_lo, 2 * n - 1 + a)
                        for p in range(4):
                            ins = nc.tensor.transpose(psT[a][:, p, :], E[:, j, 4 * a + p, :], ident[:])
                        ins.then_inc(exp_transposed, 1)

                def values(n, j, first=False):
                    if not first:
                        pe.wait_ge(normed, n)
                    pe.wait_ge(v_copied, n + 1)
                    for a in range(2):
                        pe.wait_ge(T_lo, 2 * n + a + 1)
                        for p in range(4 * a, 4 * a + 4):
                            o = pv[:, p, :, :]
                            vh, vl = (Vn[:, j, part, 2 * p * VW:(2 * p + 2) * VW] for part in range(2))
                            nc.tensor.matmul(o, Th[:, j, p, :], vh, start=True, stop=False)
                            nc.tensor.matmul(o, Th[:, j, p, :], vl, start=False, stop=False)
                            ins = nc.tensor.matmul(o, Tl[:, j, p, :], vh, start=False, stop=True)
                    ins.then_inc(values_done, 1)

                def fold_o(t):
                    pe.wait_ge(normed, 2 * t + 2)
                    pe.wait_ge(added, 1 + t)
                    for j in range(2):
                        ins = nc.tensor.matmul(psY[:, 0:P], On[:, j], fold[:, j, :], start=(j == 0), stop=(j == 1))
                    ins.then_inc(folded, 1)

                def project(t):
                    pe.wait_ge(oT_lo, t + 1)
                    nc.tensor.matmul(psY[:, P:2 * P], oTh[:], woh[:], start=True, stop=False)
                    nc.tensor.matmul(psY[:, P:2 * P], oTh[:], wol[:], start=False, stop=False)
                    nc.tensor.matmul(psY[:, P:2 * P], oTl[:], woh[:], start=False, stop=True).then_inc(projected, 1)

                def tile(t, first=False, second=False, last=False):
                    for j in range(2):
                        n = 2 * t + j
                        if not (last and j == 1):
                            scores(n + 1, 1 - j, first and j == 0)
                        if j == 1 and not (first or second):
                            project(t - 2)
                        transposes(n, j, first and j == 0)
                        if not (first and j == 0):
                            values(n - 1, 1 - j, first)
                        if j == 1 and not first:
                            fold_o(t - 1)

                pe.wait_ge(loaded, LOADED)
                pe.wait_ge(wo_lo, 1)
                pe.wait_ge(masks_ready, 2)
                pe.wait_ge(band_cast, 2)
                scores(0, 0, True)
                tile(0, first=True)
                tile(1, second=True)
                with pe.Fori(2, NT - 1) as t:
                    tile(t)
                tile(NT - 1, last=True)
                values(NB - 1, 1)
                project(NT - 2)
                fold_o(NT - 1)
                project(NT - 1)


def experts(nc, X, io, tag):
    with Stage(nc, tag) as outer:
        sb = outer.sb
        xnh, xnl = sb("xnh", [P, T], F16), sb("xnl", [P, T], F16)
        w1h, w1l = sb("w1h", [P, NE, FF], F16), sb("w1l", [P, NE, FF], F16)
        w2h, w2l = sb("w2h", [P, NE, FC, D], F16), sb("w2l", [P, NE, FC, D], F16)
        b1 = sb("b1", [P, NE, FC])
        K3, G3 = sb("K3", [3 * NE, D], F16), sb("G3", [P, NT, 3, NE], F16)
        Gs = sb("Gs", [P, NT, NE])
        identh = sb("identh", [P, P], F16)
        route(nc, X, xnh, xnl, w1h, w1l, w2h, w2l, b1, K3, G3, Gs, identh, io, tag + "r")
        mixture(nc, X, xnh, xnl, w1h, w1l, w2h, w2l, b1, K3, G3, Gs, identh, tag + "m")


def route(nc, X, xnh, xnl, w1h, w1l, w2h, w2l, b1, K3, G3, Gs, identh, io, tag):
    with Stage(nc, tag) as st:
        sb, ps, sem = st.sb, st.ps, st.sem
        w132, w232 = sb("w132", [P, NE * FF]), sb("w232", [P, NE * FF])
        ident = sb("ident", [P, P])
        K, K3c = sb("K", [P, NE]), sb("K3c", [P, 3, NE], F16)
        wr32, wrh, wrl = sb("wr32", [P, NE]), sb("wrh", [P, NE], F16), sb("wrl", [P, NE], F16)
        gamma, beta = sb("gamma", [P, 1]), sb("beta", [P, 1])
        brb = sb("brb", [P, NE])
        b2 = sb("b2", [P, NE])
        a32, ah, al = sb("a32", [P, NE, FC]), sb("ah", [P, NE, FC], F16), sb("al", [P, NE, FC], F16)
        ctot, csum = sb("ctot", [P, 1]), sb("csum", [P, NE])
        seen = sb("seen", [P, 1])
        halfneg, epsc = sb("halfneg", [P, TPC]), sb("epsc", [P, TPC])
        stats, mv = sb("stats", [P, 2, TPC, 6]), sb("mv", [P, 2, TPC, 2])
        vare, r1, vr, r2 = (sb(n, [P, 2, TPC]) for n in ("vare", "r1", "vr", "r2"))
        u = sb("u", [P, 2, TPC, D])
        xh = sb("xh", [P, 2, TPC, D])
        xn = sb("xn", [P, 2, CH])
        rank = sb("rank", [P, NE])
        L, eq, oh1, oh2, pr = (sb(n, [P, NT, NE]) for n in ("L", "eq", "oh1", "oh2", "pr"))
        m = sb("m", [P, 6, NT])
        psX = [ps(f"psX{h}", [P, CH]) for h in range(2)]
        psL = ps("psL", [P, 512])
        psK = ps("psK", [P, 512])
        lg = psL[:, 0:NT * NE].rearrange("p (t e) -> p t e", e=NE)

        loaded, w1_loaded, w2_loaded, set_up = sem("loaded"), sem("w1_loaded"), sem("w2_loaded"), sem("set_up")
        w_hi, w_lo = sem("w_hi"), sem("w_lo")
        bn_done, stats_ready, r1_ready, r2_step, r2_ready = (
            sem(n) for n in ("bn_done", "stats_ready", "r1_ready", "r2_step", "r2_ready"))
        u_ready, u_added, xhat_ready, transposed = sem("u_ready"), sem("u_added"), sem("xhat_ready"), sem("transposed")
        xn_hi, xn_ready, xn_lo, logits_done = sem("xn_hi"), sem("xn_ready"), sem("xn_lo"), sem("logits_done")
        wr_hi, wr_lo = sem("wr_hi"), sem("wr_lo")
        b1_relu, b1_hi, b1_lo, k_done, k_step = sem("b1_relu"), sem("b1_hi"), sem("b1_lo"), sem("k_done"), sem("k_step")
        rt, exp_ready, gates_scaled = sem("router_step"), sem("exp_ready"), sem("gates_scaled")
        k_halves, k_turned, k_stored = sem("k_halves"), sem("k_turned"), sem("k_stored")

        with st.block() as block:

            @block.sync
            def _(sp):
                for dst, src in ((identh[:], io["identh"]), (ident[:], io["ident"]), (gamma[:], io["gammaF"]),
                                 (beta[:], io["betaF"]), (wr32[:], io["wrF"]), (b1[:], io["b1F"]), (b2[:], io["b2F"]),
                                 (rank[:], io["rank"]),
                                 (brb[:], io["brF"].rearrange("(a n) -> a n", a=1).broadcast_to([P, NE]))):
                    sp.dma_start(dst, src).then_inc(loaded, 16)
                sp.dma_start(w132[:], io["w1F"].rearrange("p e f -> p (e f)")).then_inc(w1_loaded, 16)
                sp.dma_start(w232[:], io["w2F"].rearrange("p e f d -> p (e f d)")).then_inc(w2_loaded, 16)

            LOADED = 9 * 16

            @block.gpsimd
            def _(pool):
                pool.sem_inc(u_added, 1)
                nc.gpsimd.memset(halfneg[:], -0.5).then_inc(set_up, 1)
                nc.gpsimd.memset(epsc[:], EPS).then_inc(set_up, 1)
                pool.wait_ge(set_up, 2)

                def scales(c, h):
                    G = nc.gpsimd
                    pool.wait_ge(stats_ready, c + 1)
                    G.tensor_tensor(vare[:, h], mv[:, h, :, 1], epsc[:], ALU.add).then_inc(r2_step, 1)
                    pool.wait_ge(r2_step, 4 * c + 1)
                    G.tensor_tensor(r1[:, h], vare[:, h], halfneg[:], ALU.pow).then_inc(r1_ready, 1)
                    pool.wait_ge(r1_ready, c + 1)
                    G.tensor_tensor(vr[:, h], mv[:, h, :, 1], r1[:, h], ALU.mult).then_inc(r2_step, 1)
                    pool.wait_ge(r2_step, 4 * c + 2)
                    G.tensor_tensor(vr[:, h], vr[:, h], r1[:, h], ALU.mult).then_inc(r2_step, 1)
                    pool.wait_ge(r2_step, 4 * c + 3)
                    G.tensor_tensor(vr[:, h], vr[:, h], epsc[:], ALU.add).then_inc(r2_step, 1)
                    pool.wait_ge(r2_step, 4 * c + 4)
                    G.tensor_tensor(r2[:, h], vr[:, h], halfneg[:], ALU.pow).then_inc(r2_ready, 1)

                def add_u(c, h):
                    pool.wait_ge(u_ready, c + 1)
                    nc.gpsimd.tensor_tensor(X[:, ds(TPC * c, TPC), :], X[:, ds(TPC * c, TPC), :], u[:, h], ALU.add).then_inc(u_added, 1)

                scales(0, 0)
                scales(1, 1)
                with pool.Fori(0, NCH // 2 - 1) as b:
                    for h in range(2):
                        c = 2 * b + h
                        pool.wait_ge(xhat_ready, 1 + c + 1)
                        scales(c + 2, h)
                        add_u(c, h)
                add_u(NCH - 2, 0)
                add_u(NCH - 1, 1)

            @block.scalar
            def _(act):
                act.sem_inc(xhat_ready, 1)
                act.wait_ge(loaded, LOADED)
                nc.scalar.activation(wrh[:], wr32[:], ACT.Copy).then_inc(wr_hi, 1)
                nc.scalar.activation(a32[:], b1[:], ACT.Relu).then_inc(b1_relu, 1)
                act.wait_ge(b1_relu, 1)
                nc.scalar.activation(ah[:], a32[:], ACT.Copy).then_inc(b1_hi, 1)
                def normalise_u(c, h):
                    act.wait_ge(u_ready, c + 1)
                    act.wait_ge(r2_ready, c + 1)
                    for j in range(TPC):
                        ins = nc.scalar.activation(xh[:, h, j, :], u[:, h, j, :], ACT.Copy, scale=r2[:, h, j:j + 1])
                    ins.then_inc(xhat_ready, 1)

                def gain(c, h, first=False):
                    act.wait_ge(transposed, 1 + c + 1)
                    if not first:
                        act.wait_ge(xn_lo, 1 + c - 1)
                    nc.scalar.activation(xnh[:, ds(c * CH, CH)], psX[h][:], ACT.Identity,
                                         bias=beta[:], scale=gamma[:]).then_inc(xn_hi, 1)
                    nc.scalar.activation(xn[:, h], psX[h][:], ACT.Identity, bias=beta[:], scale=gamma[:]).then_inc(xn_ready, 1)

                def chunk(c, h):
                    gain(c - 1, 1 - h)
                    act.wait_ge(transposed, c)
                    normalise_u(c, h)

                normalise_u(0, 0)
                normalise_u(1, 1)
                gain(0, 0, first=True)
                act.wait_ge(w1_loaded, 16)
                nc.scalar.activation(w1h[:].rearrange("p e f -> p (e f)"), w132[:], ACT.Copy, scale=WS).then_inc(w_hi, 1)
                for h in range(2):
                    chunk(2 + h, h)
                act.wait_ge(w2_loaded, 16)
                nc.scalar.activation(w2h[:].rearrange("p e f d -> p (e f d)"), w232[:], ACT.Copy, scale=WS).then_inc(w_hi, 1)
                with act.Fori(2, NCH // 2) as b:
                    for h in range(2):
                        chunk(2 * b + h, h)
                gain(NCH - 1, 1)
                act.wait_ge(rt, 3)
                nc.scalar.activation(pr[:], L[:], ACT.Exp).then_inc(exp_ready, 1)

            @block.vector
            def _(dve):
                dve.sem_inc(xn_lo, 1)

                def stats_of(c, h, first=False):
                    for j in range(TPC):
                        nc.vector.bn_stats(stats[:, h, j, :], X[:, TPC * c + j, :]).then_inc(bn_done, 1)
                    for j in range(TPC):
                        if j == 0:
                            if not first:
                                dve.wait_ge(r2_ready, c - 1)
                            dve.wait_ge(bn_done, TPC * c + TPC)
                            nc.vector.tensor_copy(seen[:], stats[:, h, TPC - 1, 0:1])
                        ins = nc.vector.bn_aggr(mv[:, h, j, :], stats[:, h, j, :])
                    ins.then_inc(stats_ready, 1)

                def norm_x(c, h):
                    dve.wait_ge(r1_ready, c + 1)
                    for j in range(TPC):
                        ins = nc.vector.tensor_scalar(u[:, h, j, :], X[:, TPC * c + j, :], mv[:, h, j, 0:1],
                                                      r1[:, h, j:j + 1], ALU.subtract, ALU.mult)
                    ins.then_inc(u_ready, 1)

                def low(c, h):
                    dve.wait_ge(xn_ready, c + 1)
                    dve.wait_ge(xn_hi, c + 1)
                    nc.vector.tensor_tensor(xnl[:, ds(c * CH, CH)], xn[:, h], xnh[:, ds(c * CH, CH)], ALU.subtract).then_inc(xn_lo, 1)

                stats_of(0, 0, first=True)
                stats_of(1, 1, first=True)
                norm_x(0, 0)
                norm_x(1, 1)
                dve.wait_ge(loaded, LOADED)
                dve.wait_ge(wr_hi, 1)
                nc.vector.tensor_tensor(wrl[:], wr32[:], wrh[:], ALU.subtract).then_inc(wr_lo, 1)
                dve.wait_ge(b1_hi, 1)
                nc.vector.tensor_tensor(al[:], a32[:], ah[:], ALU.subtract).then_inc(b1_lo, 1)
                stats_of(2, 0)
                stats_of(3, 1)
                low(0, 0)
                dve.wait_ge(w_hi, 1)
                nc.vector.scalar_tensor_tensor(w1l[:].rearrange("p e f -> p (e f)"), w132[:], WS, w1h[:].rearrange("p e f -> p (e f)"),
                                               ALU.mult, ALU.subtract).then_inc(w_lo, 1)
                with dve.Fori(1, NCH // 2 - 1) as b:
                    for h in range(2):
                        c = 2 * b + h
                        dve.wait_ge(u_added, 1 + c - 1)
                        norm_x(c, h)
                        low(c - 1, 1 - h)
                        stats_of(c + 2, h)
                dve.wait_ge(w_hi, 2)
                nc.vector.scalar_tensor_tensor(w2l[:].rearrange("p e f d -> p (e f d)"), w232[:], WS,
                                               w2h[:].rearrange("p e f d -> p (e f d)"), ALU.mult, ALU.subtract).then_inc(w_lo, 1)
                for h in range(2):
                    c = NCH - 2 + h
                    dve.wait_ge(u_added, 1 + c - 1)
                    norm_x(c, h)
                    low(c - 1, 1 - h)
                low(NCH - 1, 1)

                step = [0]

                def then(ins):
                    step[0] += 1
                    ins.then_inc(rt, 1)
                    dve.wait_ge(rt, step[0])

                bc = lambda a: a[:, :, None].broadcast_to([P, NT, NE])
                rk = rank[:, None, :].broadcast_to([P, NT, NE])
                V = nc.vector
                dve.wait_ge(logits_done, NCH)
                then(V.tensor_tensor(L[:], lg, brb[:, None, :].broadcast_to([P, NT, NE]), ALU.add))
                then(V.tensor_reduce(m[:, 0], L[:], AX_X, ALU.max))
                then(V.tensor_tensor(L[:], L[:], bc(m[:, 0]), ALU.subtract))
                then(V.tensor_scalar(eq[:], L[:], 0.0, None, ALU.is_equal))
                then(V.tensor_tensor(eq[:], eq[:], rk, ALU.mult))
                then(V.tensor_reduce(m[:, 1], eq[:], AX_X, ALU.max))
                then(V.tensor_tensor(oh1[:], rk, bc(m[:, 1]), ALU.is_equal))
                then(V.scalar_tensor_tensor(oh2[:], oh1[:], -1e30, L[:], ALU.mult, ALU.add))
                then(V.tensor_reduce(m[:, 2], oh2[:], AX_X, ALU.max))
                then(V.tensor_tensor(eq[:], oh2[:], bc(m[:, 2]), ALU.is_equal))
                then(V.tensor_tensor(eq[:], eq[:], rk, ALU.mult))
                then(V.tensor_reduce(m[:, 3], eq[:], AX_X, ALU.max))
                then(V.tensor_tensor(oh2[:], rk, bc(m[:, 3]), ALU.is_equal))
                then(V.tensor_tensor(oh1[:], oh1[:], oh2[:], ALU.add))
                dve.wait_ge(exp_ready, 1)
                then(V.tensor_reduce(m[:, 4], pr[:], AX_X, ALU.add))
                then(V.reciprocal(m[:, 5], m[:, 4]))
                then(V.tensor_tensor(pr[:], pr[:], bc(m[:, 5]), ALU.mult))
                then(V.tensor_tensor(pr[:], pr[:], oh1[:], ALU.mult))
                V.tensor_scalar(Gs[:], pr[:], 1.0 / WS, None, ALU.mult).then_inc(gates_scaled, 1)
                V.tensor_copy(G3[:, :, 2], pr[:]).then_inc(gates_scaled, 1)
                then(V.tensor_copy(G3[:, :, 0], pr[:]))
                then(V.tensor_tensor(G3[:, :, 1], pr[:], G3[:, :, 0], ALU.subtract))
                dve.wait_ge(gates_scaled, 2)
                dve.wait_ge(k_done, 1)
                V.scalar_tensor_tensor(csum[:], b2[:], WS, psK[:, 0:NE], ALU.mult, ALU.add).then_inc(k_step, 1)
                dve.wait_ge(k_step, 1)
                V.tensor_reduce(ctot[:], csum[:], AX_X, ALU.add).then_inc(k_step, 1)
                dve.wait_ge(k_step, 2)
                V.tensor_scalar(K[:], psK[:, 0:NE], -1.0, ctot[:], ALU.mult, ALU.add).then_inc(k_step, 1)
                dve.wait_ge(k_step, 3)
                for i in (0, 1):
                    V.tensor_copy(K3c[:, i], K[:]).then_inc(k_step, 1)
                dve.wait_ge(k_step, 5)
                V.tensor_tensor(K3c[:, 2], K[:], K3c[:, 0], ALU.subtract).then_inc(k_halves, 1)
                dve.wait_ge(k_turned, 1)
                V.tensor_copy(K3[:], psK[0:3 * NE, 0:P]).then_inc(k_stored, 1)
                dve.wait_ge(k_stored, 1)

            @block.tensor
            def _(pe):
                def transposes(c, h):
                    pe.wait_ge(xhat_ready, 1 + c + 1)
                    for j in range(TPC):
                        ins = nc.tensor.transpose(psX[h][:, j * P:(j + 1) * P], xh[:, h, j, :], ident[:])
                    ins.then_inc(transposed, 1)

                def logits(c):
                    pe.wait_ge(xn_lo, 1 + c + 1)
                    for j in range(TPC):
                        t = TPC * c + j
                        o = psL[:, ds(t * NE, NE)]
                        nc.tensor.matmul(o, xnh[:, ds(t * P, P)], wrh[:], start=True, stop=False)
                        nc.tensor.matmul(o, xnh[:, ds(t * P, P)], wrl[:], start=False, stop=False)
                        ins = nc.tensor.matmul(o, xnl[:, ds(t * P, P)], wrh[:], start=False, stop=True)
                    ins.then_inc(logits_done, 1)

                pe.sem_inc(transposed, 1)
                pe.wait_ge(loaded, LOADED)
                pe.wait_ge(wr_lo, 1)
                transposes(0, 0)
                with pe.Fori(0, NCH // 2 - 1) as b:
                    for h in range(2):
                        pe.wait_ge(xn_lo, 1 + 2 * b + h)
                        transposes(2 * b + h + 1, 1 - h)
                        logits(2 * b + h)
                pe.wait_ge(xn_lo, 1 + NCH - 2)
                transposes(NCH - 1, 1)
                logits(NCH - 2)
                logits(NCH - 1)
                pe.wait_ge(w_lo, 2)
                pe.wait_ge(b1_lo, 1)
                for e in range(NE):
                    for f in range(FC):
                        w, wl = w2h[:, e, f, :], w2l[:, e, f, :]
                        nc.tensor.matmul(psK[:, e:e + 1], w, ah[:, e, f:f + 1], start=(f == 0), stop=False)
                        nc.tensor.matmul(psK[:, e:e + 1], w, al[:, e, f:f + 1], start=False, stop=False)
                        ins = nc.tensor.matmul(psK[:, e:e + 1], wl, ah[:, e, f:f + 1], start=False, stop=(f == FC - 1))
                ins.then_inc(k_done, 1)
                pe.wait_ge(k_halves, 1)
                nc.tensor.matmul(psK[0:3 * NE, 0:P], K3c[:].rearrange("p a e -> p (a e)"), identh[:], start=True, stop=True).then_inc(k_turned, 1)


def mixture(nc, X, xnh, xnl, w1h, w1l, w2h, w2l, b1, K3, G3, Gs, identh, tag):
    with Stage(nc, tag) as st:
        sb, ps, sem = st.sb, st.ps, st.sem
        R = sb("R", [P, 2, FC, CH])
        Hh, Hl = sb("Hh", [P, 2, FC, CH], F16), sb("Hl", [P, 2, FC, CH], F16)
        GT = sb("GT", [3 * NE, CH], F16)
        ACT_HI = 2
        psZ = [ps(f"psZ{f}", [P, CH]) for f in range(FC)]
        psY = [ps(f"psY{j}", [P, TPC, D]) for j in range(2)]
        psG, psK = ps("psG", [P, CH]), ps("psK", [P, TPC, D])

        up_done, H_hi = sem("up_done"), sem("H_hi")
        relu_done = sem("relu_done")
        H_lo = sem("H_lo")
        down_done = sem("down_done")
        y_added = sem("y_added")
        gates_turned = sem("gates_turned")
        gates_stored = sem("gates_stored")
        k_done = sem("k_done")
        k_added = sem("k_added")

        with st.block() as block:

            @block.tensor
            def _(pe):
                pe.sem_inc(down_done, 2)
                pe.sem_inc(k_done, 1)

                def up(u, c, e):
                    for f in range(FC):
                        pe.wait_ge(relu_done, FC * u + f + 1)
                        x, xl = xnh[:, ds(c * CH, CH)], xnl[:, ds(c * CH, CH)]
                        w, wl = w1h[:, ds(e, 1), f * P:(f + 1) * P], w1l[:, ds(e, 1), f * P:(f + 1) * P]
                        nc.tensor.matmul(psZ[f][:], w, x, start=True, stop=False)
                        nc.tensor.matmul(psZ[f][:], w, xl, start=False, stop=False)
                        nc.tensor.matmul(psZ[f][:], wl, x, start=False, stop=True).then_inc(up_done, 1)

                def down(u, e, j):
                    pe.wait_ge(y_added, u + 1)
                    pe.wait_ge(H_lo, 2 * FC + FC * u + FC)
                    w = [(w2h[:, ds(e, 1), f, :], w2l[:, ds(e, 1), f, :]) for f in range(FC)]
                    for t in range(TPC):
                        tokens = slice(t * P, (t + 1) * P)
                        for f in range(FC):
                            h, hl = Hh[:, j, f, tokens], Hl[:, j, f, tokens]
                            nc.tensor.matmul(psY[j][:, t, :], h, w[f][0], start=(f == 0), stop=False)
                            nc.tensor.matmul(psY[j][:, t, :], h, w[f][1], start=False, stop=False)
                            ins = nc.tensor.matmul(psY[j][:, t, :], hl, w[f][0], start=False, stop=(f == FC - 1))
                    ins.then_inc(down_done, 1)

                def pair(c, ep, first=False):
                    for j in range(2):
                        if first and j == 1:
                            gated_k(c)
                        u = NE * c + 2 * ep + j
                        q = (NE // 2) * c + ep + j
                        up(u + 1, (q // (NE // 2)) % NCH, 2 * (q % (NE // 2)) + (1 - j))
                        down(u, 2 * ep + j, j)

                def turn_gates(c):
                    pe.wait_ge(gates_stored, c + 1)
                    for j in range(TPC):
                        ins = nc.tensor.matmul(psG[0:3 * NE, j * P:(j + 1) * P],
                                               G3[:, ds(TPC * c + j, 1)].rearrange("p t a e -> p (t a e)"), identh[:],
                                               start=True, stop=True)
                    ins.then_inc(gates_turned, 1)

                def gated_k(c):
                    pe.wait_ge(gates_stored, 1 + c + 1)
                    pe.wait_ge(k_added, c + 1)
                    for j in range(TPC):
                        ins = nc.tensor.matmul(psK[:, j, :], GT[:, j * P:(j + 1) * P], K3[:], start=True, stop=True)
                    ins.then_inc(k_done, 1)

                up(0, 0, 0)
                with pe.Fori(0, NCH) as c:
                    turn_gates(c)
                    pair(c, 0, first=True)
                    with pe.Fori(1, NE // 2) as ep:
                        pair(c, ep)

            @block.scalar
            def _(act):
                act.sem_inc(relu_done, FC)
                act.sem_inc(gates_stored, 1)

                def relu(u, e, j):
                    for f in range(FC):
                        act.wait_ge(up_done, FC * u + f + 1)
                        act.wait_ge(H_lo, FC * u + f + 1)
                        if f == FC - ACT_HI:
                            act.wait_ge(down_done, u + 1)
                        ins = nc.scalar.activation(R[:, j, f, :], psZ[f][:], ACT.Relu, bias=b1[:, ds(e, 1), f], scale=1.0 / WS)
                        if f >= FC - ACT_HI:
                            ins = nc.scalar.activation(Hh[:, j, f, :], psZ[f][:], ACT.Relu, bias=b1[:, ds(e, 1), f], scale=1.0 / WS)
                        ins.then_inc(relu_done, 1)

                relu(0, 0, 0)
                with act.Fori(0, NCH) as c:
                    act.wait_ge(gates_turned, c + 1)
                    act.wait_ge(k_done, c + 1)
                    nc.scalar.activation(GT[:], psG[0:3 * NE, :], ACT.Copy).then_inc(gates_stored, 1)
                    with act.Fori(0, NE // 2) as ep:
                        for j in range(2):
                            relu(NE * c + 2 * ep + j + 1, 2 * ((ep + j) % (NE // 2)) + (1 - j), 1 - j)

            @block.vector
            def _(dve):
                dve.sem_inc(H_lo, 2 * FC)
                dve.sem_inc(y_added, 2)
                dve.sem_inc(k_added, 1)

                def split(u, j):
                    dve.wait_ge(down_done, u + 1)
                    for f in range(FC):
                        dve.wait_ge(relu_done, FC + FC * u + f + 1)
                        if f < FC - ACT_HI:
                            nc.vector.tensor_copy(Hh[:, j, f, :], R[:, j, f, :]).then_inc(H_hi, 1)
                            dve.wait_ge(H_hi, (FC - ACT_HI) * u + f + 1)
                        nc.vector.tensor_tensor(Hl[:, j, f, :], R[:, j, f, :], Hh[:, j, f, :], ALU.subtract).then_inc(H_lo, 1)

                def gate(c, u, e, j):
                    dve.wait_ge(down_done, 2 + u + 1)
                    dve.wait_ge(y_added, 2 + u)
                    for t in range(TPC):
                        ins = nc.vector.scalar_tensor_tensor(X[:, ds(TPC * c + t, 1), :], psY[j][:, t:t + 1, :],
                                                             Gs[:, ds(TPC * c + t, 1), ds(e, 1)].rearrange("p t e -> p (t e)"),
                                                             X[:, ds(TPC * c + t, 1), :], ALU.mult, ALU.add)
                    ins.then_inc(y_added, 1)

                def pair(c, ep, first=False):
                    for j in range(2):
                        u = NE * c + 2 * ep + j
                        split(u + 1, 1 - j)
                        if first and j == 1:
                            add_k(c)
                        gate(c, u, 2 * ep + j, j)

                def add_k(c):
                    dve.wait_ge(k_done, 1 + c + 1)
                    dve.wait_ge(y_added, 2 + NE * c + 1)
                    nc.vector.scalar_tensor_tensor(X[:, ds(TPC * c, TPC), :], psK[:], 1.0 / WS, X[:, ds(TPC * c, TPC), :],
                                                   ALU.mult, ALU.add).then_inc(k_added, 1)
                    dve.wait_ge(k_added, 1 + c + 1)

                split(0, 0)
                with dve.Fori(0, NCH) as c:
                    pair(c, 0, first=True)
                    with dve.Fori(1, NE // 2) as ep:
                        pair(c, ep)


def full_attention(nc, X, io):
    with Stage(nc, "full") as st:
        sb = st.sb
        woh, wol = sb("woh", [P, HB // 2, D], F16), sb("wol", [P, HB // 2, D], F16)
        OTh, OTl = sb("OTh", [P, HB // 2, T], F16), sb("OTl", [P, HB // 2, T], F16)
        with Stage(nc, "fullw") as st2:
            sb = st2.sb
            wTh, wTl = sb("wTh", [P, T], F16), sb("wTl", [P, T], F16)
            wq = sb("wqh", [P, HB, P], F16), sb("wql", [P, HB, P], F16)
            wk = sb("wkh", [P, HB, P], F16), sb("wkl", [P, HB, P], F16)
            wv = sb("wvh", [P, HB, DB], F16), sb("wvl", [P, HB, DB], F16)
            full_prepare(nc, X, wTh, wTl, wq, wk, wv, (woh, wol), io)
            full_heads(nc, wTh, wTl, wq, wk, wv, OTh, OTl, io)
        full_output(nc, X, OTh, OTl, woh, wol, io)


def full_prepare(nc, X, wTh, wTl, wq, wk, wv, wo, io):
    with Stage(nc, "bp") as st:
        sb, ps, sem = st.sb, st.ps, st.sem
        names = [("wqB", wq, HB * P), ("wkB", wk, HB * P), ("wvB", wv, HB * DB), ("woutB", wo, HB // 2 * D)]
        w32 = [sb(n, [P, size]) for n, _, size in names]
        ident = sb("ident", [P, P])
        seen = sb("seen", [P, 1])
        halfneg, epsc = sb("halfneg", [P, TPC]), sb("epsc", [P, TPC])
        stats, mv = sb("stats", [P, 2, TPC, 6]), sb("mv", [P, 2, TPC, 2])
        vare, rstd = sb("vare", [P, 2, TPC]), sb("rstd", [P, 2, TPC])
        w = sb("w", [P, 2, TPC, D])
        psX = [ps(f"psX{h}", [P, CH]) for h in range(2)]

        loaded, set_up, w_hi, w_lo = sem("loaded"), sem("set_up"), sem("w_hi"), sem("w_lo")
        bn_done, stats_ready, eps_added, rstd_ready = sem("bn_done"), sem("stats_ready"), sem("eps_added"), sem("rstd_ready")
        w_ready, transposed, wT_hi, wT_lo, added = sem("w_ready"), sem("transposed"), sem("wT_hi"), sem("wT_lo"), sem("added")
        LOADED = 5 * 16

        with st.block() as block:

            @block.sync
            def _(sp):
                sp.dma_start(ident[:], io["ident"]).then_inc(loaded, 16)
                for (n, _, _), dst in zip(names, w32):
                    src = io[n]
                    if n == "wvB":
                        sp.dma_start(dst[:], src).then_inc(loaded, 16)
                    else:
                        sp.dma_start(dst[:], src.rearrange("p a b -> p (a b)")).then_inc(loaded, 16)

            @block.gpsimd
            def _(pool):
                nc.gpsimd.memset(halfneg[:], -0.5).then_inc(set_up, 1)
                nc.gpsimd.memset(epsc[:], EPS).then_inc(set_up, 1)
                pool.wait_ge(set_up, 2)
                with pool.Fori(0, NCH // 2) as b:
                    for h in range(2):
                        c = 2 * b + h
                        pool.wait_ge(stats_ready, c + 1)
                        nc.gpsimd.tensor_tensor(vare[:, h], mv[:, h, :, 1], epsc[:], ALU.add).then_inc(eps_added, 1)
                        pool.wait_ge(eps_added, c + 1)
                        nc.gpsimd.tensor_tensor(rstd[:, h], vare[:, h], halfneg[:], ALU.pow).then_inc(rstd_ready, 1)

            @block.scalar
            def _(act):
                act.wait_ge(loaded, LOADED)
                for i, (_, (hi, _), _) in enumerate(names):
                    nc.scalar.activation(hi[:].rearrange("p a b -> p (a b)"), w32[i][:], ACT.Copy).then_inc(w_hi, 1)
                with act.Fori(0, NCH // 2) as b:
                    for h in range(2):
                        c = 2 * b + h
                        act.wait_ge(transposed, c + 1)
                        nc.scalar.activation(wTh[:, ds(c * CH, CH)], psX[h][:], ACT.Copy).then_inc(wT_hi, 1)

            @block.vector
            def _(dve):
                dve.sem_inc(wT_lo, 1)
                def stats_of(c, h):
                    for j in range(TPC):
                        nc.vector.bn_stats(stats[:, h, j, :], X[:, TPC * c + j, :]).then_inc(bn_done, 1)
                    dve.wait_ge(bn_done, TPC * c + TPC)
                    nc.vector.tensor_copy(seen[:], stats[:, h, TPC - 1, 0:1])
                    for j in range(TPC):
                        ins = nc.vector.bn_aggr(mv[:, h, j, :], stats[:, h, j, :])
                    ins.then_inc(stats_ready, 1)

                def normalise(c, h):
                    dve.wait_ge(rstd_ready, c + 1)
                    for j in range(TPC):
                        ins = nc.vector.tensor_scalar(w[:, h, j, :], X[:, TPC * c + j, :], mv[:, h, j, 0:1],
                                                      rstd[:, h, j:j + 1], ALU.subtract, ALU.mult)
                    ins.then_inc(w_ready, 1)

                def chunk(c, h, more):
                    if more:
                        stats_of(c + 2, h)
                    dve.wait_ge(w_ready, c + 1)
                    nc.vector.scalar_tensor_tensor(
                        X[:, ds(TPC * c, TPC), :], w[:, h], RSQRT2, X[:, ds(TPC * c, TPC), :],
                        ALU.mult, ALU.add).then_inc(added, 1)
                    if more or h == 0:
                        normalise(c + 1, 1 - h)
                    dve.wait_ge(wT_hi, c + 1)
                    nc.vector.tensor_tensor(wTl[:, ds(c * CH, CH)], psX[h][:], wTh[:, ds(c * CH, CH)], ALU.subtract).then_inc(wT_lo, 1)

                stats_of(0, 0)
                stats_of(1, 1)
                normalise(0, 0)
                with dve.Fori(0, NCH // 2 - 1) as b:
                    for h in range(2):
                        chunk(2 * b + h, h, True)
                for h in range(2):
                    chunk(NCH - 2 + h, h, False)
                for i, (_, (hi, lo), _) in enumerate(names):
                    dve.wait_ge(w_hi, i + 1)
                    nc.vector.tensor_tensor(lo[:].rearrange("p a b -> p (a b)"), w32[i][:],
                                            hi[:].rearrange("p a b -> p (a b)"), ALU.subtract).then_inc(w_lo, 1)

            @block.tensor
            def _(pe):
                pe.wait_ge(loaded, LOADED)
                with pe.Fori(0, NCH // 2) as b:
                    for h in range(2):
                        pe.wait_ge(w_ready, 2 * b + h + 1)
                        pe.wait_ge(wT_lo, 1 + 2 * b)
                        for j in range(TPC):
                            ins = nc.tensor.transpose(psX[h][:, j * P:(j + 1) * P], w[:, h, j, :], ident[:])
                        ins.then_inc(transposed, 1)


def full_heads(nc, wTh, wTl, wq, wk, wv, OTh, OTl, io):
    with Stage(nc, "bh") as st:
        sb, ps, sem = st.sb, st.ps, st.sem
        HALF = S // 2
        U = B * HB
        MROW = DB
        MROW2 = 96
        SUMS = KT - 1
        identh = sb("identh", [P, P], F16)
        ones = sb("ones", [P, DB])
        bq, bk = sb("bq", [P, 2 * HB]), sb("bk", [P, 2 * HB])
        bvb = sb("bvb", [P, HB, DB])
        KH = sb("KH", [P, 2, S], F16)
        K1 = sb("K1", [P, 2, S], F16)
        QH = sb("QH", [P, 2, S], F16)
        QL = sb("QL", [P, 2, S], F16)
        Vb = sb("Vb", [P, 2 * KT, HB, DB])
        V = sb("V", [P, 2, KT, DB])
        Mx = sb("Mx", [P, KT, 2])
        Mn, Ml = sb("Mn", [P, KT]), sb("Ml", [P, KT, 2], F16)
        E = sb("E", [P, KT, S])
        Es = sb("Es", [P, S])
        rden = sb("rden", [P, HALF])
        O = sb("O", [P, S])
        psA = ps("psA", [P, 2, HALF])
        psS = [ps(f"psS{i}", [P, 2, HALF]) for i in range(2)]
        psO = [ps(f"psO{i}", [P, HALF]) for i in range(2)]

        first_v = [psS[i][:, a] for i in range(2) for a in range(2)]

        loaded, set_up = sem("loaded"), sem("set_up")
        k_done, v_done, q_done = sem("k_done"), sem("v_done"), sem("q_done")
        k_hi, k_split, k_copied, v_biased, v_copied, q_hi, q_split = (
            sem(n) for n in ("k_hi", "k_split", "k_copied", "v_biased", "v_copied", "q_hi", "q_split"))
        rows_done, max_done, max_hi, max_split, max_row_done, max_row = (
            sem("rows_done"), sem("max_done"), sem("max_hi"), sem("max_split"), sem("max_row_done"), sem("max_row"))
        scores_done = sem("scores_done")
        exp_done = sem("exp_done")
        value_done = sem("value_done")
        summed = sem("summed")
        den_done = sem("den_done")
        recip_done = sem("recip_done")
        normed = sem("normed")
        o_hi = sem("o_hi")
        o_lo = sem("o_lo")
        half_normed = sem("half_normed")

        batch = lambda u: u // HB
        head = lambda u: u % HB

        row_bank = lambda s, i: (psO[s][:], psA[:, 1], psA[:, 0])[i % 3]

        def add_tile(eng, engine, u, t):
            eng.wait_ge(exp_done, 2 + KT * u + t + 1)
            if t == 1:
                eng.wait_ge(den_done, 1 + u)
                engine.tensor_tensor(Es[:], E[:, 0, :], E[:, 1, :], ALU.add).then_inc(summed, 1)
            else:
                eng.wait_ge(summed, SUMS * (u + 1) + t - 1)
                engine.tensor_tensor(Es[:], Es[:], E[:, t, :], ALU.add).then_inc(summed, 1)

        with st.block() as block:

            @block.sync
            def _(sp):
                sp.dma_start(identh[:], io["identh"]).then_inc(loaded, 16)
                for a in range(2):
                    sp.dma_start(bq[:, a * HB:(a + 1) * HB], io["bqB"]).then_inc(loaded, 16)
                    sp.dma_start(bk[:, a * HB:(a + 1) * HB], io["bkB"]).then_inc(loaded, 16)
                sp.dma_start(bvb[:].rearrange("p a b -> p (a b)"),
                             io["bvB"].rearrange("(a n) -> a n", a=1).broadcast_to([P, HB * DB])).then_inc(loaded, 16)

            LOADED = 6 * 16

            @block.tensor
            def _(pe):
                pe.sem_inc(den_done, 1)
                def three(out, a, b, first=True, last=True):
                    nc.tensor.matmul(out, a[0], b[0], start=first, stop=False)
                    nc.tensor.matmul(out, a[0], b[1], start=False, stop=False)
                    return nc.tensor.matmul(out, a[1], b[0], start=False, stop=last)

                def tokens(u, at, n):
                    return wTh[:, ds(batch(u) * S + at, n)], wTl[:, ds(batch(u) * S + at, n)]

                def make_k(u, a):
                    three(psA[:, 1 - a], [x[:, ds(head(u), 1), :] for x in wk], tokens(u, a * HALF, HALF)).then_inc(k_done, 1)

                def make_v(i, out=psA[:, 1]):
                    token = [x[:, ds(i * P, P)] for x in (wTh, wTl)]
                    three(out, token, [x[:].rearrange("p a b -> p (a b)") for x in wv]).then_inc(v_done, 1)

                def make_q(u, a, first=False):
                    if a == 0:
                        pe.wait_ge(v_biased, KT + u)
                        if first:
                            pe.wait_ge(k_split, 2 * u + 1)
                    elif first:
                        pe.wait_ge(k_split, 2 * u + 2)
                    else:
                        pe.wait_ge(recip_done, u - 1)
                    three(psA[:, 1 - a], [x[:, ds(head(u), 1), :] for x in wq], tokens(u, a * HALF, HALF)).then_inc(q_done, 1)

                def rows(u, s, i):
                    t, a = i // 2, i % 2
                    if i == 0:
                        pe.wait_ge(q_hi, 2 * u + 1)
                        pe.wait_ge(normed, u + 1)
                    elif i < 3:
                        pe.wait_ge(q_split, 2 * u + i)
                    else:
                        pe.wait_ge(max_done, 2 * KT * u + i - 2)
                    nc.tensor.matmul(row_bank(s, i), QH[:, s, t * P:(t + 1) * P], KH[:, s, a * HALF:(a + 1) * HALF],
                                     start=True, stop=True).then_inc(rows_done, 1)

                def max_rows(u):
                    pe.wait_ge(max_split, u + 1)
                    for t in range(KT):
                        at = MROW if t < KT // 2 else MROW2
                        ins = nc.tensor.matmul(psA[at:at + 2, 0, t % 4 * P:(t % 4 + 1) * P], Ml[:, t, :], identh[:],
                                               start=True, stop=True)
                    ins.then_inc(max_row_done, 1)

                def scores(u, s, t, halves=(0, 1)):
                    if 0 in halves:
                        pe.wait_ge(exp_done, KT * u + t + 1)
                        if t == 0:
                            pe.wait_ge(k_copied, u + 1)
                            pe.wait_ge(max_row, 2 * u + 2)
                    keys = slice(t * P, (t + 1) * P)
                    for a in halves:
                        q = slice(a * HALF, (a + 1) * HALF)
                        nc.tensor.matmul(psS[t % 2][:, a], KH[:, s, keys], QH[:, s, q], start=True, stop=False)
                        ins = nc.tensor.matmul(psS[t % 2][:, a], K1[:, s, keys], QL[:, s, q], start=False, stop=True)
                    if 1 in halves:
                        ins.then_inc(scores_done, 1)

                def values(u, s, t):
                    pe.wait_ge(exp_done, 2 + KT * u + t + 1)
                    if t == 0:
                        pe.wait_ge(normed, u + 1)
                        pe.wait_ge(v_copied, u + 1)
                    for a in range(2):
                        ins = nc.tensor.matmul(psO[s][DB * a:DB * (a + 1), :], V[:, s, t, :], E[:, t, a * HALF:(a + 1) * HALF],
                                               start=(t == 0), stop=(t == KT - 1))
                    ins.then_inc(value_done, 1)

                def denominators(u):
                    pe.wait_ge(summed, SUMS * (u + 2))
                    for a in range(2):
                        ins = nc.tensor.matmul(psA[DB * a:DB * (a + 1), 0], ones[:], Es[:, a * HALF:(a + 1) * HALF],
                                               start=True, stop=True)
                    ins.then_inc(den_done, 1)

                def next_k(u, a, done, value):
                    pe.wait_ge(done, value)
                    make_k(u, a)

                def unit(u, s, first=False, more=2):
                    n, o = u + 1, 1 - s
                    if more:
                        make_q(n, 0)
                    if not first:
                        if more:
                            pe.wait_ge(k_split, 2 * n + 2)
                        denominators(u - 1)
                    scores(u, s, 1)
                    values(u, s, 0)
                    scores(u, s, 2)
                    values(u, s, 1)
                    scores(u, s, 3)
                    if more:
                        make_q(n, 1, first)
                    values(u, s, 2)
                    for t in range(4, KT):
                        if more:
                            rows(n, o, 4 * t - 16)
                        scores(u, s, t, (0,))
                        if more:
                            rows(n, o, 4 * t - 15)
                        scores(u, s, t, (1,))
                        if more:
                            rows(n, o, 4 * t - 14)
                        values(u, s, t - 1)
                        if more:
                            rows(n, o, 4 * t - 13)
                    if more == 2:
                        next_k(n + 1, 0, max_done, 2 * KT * (n + 1) - 2)
                    if more:
                        max_rows(n)
                    values(u, s, 7)
                    if more == 2:
                        pe.wait_ge(k_split, 2 * n + 3)
                        make_v((KT + 1 + u) % NT)
                        next_k(n + 1, 1, max_row, 2 * n + 2)
                    if more:
                        scores(n, o, 0)

                pe.wait_ge(loaded, LOADED)
                pe.wait_ge(set_up, 4)
                make_k(0, 0)
                make_k(0, 1)
                for t in range(KT):
                    if t >= len(first_v):
                        pe.wait_ge(v_biased, t - len(first_v) + 1)
                    make_v(t, first_v[t % len(first_v)])
                make_q(0, 0)
                make_q(0, 1, first=True)
                for i in range(2 * KT):
                    rows(0, 0, i)
                next_k(1, 0, max_done, 2 * KT - 2)
                max_rows(0)
                pe.wait_ge(k_split, 3)
                make_v(KT)
                next_k(1, 1, max_row, 2)
                scores(0, 0, 0)
                unit(0, 0, first=True)
                unit(1, 1)
                with pe.Fori(1, U // 2 - 1) as pr:
                    for s in range(2):
                        unit(2 * pr + s, s)
                unit(U - 2, 0, more=1)
                unit(U - 1, 1, more=0)
                pe.wait_ge(recip_done, U - 1)
                denominators(U - 1)

            @block.scalar
            def _(act):
                act.sem_inc(exp_done, 2)

                def hi(u, s, a, dst, bias, done, signal):
                    act.wait_ge(done, 2 * u + a + 1)
                    nc.scalar.activation(dst[:, s, a * HALF:(a + 1) * HALF], psA[:, 1 - a], ACT.Identity,
                                         bias=bias[:, ds(a * HB + head(u), 1)]).then_inc(signal, 1)

                def row(u, s):
                    act.wait_ge(max_row_done, u + 1)
                    for a, at in enumerate((MROW, MROW2)):
                        nc.scalar.activation(QL[MROW:MROW + 2, s, a * HALF:(a + 1) * HALF], psA[at:at + 2, 0],
                                             ACT.Copy).then_inc(max_row, 1)

                def exp(u, s, t):
                    act.wait_ge(scores_done, KT * u + t + 1)
                    act.wait_ge(value_done, KT * u + t + 1)
                    act.wait_ge(summed, SUMS * u + max(t, 1))
                    nc.scalar.activation(E[:, t, :], psS[t % 2][:].rearrange("p a q -> p (a q)"), ACT.Exp,
                                         scale=SCALE_B).then_inc(exp_done, 1)

                def out_hi(u, s):
                    act.wait_ge(half_normed, 2 * u + 2)
                    rows_ = slice(DB * s, DB * (s + 1))
                    nc.scalar.activation(OTh[rows_, ds(head(u) // 2, 1), ds(batch(u) * S, S)], O[rows_, None, :],
                                         ACT.Copy).then_inc(o_hi, 1)

                def copy_v(u, s):
                    act.wait_ge(v_biased, KT * (batch(u) + 1))
                    act.wait_ge(value_done, KT * u)
                    nc.scalar.activation(V[:, s], Vb[:, ds(batch(u) % 2 * KT, KT), ds(head(u), 1), :], ACT.Copy).then_inc(v_copied, 1)

                def unit(u, s, first=False, more=2):
                    n, o = u + 1, 1 - s
                    exp(u, s, 0)
                    if more:
                        hi(n, o, 0, QH, bq, q_done, q_hi)
                    exp(u, s, 1)
                    exp(u, s, 2)
                    exp(u, s, 3)
                    if more:
                        hi(n, o, 1, QH, bq, q_done, q_hi)
                    exp(u, s, 4)
                    if not first:
                        out_hi(u - 1, o)
                    exp(u, s, 5)
                    if more:
                        copy_v(n, o)
                    exp(u, s, 6)
                    exp(u, s, 7)
                    if more == 2:
                        hi(n + 1, s, 0, KH, bk, k_done, k_hi)
                    if more:
                        row(n, o)
                    if more == 2:
                        hi(n + 1, s, 1, KH, bk, k_done, k_hi)

                act.wait_ge(loaded, LOADED)
                for dst, bias, done, signal in ((KH, bk, k_done, k_hi), (QH, bq, q_done, q_hi)):
                    for a in range(2):
                        hi(0, 0, a, dst, bias, done, signal)
                copy_v(0, 0)
                act.wait_ge(set_up, 4)
                hi(1, 1, 0, KH, bk, k_done, k_hi)
                row(0, 0)
                hi(1, 1, 1, KH, bk, k_done, k_hi)
                unit(0, 0, first=True)
                unit(1, 1)
                with act.Fori(1, U // 2 - 1) as pr:
                    for s in range(2):
                        unit(2 * pr + s, s)
                unit(U - 2, 0, more=1)
                unit(U - 1, 1, more=0)
                out_hi(U - 1, 1)

            @block.vector
            def _(dve):
                dve.sem_inc(normed, 2)
                flat = lambda x: x.rearrange("p a q -> p (a q)")

                def k_low(u, s, a):
                    dve.wait_ge(k_hi, 2 * u + a + 1)
                    q = slice(a * HALF, (a + 1) * HALF)
                    nc.vector.scalar_tensor_tensor(KH[DB:P, s, q], psA[DB:P, 1 - a], bk[DB:P, ds(head(u), 1)], KH[DB:P, s, q],
                                                   ALU.add, ALU.subtract).then_inc(k_split, 1)

                def k_copy(u, s):
                    nc.vector.tensor_copy(K1[0:DB, s, :], KH[0:DB, s, :]).then_inc(k_copied, 1)

                def v_bias(i, src=psA[:, 1]):
                    dve.wait_ge(v_done, i + 1)
                    nc.vector.tensor_tensor(Vb[:, ds(i % (2 * KT), 1)], src.rearrange("p (h d) -> p h d", d=DB)[:, None],
                                            bvb[:, None], ALU.add).then_inc(v_biased, 1)

                def q_low(u, s, a):
                    dve.wait_ge(q_hi, 2 * u + a + 1)
                    q = slice(a * HALF, (a + 1) * HALF)
                    nc.vector.scalar_tensor_tensor(QL[0:DB, s, q], psA[0:DB, 1 - a], bq[0:DB, ds(head(u), 1)], QH[0:DB, s, q],
                                                   ALU.add, ALU.subtract).then_inc(q_split, 1)

                def row_max(u, s, i):
                    dve.wait_ge(rows_done, 2 * KT * u + i + 1)
                    nc.vector.tensor_reduce(Mx[:, i // 2, i % 2:i % 2 + 1], row_bank(s, i), AX_X, ALU.max).then_inc(max_done, 1)

                def max_halves(u):
                    dve.wait_ge(max_done, 2 * KT * (u + 1))
                    nc.vector.tensor_reduce(Mn[:], Mx[:], AX_X, ALU.max, negate=True).then_inc(max_hi, 1)
                    nc.vector.tensor_reduce(Ml[:, :, 0], Mx[:], AX_X, ALU.max, negate=True).then_inc(max_hi, 1)
                    dve.wait_ge(max_hi, 2 * u + 2)
                    nc.vector.tensor_tensor(Ml[:, :, 1], Mn[:], Ml[:, :, 0], ALU.subtract).then_inc(max_split, 1)

                def norm(u, s):
                    dve.wait_ge(den_done, 1 + u + 1)
                    nc.vector.reciprocal(rden[:], psA[:, 0]).then_inc(recip_done, 1)
                    dve.wait_ge(recip_done, u + 1)
                    dve.wait_ge(value_done, KT + KT * u + KT)
                    dve.wait_ge(o_lo, u + 1)
                    for a in range(2):
                        src = slice(DB * a, DB * (a + 1))
                        nc.vector.tensor_tensor(O[DB * s:DB * (s + 1), a * HALF:(a + 1) * HALF], psO[s][src, :], rden[src, :],
                                                ALU.mult).then_inc(half_normed, 1)
                    dve.wait_ge(half_normed, 2 * u + 2)
                    dve.sem_inc(normed, 1)

                def unit(u, s, first=False, more=2):
                    n, o = u + 1, 1 - s
                    if more:
                        q_low(n, o, 0)
                    if not first:
                        norm(u - 1, o)
                    if more:
                        q_low(n, o, 1)
                    for i in range(2 * KT):
                        if i == 3 and not first and more:
                            k_copy(n, o)
                        if more:
                            row_max(n, o, i)
                    if more:
                        max_halves(n)
                    if not more:
                        for t in range(1, KT):
                            add_tile(dve, nc.vector, u, t)
                    if more == 2:
                        k_low(n + 1, s, 0)
                        v_bias(KT + 1 + u)
                        k_low(n + 1, s, 1)

                nc.vector.memset(ones[:], 1.0).then_inc(set_up, 1)
                nc.vector.memset(K1[DB:P, :, :], 0.0).then_inc(set_up, 1)
                nc.vector.memset(QL[DB:P, :, :], 0.0).then_inc(set_up, 1)
                dve.wait_ge(set_up, 3)
                nc.vector.memset(K1[DB:DB + 2, :, :], 1.0).then_inc(set_up, 1)
                dve.wait_ge(loaded, LOADED)
                k_low(0, 0, 0)
                for t in range(KT):
                    v_bias(t, first_v[t % len(first_v)])
                k_low(0, 0, 1)
                k_copy(0, 0)
                q_low(0, 0, 0)
                q_low(0, 0, 1)
                for i in range(2 * KT):
                    row_max(0, 0, i)
                max_halves(0)
                k_low(1, 1, 0)
                v_bias(KT)
                k_low(1, 1, 1)
                k_copy(1, 1)
                unit(0, 0, first=True)
                unit(1, 1)
                with dve.Fori(1, U // 2 - 1) as pr:
                    for s in range(2):
                        unit(2 * pr + s, s)
                unit(U - 2, 0, more=1)
                unit(U - 1, 1, more=0)
                norm(U - 1, 1)

            @block.gpsimd
            def _(pool):
                pool.sem_inc(summed, SUMS)
                pool.sem_inc(value_done, KT)
                pool.sem_inc(o_lo, 2)
                def out_lo(u, s, sums_so_far):
                    pool.wait_ge(summed, SUMS + sums_so_far)
                    pool.wait_ge(o_hi, u + 1)
                    rows_ = slice(DB * s, DB * (s + 1))
                    nc.gpsimd.tensor_tensor(OTl[rows_, ds(head(u) // 2, 1), ds(batch(u) * S, S)], O[rows_, None, :],
                                            OTh[rows_, ds(head(u) // 2, 1), ds(batch(u) * S, S)], ALU.subtract).then_inc(o_lo, 1)

                def unit(u, s, first=False, last=False):
                    for t in range(1, 4):
                        add_tile(pool, nc.gpsimd, u, t)
                    if not first:
                        out_lo(u - 1, 1 - s, SUMS * u + 3)
                        pool.wait_ge(o_lo, 2 + u)
                    for t in range(4, KT):
                        add_tile(pool, nc.gpsimd, u, t)

                unit(0, 0, first=True)
                unit(1, 1)
                with pool.Fori(1, U // 2 - 1) as pr:
                    for s in range(2):
                        unit(2 * pr + s, s)
                unit(U - 2, 0)
                out_lo(U - 2, 0, SUMS * (U - 1))
                out_lo(U - 1, 1, SUMS * U)
                pool.wait_ge(o_lo, 2 + U)


def full_output(nc, X, OTh, OTl, woh, wol, io):
    with Stage(nc, "bo") as st:
        sb, ps, sem = st.sb, st.ps, st.sem
        bob, gb, bb = sb("bob", [P, D]), sb("gb", [P, D]), sb("bb", [P, D])
        g2, b2 = sb("g2", [P, D]), sb("b2", [P, D])
        seen = sb("seen", [P, 1])
        halfneg, epsc = sb("halfneg", [P, TPC]), sb("epsc", [P, TPC])
        stats, mv = sb("stats", [P, 2, TPC, 6]), sb("mv", [P, 2, TPC, 2])
        vare, rstd = sb("vare", [P, 2, TPC]), sb("rstd", [P, 2, TPC])
        y, yn = sb("y", [P, 2, TPC, D]), sb("yn", [P, 2, TPC, D])
        psY = [ps(f"psY{h}", [P, TPC, D]) for h in range(2)]

        loaded, set_up, scaled = sem("loaded"), sem("set_up"), sem("scaled")
        projected, biased = sem("projected"), sem("biased")
        bn_done, stats_ready, eps_added, rstd_ready = sem("bn_done"), sem("stats_ready"), sem("eps_added"), sem("rstd_ready")
        normed, gained, shifted, added = sem("normed"), sem("gained"), sem("shifted"), sem("added")

        wide = lambda a: a[:, None, :].broadcast_to([P, TPC, D])

        with st.block() as block:

            @block.sync
            def _(sp):
                for dst, n in ((bob, "boutB"), (gb, "lngB"), (bb, "lnbB")):
                    sp.dma_start(dst[:], io[n].rearrange("(a n) -> a n", a=1).broadcast_to([P, D])).then_inc(loaded, 16)

            @block.tensor
            def _(pe):
                with pe.Fori(0, NCH // 2) as b:
                    for h in range(2):
                        c = 2 * b + h
                        pe.wait_ge(biased, 1 + 2 * b)
                        for j in range(TPC):
                            for m in range(HB // 2):
                                o = psY[h][:, j, :]
                                oh, ol = OTh[:, m, ds(c * CH + j * P, P)], OTl[:, m, ds(c * CH + j * P, P)]
                                nc.tensor.matmul(o, oh, woh[:, m, :], start=(m == 0), stop=False)
                                nc.tensor.matmul(o, oh, wol[:, m, :], start=False, stop=False)
                                ins = nc.tensor.matmul(o, ol, woh[:, m, :], start=False, stop=(m == HB // 2 - 1))
                        ins.then_inc(projected, 1)

            @block.vector
            def _(dve):
                dve.sem_inc(biased, 1)
                dve.sem_inc(normed, 1)
                def stats_of(c, h, first=False):
                    dve.wait_ge(projected, c + 1)
                    if not first:
                        dve.wait_ge(normed, c)
                    nc.vector.tensor_tensor(y[:, h], psY[h][:], wide(bob), ALU.add).then_inc(biased, 1)
                    dve.wait_ge(biased, 1 + c + 1)
                    for j in range(TPC):
                        nc.vector.bn_stats(stats[:, h, j, :], y[:, h, j, :]).then_inc(bn_done, 1)
                    dve.wait_ge(bn_done, TPC * c + TPC)
                    nc.vector.tensor_copy(seen[:], stats[:, h, TPC - 1, 0:1])
                    for j in range(TPC):
                        ins = nc.vector.bn_aggr(mv[:, h, j, :], stats[:, h, j, :])
                    ins.then_inc(stats_ready, 1)

                def normalise(c, h):
                    dve.wait_ge(rstd_ready, c + 1)
                    dve.wait_ge(added, 1 + 2 * (c // 2))
                    for j in range(TPC):
                        ins = nc.vector.tensor_scalar(yn[:, h, j, :], y[:, h, j, :], mv[:, h, j, 0:1],
                                                      rstd[:, h, j:j + 1], ALU.subtract, ALU.mult)
                    ins.then_inc(normed, 1)

                dve.wait_ge(loaded, 48)
                nc.vector.tensor_scalar(g2[:], gb[:], RSQRT2, None, ALU.mult).then_inc(scaled, 1)
                nc.vector.tensor_scalar(b2[:], bb[:], RSQRT2, None, ALU.mult).then_inc(scaled, 1)
                dve.wait_ge(scaled, 2)
                stats_of(0, 0, first=True)
                nc.vector.tensor_tensor(X[:], X[:], b2[:, None, :].broadcast_to([P, NT, D]), ALU.add).then_inc(shifted, 1)
                with dve.Fori(0, NCH // 2 - 1) as b:
                    for h in range(2):
                        stats_of(2 * b + h + 1, 1 - h)
                        normalise(2 * b + h, h)
                stats_of(NCH - 1, 1)
                normalise(NCH - 2, 0)
                normalise(NCH - 1, 1)
                dve.wait_ge(added, 1 + NCH)

            @block.gpsimd
            def _(pool):
                pool.sem_inc(added, 1)
                nc.gpsimd.memset(halfneg[:], -0.5).then_inc(set_up, 1)
                nc.gpsimd.memset(epsc[:], EPS).then_inc(set_up, 1)
                pool.wait_ge(set_up, 2)

                def rstd_of(c, h):
                    pool.wait_ge(stats_ready, c + 1)
                    nc.gpsimd.tensor_tensor(vare[:, h], mv[:, h, :, 1], epsc[:], ALU.add).then_inc(eps_added, 1)
                    pool.wait_ge(eps_added, c + 1)
                    nc.gpsimd.tensor_tensor(rstd[:, h], vare[:, h], halfneg[:], ALU.pow).then_inc(rstd_ready, 1)

                def add(c, h):
                    pool.wait_ge(normed, 1 + c + 1)
                    nc.gpsimd.tensor_tensor(yn[:, h], yn[:, h], wide(g2), ALU.mult).then_inc(gained, 1)
                    pool.wait_ge(gained, c + 1)
                    nc.gpsimd.tensor_tensor(X[:, ds(TPC * c, TPC), :], yn[:, h], X[:, ds(TPC * c, TPC), :], ALU.add).then_inc(added, 1)

                rstd_of(0, 0)
                pool.wait_ge(scaled, 2)
                pool.wait_ge(shifted, 1)
                with pool.Fori(0, NCH // 2 - 1) as b:
                    for h in range(2):
                        rstd_of(2 * b + h + 1, 1 - h)
                        add(2 * b + h, h)
                rstd_of(NCH - 1, 1)
                add(NCH - 2, 0)
                add(NCH - 1, 1)


def transformer_layer(nc, io, out):
    X_ctx = ExitStack()
    with X_ctx:
        X = X_ctx.enter_context(nc.sbuf_tensor("X", [P, NT, D], F32))
        with Stage(nc, "band") as st:
            Q4 = st.sb("Q4", [P, 4, T], F16)
            K4 = st.sb("K4", [P, 4, WIN + T], F16)
            V = st.sb("V", [P, NB, 2, HA, VW], F16)
            qk = {(n, part): st.sb(f"{n}{part}", [P, T], F16) for n in "qk" for part in "hl"}
            qk_hi, qk_lo, stacked, batch_stacked = (st.sem(n) for n in ("qk_hi", "qk_lo", "stacked", "batch_stacked"))
            band_project(nc, X, Q4, K4, V, qk, qk_hi, qk_lo, stacked, batch_stacked, io)
            band_attend(nc, X, Q4, K4, V, qk, qk_hi, qk_lo, stacked, batch_stacked, io)
        experts(nc, X, io, "f1")
        full_attention(nc, X, io)
        experts(nc, X, io, "f2")
        with Stage(nc, "out") as st:
            stored = st.sem("stored")
            with st.block() as block:
                @block.sync
                def _(sp):
                    sp.dma_start(out.rearrange("b (t p) d -> p (b t) d", p=P), X[:]).then_inc(stored, 16)
                    sp.wait_ge(stored, 16)


def shape_constants():
    half = D // 2
    inv = (np.float32(1.0) / np.power(10000.0, np.arange(half) / half).astype(np.float32)).astype(np.float32)
    ang = (np.arange(S, dtype=np.float32)[:, None] * inv[None, :]).T
    c, s = np.cos(ang), np.sin(ang)
    q, k = np.arange(P)[:, None] % WIN, np.arange(P)[None, :]
    band = (k >= q) & (k <= q + WIN)
    row = np.arange(P)
    fold = np.zeros((P, 2, P), np.float32)
    for j in range(2):
        fold[row, j, WIN * j + row % WIN] = 1.0
    return {
        "cos": np.concatenate([c, c]).astype(np.float32),
        "sin": np.concatenate([-s, s]).astype(np.float32),
        "ident": np.eye(P, dtype=np.float32),
        "identh": np.eye(P, dtype=np.float16),
        "bandm": np.where(np.stack([band & (k >= WIN), band], 1), 0.0, -1e30).astype(np.float32),
        "headm": ((row[:, None] % 32) // DA == np.arange(4)[None, :]).astype(np.float16),
        "parm": (row[:, None] // WIN == np.arange(2)[None, :]).astype(np.float32),
        "fold": fold,
        "rank": np.broadcast_to((NE - np.arange(NE)).astype(np.float32), (P, NE)).copy(),
    }


def laid_out(a):
    f = {k: np.asarray(v) for k, v in a.items()}
    wq, wk, wv = f["L0_attn_a_Wq"], f["L0_attn_a_Wk"], f["L0_attn_a_Wv"]
    bq, bk = f["L0_attn_a_bq"], f["L0_attn_a_bk"]
    half = D // 2
    roll = lambda x: np.concatenate([x[half:], x[:half]])
    wqk = f["L0_attn_b_W_qk"].reshape(D, HB, DB, 2)
    bqk = f["L0_attn_b_b_qk"].reshape(HB, DB, 2)
    dup = lambda x: np.concatenate([x, x], axis=-1)
    c = np.ascontiguousarray
    return {
        "x": f["L0_attn_a_hidden_state"],
        "wA": c(np.stack([wq.T, roll(wq).T, wk.T, roll(wk).T, wv.T], axis=1)),
        "biasA": c(np.stack([bq, roll(bq), bk, roll(bk)], axis=1)),
        "bv": f["L0_attn_a_bv"],
        "woT": c(f["L0_attn_a_Wo"].T),
        "bo": f["L0_attn_a_bo"],
        "wqB": c(dup(wqk[..., 0])), "wkB": c(dup(wqk[..., 1])),
        "bqB": c(dup(bqk[..., 0]).T), "bkB": c(dup(bqk[..., 1]).T),
        "wvB": f["L0_attn_b_W_v"], "bvB": f["L0_attn_b_b_v"],
        "woutB": c(f["L0_attn_b_W_out"].reshape(HB // 2, 2 * DB, D).transpose(1, 0, 2)),
        "boutB": f["L0_attn_b_b_out"],
        "lngB": f["L0_attn_b_ln_gamma"], "lnbB": f["L0_attn_b_ln_beta"],
        "gammaF": c(f["L0_ffn_gamma"][:, None]), "betaF": c(f["L0_ffn_beta"][:, None]),
        "wrF": f["L0_ffn_Wr"], "brF": f["L0_ffn_br"],
        "w1F": c(f["L0_ffn_W1"].transpose(1, 0, 2)),
        "b1F": c(f["L0_ffn_b1"].reshape(NE, FC, P).transpose(2, 0, 1)),
        "w2F": c(f["L0_ffn_W2"].reshape(NE, FC, P, D).transpose(2, 0, 1, 3)),
        "b2F": c(f["L0_ffn_b2"].T),
        **shape_constants(),
    }


def kernel(**inputs):
    import concourse.bacc as bacc
    from concourse.bass_utils import run_bass_kernel_spmd

    nc = bacc.Bacc("TRN2", target_bir_lowering=False, num_devices=1)
    arrays = laid_out(inputs)
    io = {n: nc.dram_tensor(f"in_{n}", a.shape, mybir.dt.from_np(a.dtype), kind="ExternalInput").ap()
          for n, a in arrays.items()}
    out = nc.dram_tensor("out", (B, S, D), F32, kind="ExternalOutput").ap()
    transformer_layer(nc, io, out)
    r = run_bass_kernel_spmd(nc, [{f"in_{n}": a for n, a in arrays.items()}], core_ids=[0])
    return r.results[0]["out"]
```

```python
from contextlib import ExitStack

import numpy as np

import concourse.bass as bass
from concourse import mybir

F32 = mybir.dt.float32
F16 = mybir.dt.float16
BF16 = mybir.dt.bfloat16
ALU = mybir.AluOpType
ACT = mybir.ActivationFunctionType
AX_X = mybir.AxisListType.X
ds = bass.ds

P = 128
D = 128
B, S = 4, 1024
T = B * S
NT = T // P
CH = 512
NCH = T // CH
TPC = CH // P
EPS = 1e-5

HA, DA = 16, 8
WIN = 64
NB = T // WIN
SCALE_A = 1.0 / float(np.sqrt(np.float32(DA)))
VW = DA + 1

HB, DB = 8, 64
SCALE_B = DB ** -0.5
KT = S // P
RSQRT2 = 2 ** -0.5

NE, FF = 8, 512
FC = FF // P
WS = 64.0



class Stage:

    def __init__(self, nc, tag):
        self.nc, self.tag, self.ctx, self.sems = nc, tag, ExitStack(), []

    def __enter__(self):
        self.ctx.__enter__()
        return self

    def __exit__(self, *e):
        if self.sems:
            self.nc.clear_and_free_semaphores(self.sems)
            self.nc.all_engine_barrier()
        return self.ctx.__exit__(*e)

    def sb(self, name, shape, dt=F32):
        return self.ctx.enter_context(self.nc.sbuf_tensor(f"{self.tag}_{name}", shape, dt))

    def ps(self, name, shape, dt=F32):
        return self.ctx.enter_context(self.nc.psum_tensor(f"{self.tag}_{name}", shape, dt))

    def sem(self, name):
        self.sems.append(self.nc.alloc_semaphore(name=f"{self.tag}_{name}"))
        return self.sems[-1]

    def block(self):
        return self.nc.Block()


def stack(sp, batches, Q4, K4, qk, qk_hi, qk_lo, stacked, batch_stacked):
    with sp.Fori(*batches) as b:
        sp.wait_ge(qk_hi, 1 + (b + 1) * 2 * (S // CH))
        sp.wait_ge(qk_lo, 1 + (b + 1) * 2 * (S // CH))
        for g in range(4):
            for j in range(4):
                rows, src = slice(32 * j, 32 * j + 32), slice(32 * g, 32 * g + 32)
                sp.dma_start(Q4[rows, g, ds(b * S, S)], qk["q", "hhll"[j]][src, ds(b * S, S)]).then_inc(stacked, 16)
                sp.dma_start(K4[rows, g, ds(b * S + WIN, S)], qk["k", "hlhl"[j]][src, ds(b * S, S)]).then_inc(stacked, 16)
        sp.wait_ge(stacked, STACKS * (b + 1))
        sp.sem_inc(batch_stacked, 1)


class SecondPart:

    def __init__(self, st):
        sb = st.sb
        self.ident, self.identb = sb("ident", [P, P]), sb("identb", [P, P], BF16)
        self.bandm32 = sb("bandm32", [P, 2, P])
        self.bandm = sb("bandm", [P, 2, P], BF16)
        self.masks = sb("masks", [P, NT, P], BF16)
        self.headm = sb("headm", [P, 4], F16)
        self.parm = sb("parm", [P, 2])
        self.fold = sb("fold", [P, 2, P])
        self.wo32, self.woh, self.wol = sb("wo32", [P, D]), sb("woh", [P, D], F16), sb("wol", [P, D], F16)
        self.bob = sb("bob", [P, D])
        self.loaded, self.prepared, self.masked = st.sem("late_loaded"), st.sem("late_prepared"), st.sem("late_masked")

    def load(self, sp, io):
        sp.dma_start(self.ident[:], io["ident"]).then_inc(self.loaded, 16)
        sp.dma_start(self.wo32[:], io["woT"]).then_inc(self.loaded, 16)
        sp.dma_start(self.bandm32[:], io["bandm"]).then_inc(self.loaded, 16)
        sp.dma_start(self.headm[:], io["headm"]).then_inc(self.loaded, 16)
        sp.dma_start(self.parm[:], io["parm"]).then_inc(self.loaded, 16)
        sp.dma_start(self.fold[:], io["fold"]).then_inc(self.loaded, 16)
        sp.dma_start(self.bob[:], io["bo"].rearrange("(a n) -> a n", a=1).broadcast_to([P, D])).then_inc(self.loaded, 16)

    def prepare(self, nc, pool):
        pool.wait_ge(self.loaded, 7 * 16)
        nc.gpsimd.tensor_copy(self.woh[:], self.wo32[:]).then_inc(self.prepared, 1)
        nc.gpsimd.tensor_copy(self.identb[:], self.ident[:]).then_inc(self.prepared, 1)
        nc.gpsimd.tensor_copy(self.bandm[:], self.bandm32[:]).then_inc(self.prepared, 1)
        pool.wait_ge(self.prepared, 3)
        nc.gpsimd.tensor_tensor(self.wol[:], self.wo32[:], self.woh[:], ALU.subtract).then_inc(self.prepared, 1)

    def copy_masks(self, sp):
        sp.wait_ge(self.prepared, 3)
        sp.dma_start(self.masks[:], self.bandm[:, 1:2, :].broadcast_to([P, NT, P])).then_inc(self.masked, 16)
        sp.wait_ge(self.masked, 16)
        sp.dma_start(self.masks[:].rearrange("p (b i) k -> p b i k", b=B)[:, :, 0, :],
                     self.bandm[:, 0:1, :].broadcast_to([P, B, P])).then_inc(self.masked, 16)

    PREPARED, MASKED = 4, 32


STACKED_FIRST = B // 2
STACKS = 32 * 16


def band_project(nc, X, Q4, K4, V, qk, qk_hi, qk_lo, stacked, batch_stacked, late, io):
    with Stage(nc, "a1") as st:
        sb, ps, sem = st.sb, st.ps, st.sem
        w32, whi, wlo = sb("w32", [P, 5, D]), sb("whi", [P, 5, D], F16), sb("wlo", [P, 5, D], F16)
        bias = sb("bias", [P, 4])
        bvb = sb("bvb", [P, D])
        cos, sin = sb("cos", [P, S]), sb("sin", [P, S])
        ident = sb("ident", [P, P])
        seen = sb("seen", [P, 1])
        halfneg, epsc = sb("halfneg", [P, TPC]), sb("epsc", [P, TPC])
        stats, mv = sb("stats", [P, 2, TPC, 6]), sb("mv", [P, 2, TPC, 2])
        vare, rstd = sb("vare", [P, 2, TPC]), sb("rstd", [P, 2, TPC])
        xh = sb("xh", [P, TPC, D])
        xTh, xTl = sb("xTh", [P, WIN + S], F16), sb("xTl", [P, WIN + S], F16)
        t1, t2, rot = sb("t1", [P, CH]), sb("t2", [P, CH]), sb("rot", [P, 2, CH])
        v32 = sb("v32", [P, 8, D])
        psX = ps("psX", [P, CH])
        psP = [ps(f"psP{i}", [P, CH]) for i in range(4)]
        psV = ps("psV", [P, 8, D])

        weights_loaded, const_loaded, x_first, x_loaded = sem("weights_loaded"), sem("const_loaded"), sem("x_first"), sem("x_loaded")
        weights_scaled, weights_hi, weights_lo = sem("weights_scaled"), sem("weights_hi"), sem("weights_lo")
        zeroed = sem("zeroed")
        bn_done, stats_ready, eps_added, rstd_ready = sem("bn"), sem("stats_ready"), sem("eps_added"), sem("rstd_ready")
        xhat_ready, xhat_transposed = sem("xhat_ready"), sem("xhat_transposed")
        xT_hi, xT_lo = sem("xT_hi"), sem("xT_lo")
        proj_done, v_done = sem("proj_done"), sem("v_done")
        cos_part, rope_parts, rotated = sem("cos_part"), sem("rope_parts"), sem("rotated")
        v_biased, v_hi, v_lo = sem("v_biased"), sem("v_hi"), sem("v_lo")

        xt = io["x"].rearrange("b (t p) d -> p (b t) d", p=P)
        chunks_of_batch = S // CH

        with st.block() as block:

            @block.sync
            def _(sp):
                for a, b, loaded in ((0, 2, x_first), (2, NCH // 2, x_loaded), (NCH // 2, NCH, x_loaded)):
                    sp.dma_start(X[:, a * TPC:b * TPC, :], xt[:, a * TPC:b * TPC, :]).then_inc(loaded, 16)
                late.load(sp, io)
                late.copy_masks(sp)
                stack(sp, (0, STACKED_FIRST), Q4, K4, qk, qk_hi, qk_lo, stacked, batch_stacked)

            @block.gpsimd
            def _(pool):
                pool.sem_inc(v_lo, 1)
                pool.sem_inc(qk_lo, 1)
                nc.gpsimd.memset(halfneg[:], -0.5).then_inc(zeroed, 1)
                nc.gpsimd.memset(epsc[:], EPS).then_inc(zeroed, 1)
                nc.gpsimd.memset(xTh[:, 0:WIN], 0.0).then_inc(zeroed, 1)
                nc.gpsimd.memset(xTl[:, 0:WIN], 0.0).then_inc(zeroed, 1)
                pool.wait_ge(zeroed, 2)

                def rstd_of(c, h):
                    pool.wait_ge(stats_ready, c + 1)
                    nc.gpsimd.tensor_tensor(vare[:, h], mv[:, h, :, 1], epsc[:], ALU.add).then_inc(eps_added, 1)
                    pool.wait_ge(eps_added, c + 1)
                    nc.gpsimd.tensor_tensor(rstd[:, h], vare[:, h], halfneg[:], ALU.pow).then_inc(rstd_ready, 1)

                def lows(b, h):
                    c = chunks_of_batch * b + h
                    for n, name in enumerate("qk"):
                        pool.wait_ge(qk_hi, 1 + 2 * c + n + 1)
                        nc.gpsimd.tensor_tensor(qk[name, "l"][:, ds(c * CH, CH)], rot[:, n, :],
                                                qk[name, "h"][:, ds(c * CH, CH)], ALU.subtract).then_inc(qk_lo, 1)
                    pool.wait_ge(v_hi, c + 1)
                    nc.gpsimd.tensor_tensor(
                        V[:, ds(c * 8, 8), 1, :, 0:DA], v32[:].rearrange("p w (h d) -> p w h d", d=DA),
                        V[:, ds(c * 8, 8), 0, :, 0:DA], ALU.subtract).then_inc(v_lo, 1)

                rstd_of(0, 0)
                rstd_of(1, 1)
                nc.gpsimd.memset(V[:, :, 0, :, DA], 1.0).then_inc(zeroed, 1)
                nc.gpsimd.memset(V[:, :, 1, :, DA], 0.0).then_inc(zeroed, 1)
                nc.gpsimd.memset(K4[:, :, 0:WIN], 0.0).then_inc(zeroed, 1)
                late.prepare(nc, pool)
                with pool.Fori(0, B - 1) as b:
                    for h in range(chunks_of_batch):
                        rstd_of(2 * b + h + 2, h)
                        lows(b, h)
                for h in range(chunks_of_batch):
                    lows(B - 1, h)

            @block.scalar
            def _(act):
                act.sem_inc(qk_hi, 1)
                act.dma_start(w32[:], io["wA"]).then_inc(weights_loaded, 16)
                act.dma_start(ident[:], io["ident"]).then_inc(weights_loaded, 16)
                act.dma_start(bias[:], io["biasA"]).then_inc(const_loaded, 16)
                act.dma_start(bvb[:], io["bv"].rearrange("(a n) -> a n", a=1).broadcast_to([P, D])).then_inc(const_loaded, 16)
                act.dma_start(cos[:], io["cos"]).then_inc(const_loaded, 16)
                act.dma_start(sin[:], io["sin"]).then_inc(const_loaded, 16)
                act.wait_ge(weights_loaded, 32)
                nc.scalar.activation(whi[:], w32[:], ACT.Copy).then_inc(weights_hi, 1)

                def xT_high(b, h):
                    c = chunks_of_batch * b + h
                    act.wait_ge(xhat_transposed, c + 1)
                    act.wait_ge(v_done, 1 + chunks_of_batch * b)
                    nc.scalar.activation(xTh[:, WIN + h * CH:WIN + (h + 1) * CH], psX[:], ACT.Copy).then_inc(xT_hi, 1)

                def chunk(b, h, last=False):
                    c = chunks_of_batch * b + h
                    if not last:
                        xT_high(b + h, 1 - h)
                    for n, name in enumerate("qk"):
                        act.wait_ge(rotated, 2 * c + n + 1)
                        nc.scalar.activation(qk[name, "h"][:, ds(c * CH, CH)], rot[:, n, :], ACT.Copy).then_inc(qk_hi, 1)
                    act.wait_ge(v_biased, 1 + c + 1)
                    nc.scalar.activation(V[:, ds(c * 8, 8), 0, :, 0:DA], v32[:].rearrange("p w (h d) -> p w h d", d=DA),
                                         ACT.Copy).then_inc(v_hi, 1)

                xT_high(0, 0)
                with act.Fori(0, B - 1) as b:
                    for h in range(chunks_of_batch):
                        chunk(b, h)
                chunk(B - 1, 0)
                chunk(B - 1, 1, last=True)

            @block.vector
            def _(dve):
                dve.sem_inc(v_biased, 1)
                dve.sem_inc(rope_parts, 2)
                def stats_of(c, h):
                    for j in range(TPC):
                        nc.vector.bn_stats(stats[:, h, j, :], X[:, TPC * c + j, :]).then_inc(bn_done, 1)
                    for j in range(TPC):
                        if j == 0:
                            dve.wait_ge(bn_done, TPC * c + TPC)
                            nc.vector.tensor_copy(seen[:], stats[:, h, TPC - 1, 0:1])
                        ins = nc.vector.bn_aggr(mv[:, h, j, :], stats[:, h, j, :])
                    ins.then_inc(stats_ready, 1)

                def normalise(c, h):
                    dve.wait_ge(rstd_ready, c + 1)
                    dve.wait_ge(xhat_transposed, c)
                    for j in range(TPC):
                        ins = nc.vector.tensor_scalar(xh[:, j, :], X[:, TPC * c + j, :], mv[:, h, j, 0:1],
                                                      rstd[:, h, j:j + 1], ALU.subtract, ALU.mult)
                    ins.then_inc(xhat_ready, 1)

                def xT_low(c, h):
                    dve.wait_ge(xT_hi, c + 1)
                    cols = slice(WIN + h * CH, WIN + (h + 1) * CH)
                    nc.vector.tensor_tensor(xTl[:, cols], psX[:], xTh[:, cols], ALU.subtract).then_inc(xT_lo, 1)

                def chunk(b, h, more):
                    c = chunks_of_batch * b + h
                    if more:
                        stats_of(c + 2, h)
                    if more or h == 0:
                        normalise(c + 1, 1 - h)
                    for n in range(2):
                        dve.wait_ge(proj_done, 4 * c + 2 * n + 1)
                        nc.vector.scalar_tensor_tensor(t1[:], psP[2 * n][:], bias[:, 2 * n:2 * n + 1],
                                                       cos[:, h * CH:(h + 1) * CH], ALU.add, ALU.mult).then_inc(cos_part, 1)
                        dve.wait_ge(proj_done, 4 * c + 2 * n + 2)
                        nc.vector.scalar_tensor_tensor(t2[:], psP[2 * n + 1][:], bias[:, 2 * n + 1:2 * n + 2],
                                                       sin[:, h * CH:(h + 1) * CH], ALU.add, ALU.mult).then_inc(rope_parts, 1)
                        dve.wait_ge(cos_part, 2 * c + n + 1)
                        dve.wait_ge(rope_parts, 2 + 2 * c + n + 1)
                        dve.wait_ge(qk_lo, 1 + 2 * c)
                        nc.vector.tensor_tensor(rot[:, n, :], t1[:], t2[:], ALU.add).then_inc(rotated, 1)
                        dve.wait_ge(rotated, 2 * c + n + 1)
                        if n == 0 and (more or h == 0):
                            xT_low(c + 1, 1 - h)
                    dve.wait_ge(v_done, 1 + c + 1)
                    dve.wait_ge(v_lo, 1 + c)
                    nc.vector.tensor_tensor(v32[:], psV[:], bvb[:, None, :].broadcast_to([P, 8, D]),
                                            ALU.add).then_inc(v_biased, 1)

                dve.wait_ge(x_first, 16)
                stats_of(0, 0)
                stats_of(1, 1)
                normalise(0, 0)
                dve.wait_ge(weights_hi, 1)
                nc.vector.tensor_tensor(wlo[:], w32[:], whi[:], ALU.subtract).then_inc(weights_lo, 1)
                dve.wait_ge(const_loaded, 64)
                dve.wait_ge(x_loaded, 2 * 16)
                xT_low(0, 0)
                with dve.Fori(0, B - 1) as b:
                    for h in range(chunks_of_batch):
                        chunk(b, h, True)
                for h in range(chunks_of_batch):
                    chunk(B - 1, h, False)

            @block.tensor
            def _(pe):
                pe.sem_inc(v_done, 1)
                def transposes(c):
                    pe.wait_ge(xhat_ready, c + 1)
                    pe.wait_ge(xT_lo, c)
                    for j in range(TPC):
                        ins = nc.tensor.transpose(psX[:, j * P:(j + 1) * P], xh[:, j, :], ident[:])
                    ins.then_inc(xhat_transposed, 1)

                def project(b, h, last=False):
                    c = chunks_of_batch * b + h
                    pe.wait_ge(xT_hi, c + 1)
                    pe.wait_ge(xT_lo, c + 1)
                    for i in range(4):
                        pe.wait_ge(rope_parts, 2 * c + i // 2 + 1)
                        cols = slice(WIN + h * CH, WIN + (h + 1) * CH)
                        nc.tensor.matmul(psP[i][:], whi[:, i, :], xTh[:, cols], start=True, stop=False)
                        nc.tensor.matmul(psP[i][:], whi[:, i, :], xTl[:, cols], start=False, stop=False)
                        nc.tensor.matmul(psP[i][:], wlo[:, i, :], xTh[:, cols], start=False, stop=True).then_inc(proj_done, 1)
                    pe.wait_ge(v_biased, 1 + c)
                    for w in range(8):
                        cols = slice((8 * h + w) * WIN, (8 * h + w) * WIN + P)
                        nc.tensor.matmul(psV[:, w, :], xTh[:, cols], whi[:, 4, :], start=True, stop=False)
                        nc.tensor.matmul(psV[:, w, :], xTl[:, cols], whi[:, 4, :], start=False, stop=False)
                        ins = nc.tensor.matmul(psV[:, w, :], xTh[:, cols], wlo[:, 4, :], start=False, stop=True)
                    ins.then_inc(v_done, 1)
                    if not last:
                        transposes(c + 1)

                pe.wait_ge(weights_loaded, 32)
                pe.wait_ge(weights_lo, 1)
                pe.wait_ge(zeroed, 4)
                transposes(0)
                with pe.Fori(0, B - 1) as b:
                    for h in range(chunks_of_batch):
                        project(b, h)
                project(B - 1, 0)
                project(B - 1, 1, last=True)


def band_attend(nc, X, Q4, K4, V, qk, qk_hi, qk_lo, stacked, batch_stacked, late):
    with Stage(nc, "a2") as st:
        sb, ps, sem = st.sb, st.ps, st.sem
        NP_ = HA // 2
        ident, identb, bandm, masks = late.ident, late.identb, late.bandm, late.masks
        headm, parm, fold, woh, wol, bob = late.headm, late.parm, late.fold, late.woh, late.wol, late.bob
        Qx = sb("Qx", [P, 2, HA, WIN], F16)
        mx, nb = sb("mx", [P, 2, NP_]), sb("nb", [P, 2, NP_])
        E = sb("E", [P, 2, NP_, P])
        Th, Tl = sb("Th", [P, 2, NP_, P], F16), sb("Tl", [P, 2, NP_, P], F16)
        Vn = sb("Vn", [P, 2, 2, HA * VW], F16)
        rd, rm = sb("rd", [P, NP_, 2]), sb("rm", [P, NP_, 2])
        On = sb("On", [P, 2, NP_ * 2, DA])
        oTh, oTl = sb("oTh", [P, P], F16), sb("oTl", [P, P], F16)
        psS = [[ps(f"psS{j}{a}", [P, 4, P]) for a in range(2)] for j in range(2)]
        psT = [ps(f"psT{a}", [P, 4, P]) for a in range(2)]
        psO = ps("psO", [P, 512])
        psY = ps("psY", [P, 512])
        pv = psO[:, 0:NP_ * 2 * VW].rearrange("p (m r w) -> p m r w", r=2, w=VW)

        q_masked = sem("q_masked")
        scores_done = sem("scores_done")
        max_done, bias_done, exps_done = sem("max_done"), sem("bias_done"), sem("exps_done")
        exp_transposed, T_hi, T_lo = sem("exp_transposed"), sem("T_hi"), sem("T_lo")
        v_copied, values_done = sem("v_copied"), sem("values_done")
        recip_done, recip_masked, normed = sem("recip_done"), sem("recip_masked"), sem("normed")
        folded, oT_hi, oT_lo, projected, bias_added, added = (
            sem("folded"), sem("oT_hi"), sem("oT_lo"), sem("projected"), sem("bias_added"), sem("added"))

        with st.block() as block:

            @block.sync
            def _(sp):
                stack(sp, (STACKED_FIRST, B), Q4, K4, qk, qk_hi, qk_lo, stacked, batch_stacked)

            @block.gpsimd
            def _(pool):
                def mask_q(n, j, first=False):
                    pool.wait_ge(batch_stacked, n // (S // WIN) + 1)
                    if not first:
                        pool.wait_ge(scores_done, 2 * n - 2)
                    nc.gpsimd.tensor_tensor(
                        Qx[:, j].rearrange("p (g h) q -> p g h q", h=4),
                        Q4[:, :, None, ds(WIN * n, WIN)].broadcast_to([P, 4, 4, WIN]),
                        headm[:, None, :, None].broadcast_to([P, 4, 4, WIN]), ALU.mult).then_inc(q_masked, 1)

                def add_bias(t):
                    nc.gpsimd.tensor_tensor(X[:, ds(t, 1), :], X[:, ds(t, 1), :], bob[:, None, :], ALU.add).then_inc(bias_added, 1)

                def copy_v(n, j, first=False):
                    if not first:
                        pool.wait_ge(values_done, n - 1)
                    nc.gpsimd.tensor_copy(Vn[:, j, None], V[:, ds(n, 1)].rearrange("p n c h w -> p n c (h w)")).then_inc(v_copied, 1)

                def tile(t, first=False):
                    for j in range(2):
                        mask_q(2 * t + j, j)
                        copy_v(2 * t + j - 2, j, first)
                    add_bias(t)

                mask_q(0, 0, True)
                mask_q(1, 1, True)
                add_bias(0)
                tile(1, first=True)
                with pool.Fori(2, NT) as t:
                    tile(t)
                for j in range(2):
                    copy_v(NB - 2 + j, j)

            @block.scalar
            def _(act):
                def exps(n, j, a):
                    act.wait_ge(bias_done, 2 * n + a + 1)
                    for p in range(4):
                        ins = nc.scalar.activation(E[:, j, 4 * a + p, :], psS[j][a][:, p, :], ACT.Exp,
                                                   bias=nb[:, j, 4 * a + p:4 * a + p + 1], scale=SCALE_A)
                    ins.then_inc(exps_done, 1)

                def T_high(n, j, a):
                    act.wait_ge(exp_transposed, 2 * n + a + 1)
                    nc.scalar.activation(Th[:, j, 4 * a:4 * a + 4, :], psT[a][:], ACT.Copy).then_inc(T_hi, 1)

                def o_high(t):
                    act.wait_ge(folded, t + 1)
                    nc.scalar.activation(oTh[:], psY[:, 0:P], ACT.Copy).then_inc(oT_hi, 1)

                def tile(t, first=False, second=False, last=False):
                    for j in range(2):
                        n = 2 * t + j
                        if not first:
                            act.wait_ge(values_done, n - 1)
                        for a in range(2):
                            T_high(n, j, a)
                            if a == 0 and j == 0 and not (first or second):
                                o_high(t - 2)
                            if not (last and j == 1):
                                exps(n + 1, 1 - j, a)

                for a in range(2):
                    exps(0, 0, a)
                tile(0, first=True)
                tile(1, second=True)
                with act.Fori(2, NT - 1) as t:
                    tile(t)
                tile(NT - 1, last=True)
                o_high(NT - 2)
                o_high(NT - 1)

            @block.vector
            def _(dve):
                dve.sem_inc(added, 1)
                def maximum(n, j, a):
                    dve.wait_ge(scores_done, 2 * n + a + 1)
                    nc.vector.tensor_reduce(mx[:, j, 4 * a:4 * a + 4], psS[j][a][:], AX_X, ALU.max).then_inc(max_done, 1)

                def exp_bias(n, j, a):
                    dve.wait_ge(max_done, 2 * n + a + 1)
                    nc.vector.tensor_scalar(nb[:, j, 4 * a:4 * a + 4], mx[:, j, 4 * a:4 * a + 4], -SCALE_A, None,
                                            ALU.mult).then_inc(bias_done, 1)

                def recip(n):
                    dve.wait_ge(values_done, n + 1)
                    nc.vector.reciprocal(rd[:], pv[:, :, :, DA]).then_inc(recip_done, 1)

                def mask_recip(n):
                    dve.wait_ge(recip_done, n + 1)
                    nc.vector.tensor_tensor(rm[:], rd[:], parm[:, None, :].broadcast_to([P, NP_, 2]),
                                            ALU.mult).then_inc(recip_masked, 1)

                def norm(n, j):
                    dve.wait_ge(recip_masked, n + 1)
                    nc.vector.tensor_tensor(
                        On[:, j].rearrange("p (m r) d -> p m r d", r=2), pv[:, :, :, 0:DA],
                        rm[:, :, :, None].broadcast_to([P, NP_, 2, DA]), ALU.mult).then_inc(normed, 1)

                def shift_and_norm(n, j, shift=True, first=False, normalise=True, after_fold=None):
                    if shift and not first:
                        dve.wait_ge(exps_done, 2 * n - 2)
                        dve.wait_ge(bias_done, 2 * n - 2)
                    if shift:
                        maximum(n, j, 0)
                    if normalise:
                        recip(n - 3)
                    if shift:
                        exp_bias(n, j, 0)
                    if normalise:
                        mask_recip(n - 3)
                    if shift:
                        maximum(n, j, 1)
                    if normalise:
                        if after_fold is not None:
                            dve.wait_ge(folded, after_fold)
                        norm(n - 3, 1 - j)
                    if shift:
                        exp_bias(n, j, 1)

                def add(t):
                    dve.wait_ge(bias_added, t + 1)
                    dve.wait_ge(projected, t + 1)
                    nc.vector.tensor_tensor(X[:, ds(t, 1), :], psY[:, None, P:2 * P], X[:, ds(t, 1), :], ALU.add).then_inc(added, 1)

                def split_o(t):
                    dve.wait_ge(oT_hi, t + 1)
                    nc.vector.tensor_tensor(oTl[:], psY[:, 0:P], oTh[:], ALU.subtract).then_inc(oT_lo, 1)

                def T_low(n, j, a):
                    dve.wait_ge(T_hi, 2 * n + a + 1)
                    nc.vector.tensor_tensor(Tl[:, j, 4 * a:4 * a + 4, :], psT[a][:], Th[:, j, 4 * a:4 * a + 4, :],
                                            ALU.subtract).then_inc(T_lo, 1)

                def tile(t, first=False, second=False, last=False):
                    for j in range(2):
                        n = 2 * t + j
                        shift_and_norm(n + 1, 1 - j, shift=not (last and j == 1), first=first and j == 0,
                                       normalise=not first, after_fold=None if first or second or j == 1 else t - 1)
                        if j == 1 and not (first or second):
                            add(t - 2)
                        T_low(n, j, 0)
                        if j == 0 and not (first or second):
                            split_o(t - 2)
                        T_low(n, j, 1)

                shift_and_norm(0, 0, first=True, normalise=False)
                tile(0, first=True)
                tile(1, second=True)
                with dve.Fori(2, NT - 1) as t:
                    tile(t)
                tile(NT - 1, last=True)
                shift_and_norm(NB + 1, 1, shift=False, after_fold=NT - 1)
                shift_and_norm(NB + 2, 0, shift=False)
                split_o(NT - 2)
                add(NT - 2)
                split_o(NT - 1)
                add(NT - 1)

            @block.tensor
            def _(pe):
                def scores(n, j, halves, first=False):
                    if 0 in halves:
                        pe.wait_ge(q_masked, n + 1)
                        if not first:
                            pe.wait_ge(exps_done, 2 * n - 2)
                    for a in halves:
                        m = masks[:, ds(n // 2, 1), :] if j == 0 else bandm[:, 1:2, :]
                        nc.tensor.matmul(psS[j][a][:], identb[:], m.broadcast_to([P, 4, P]), start=True, stop=False)
                        for p in range(4):
                            q = Qx[:, j, 8 * a + 2 * p:8 * a + 2 * p + 2, :]
                            ins = nc.tensor.matmul(psS[j][a][:, p, :], q, K4[:, 2 * a + p // 2, ds(WIN * n, P)],
                                                   start=False, stop=(p == 3))
                        ins.then_inc(scores_done, 1)

                def transposes(n, j, halves, first=False):
                    for a in halves:
                        pe.wait_ge(exps_done, 2 * n + a + 1)
                        if not first:
                            pe.wait_ge(T_lo, 2 * n - 1 + a)
                        for p in range(4):
                            ins = nc.tensor.transpose(psT[a][:, p, :], E[:, j, 4 * a + p, :], ident[:])
                        ins.then_inc(exp_transposed, 1)

                def values(n, j, first=False):
                    if not first:
                        pe.wait_ge(normed, n)
                    pe.wait_ge(v_copied, n + 1)
                    for a in range(2):
                        pe.wait_ge(T_lo, 2 * n + a + 1)
                        for p in range(4 * a, 4 * a + 4):
                            o = pv[:, p, :, :]
                            vh, vl = (Vn[:, j, part, 2 * p * VW:(2 * p + 2) * VW] for part in range(2))
                            nc.tensor.matmul(o, Th[:, j, p, :], vh, start=True, stop=False)
                            nc.tensor.matmul(o, Th[:, j, p, :], vl, start=False, stop=False)
                            ins = nc.tensor.matmul(o, Tl[:, j, p, :], vh, start=False, stop=True)
                    ins.then_inc(values_done, 1)

                def fold_o(t):
                    pe.wait_ge(normed, 2 * t + 2)
                    pe.wait_ge(added, 1 + t)
                    for j in range(2):
                        ins = nc.tensor.matmul(psY[:, 0:P], On[:, j], fold[:, j, :], start=(j == 0), stop=(j == 1))
                    ins.then_inc(folded, 1)

                def project(t):
                    pe.wait_ge(oT_lo, t + 1)
                    nc.tensor.matmul(psY[:, P:2 * P], oTh[:], woh[:], start=True, stop=False)
                    nc.tensor.matmul(psY[:, P:2 * P], oTh[:], wol[:], start=False, stop=False)
                    nc.tensor.matmul(psY[:, P:2 * P], oTl[:], woh[:], start=False, stop=True).then_inc(projected, 1)

                def tile(t, first=False, second=False, last=False):
                    for j in range(2):
                        n = 2 * t + j
                        for a in range(2):
                            if not (last and j == 1):
                                scores(n + 1, 1 - j, (a,), first and j == 0)
                            if a == 1 and j == 1 and not (first or second):
                                project(t - 2)
                            transposes(n, j, (a,), first and j == 0)
                        if not (first and j == 0):
                            values(n - 1, 1 - j, first)
                        if j == 1 and not first:
                            fold_o(t - 1)

                pe.wait_ge(late.prepared, late.PREPARED)
                pe.wait_ge(late.masked, late.MASKED)
                scores(0, 0, (0, 1), first=True)
                tile(0, first=True)
                tile(1, second=True)
                with pe.Fori(2, NT - 1) as t:
                    tile(t)
                tile(NT - 1, last=True)
                values(NB - 1, 1)
                project(NT - 2)
                fold_o(NT - 1)
                project(NT - 1)


def experts(nc, X, io, tag):
    with Stage(nc, tag) as outer:
        sb = outer.sb
        xnh, xnl = sb("xnh", [P, T], F16), sb("xnl", [P, T], F16)
        w1h, w1l = sb("w1h", [P, NE, FF], F16), sb("w1l", [P, NE, FF], F16)
        w2h, w2l = sb("w2h", [P, NE, FC, D], F16), sb("w2l", [P, NE, FC, D], F16)
        b1 = sb("b1", [P, NE, FC])
        K3, G3 = sb("K3", [3 * NE, D], F16), sb("G3", [P, NT, 3, NE], F16)
        Gs = sb("Gs", [P, NT, NE])
        identh = sb("identh", [P, P], F16)
        route(nc, X, xnh, xnl, w1h, w1l, w2h, w2l, b1, K3, G3, Gs, identh, io, tag + "r")
        mixture(nc, X, xnh, xnl, w1h, w1l, w2h, w2l, b1, K3, G3, Gs, identh, tag + "m")


def route(nc, X, xnh, xnl, w1h, w1l, w2h, w2l, b1, K3, G3, Gs, identh, io, tag):
    with Stage(nc, tag) as st:
        sb, ps, sem = st.sb, st.ps, st.sem
        PAIR = 2 * TPC
        w132, w232 = sb("w132", [P, NE * FF]), sb("w232", [P, NE * FF])
        ident = sb("ident", [P, P])
        K, K3c = sb("K", [P, NE]), sb("K3c", [P, 3, NE], F16)
        wr32, wrh, wrl = sb("wr32", [P, NE]), sb("wrh", [P, NE], F16), sb("wrl", [P, NE], F16)
        gamma, beta = sb("gamma", [P, 1]), sb("beta", [P, 1])
        brb = sb("brb", [P, NE])
        b2 = sb("b2", [P, NE])
        a32, ah, al = sb("a32", [P, NE, FC]), sb("ah", [P, NE, FC], F16), sb("al", [P, NE, FC], F16)
        ctot, csum = sb("ctot", [P, 1]), sb("csum", [P, NE])
        seen = sb("seen", [P, 1])
        halfneg, epsc = sb("halfneg", [P, PAIR]), sb("epsc", [P, PAIR])
        stats, mv = sb("stats", [P, 2, TPC, 6]), sb("mv", [P, NT, 2])
        mvc = sb("mvc", [P, 2, TPC, 2])
        vare, r1, vr, r2 = (sb(n, [P, NT]) for n in ("vare", "r1", "vr", "r2"))
        u = sb("u", [P, NT, D])
        xh = sb("xh", [P, 2, TPC, D])
        xn = sb("xn", [P, 2, CH])
        rank = sb("rank", [P, NE])
        L, eq, oh1, oh2, pr = (sb(n, [P, NT, NE]) for n in ("L", "eq", "oh1", "oh2", "pr"))
        m = sb("m", [P, 6, NT])
        psX = [ps(f"psX{h}", [P, CH]) for h in range(2)]
        psL = ps("psL", [P, 512])
        psK = ps("psK", [P, 512])
        lg = psL[:, 0:NT * NE].rearrange("p (t e) -> p t e", e=NE)

        loaded, w1_loaded, w2_loaded, set_up = sem("loaded"), sem("w1_loaded"), sem("w2_loaded"), sem("set_up")
        aggregated = sem("aggregated")
        w1_scaled, w1_hi, w1_lo, w2_hi, w2_lo = sem("w1_scaled"), sem("w1_hi"), sem("w1_lo"), sem("w2_hi"), sem("w2_lo")
        bn_done, stats_ready, r1_ready, r2_step, r2_ready = (
            sem(n) for n in ("bn_done", "stats_ready", "r1_ready", "r2_step", "r2_ready"))
        u_ready, u_added, xhat_ready, transposed = sem("u_ready"), sem("u_added"), sem("xhat_ready"), sem("transposed")
        xn_hi, xn_ready, xn_lo, logits_done = sem("xn_hi"), sem("xn_ready"), sem("xn_lo"), sem("logits_done")
        wr_hi, wr_lo = sem("wr_hi"), sem("wr_lo")
        b1_relu, b1_hi, b1_lo, k_done, k_step = sem("b1_relu"), sem("b1_hi"), sem("b1_lo"), sem("k_done"), sem("k_step")
        rt, exp_ready, gates_scaled = sem("router_step"), sem("exp_ready"), sem("gates_scaled")
        k_halves, k_turned, k_stored = sem("k_halves"), sem("k_turned"), sem("k_stored")

        with st.block() as block:

            @block.sync
            def _(sp):
                for dst, src in ((identh[:], io["identh"]), (ident[:], io["ident"]), (gamma[:], io["gammaF"]),
                                 (beta[:], io["betaF"]), (wr32[:], io["wrF"]), (b1[:], io["b1F"]), (b2[:], io["b2F"]),
                                 (rank[:], io["rank"]),
                                 (brb[:], io["brF"].rearrange("(a n) -> a n", a=1).broadcast_to([P, NE]))):
                    sp.dma_start(dst, src).then_inc(loaded, 16)
                sp.dma_start(w132[:], io["w1F"].rearrange("p e f -> p (e f)")).then_inc(w1_loaded, 16)
                sp.dma_start(w232[:], io["w2F"].rearrange("p e f d -> p (e f d)")).then_inc(w2_loaded, 16)

            LOADED = 9 * 16

            @block.gpsimd
            def _(pool):
                nc.gpsimd.memset(halfneg[:], -0.5).then_inc(set_up, 1)
                nc.gpsimd.memset(epsc[:], EPS).then_inc(set_up, 1)
                pool.wait_ge(set_up, 2)

                def scales(g):
                    G, tiles = nc.gpsimd, slice(g * PAIR, (g + 1) * PAIR)
                    pool.wait_ge(stats_ready, 2 * g + 2)
                    G.tensor_tensor(vare[:, tiles], mv[:, tiles, 1], epsc[:], ALU.add).then_inc(r2_step, 1)
                    pool.wait_ge(r2_step, 4 * g + 1)
                    G.tensor_tensor(r1[:, tiles], vare[:, tiles], halfneg[:], ALU.pow).then_inc(r1_ready, 1)
                    pool.wait_ge(r1_ready, g + 1)
                    G.tensor_tensor(vr[:, tiles], mv[:, tiles, 1], r1[:, tiles], ALU.mult).then_inc(r2_step, 1)
                    pool.wait_ge(r2_step, 4 * g + 2)
                    G.tensor_tensor(vr[:, tiles], vr[:, tiles], r1[:, tiles], ALU.mult).then_inc(r2_step, 1)
                    pool.wait_ge(r2_step, 4 * g + 3)
                    G.tensor_tensor(vr[:, tiles], vr[:, tiles], epsc[:], ALU.add).then_inc(r2_step, 1)
                    pool.wait_ge(r2_step, 4 * g + 4)
                    G.tensor_tensor(r2[:, tiles], vr[:, tiles], halfneg[:], ALU.pow).then_inc(r2_ready, 1)

                for g in range(NCH // 2):
                    scales(g)
                with pool.Fori(0, NCH) as c:
                    pool.wait_ge(u_ready, c + 1)
                    tiles = ds(TPC * c, TPC)
                    nc.gpsimd.tensor_tensor(X[:, tiles, :], X[:, tiles, :], u[:, tiles, :], ALU.add).then_inc(u_added, 1)
                for half in range(2):
                    pool.wait_ge(w1_scaled, half + 1)
                    pool.wait_ge(w1_hi, half + 1)
                    cols = slice(half * NE * FF // 2, (half + 1) * NE * FF // 2)
                    nc.gpsimd.tensor_tensor(w1l[:].rearrange("p e f -> p (e f)")[:, cols], w132[:, cols],
                                            w1h[:].rearrange("p e f -> p (e f)")[:, cols], ALU.subtract).then_inc(w1_lo, 1)

            @block.scalar
            def _(act):
                act.wait_ge(loaded, LOADED)
                nc.scalar.activation(wrh[:], wr32[:], ACT.Copy).then_inc(wr_hi, 1)
                nc.scalar.activation(a32[:], b1[:], ACT.Relu).then_inc(b1_relu, 1)
                act.wait_ge(b1_relu, 1)
                nc.scalar.activation(ah[:], a32[:], ACT.Copy).then_inc(b1_hi, 1)
                def normalise_u(c, h):
                    act.wait_ge(u_ready, c + 1)
                    for j in range(TPC):
                        ins = nc.scalar.activation(xh[:, h, j, :], u[:, TPC * c + j, :], ACT.Copy, scale=r2[:, ds(TPC * c + j, 1)])
                    ins.then_inc(xhat_ready, 1)

                def gain(c, h, first=False):
                    act.wait_ge(transposed, c + 1)
                    if not first:
                        act.wait_ge(xn_lo, 1 + c - 1)
                    nc.scalar.activation(xnh[:, ds(c * CH, CH)], psX[h][:], ACT.Identity,
                                         bias=beta[:], scale=gamma[:]).then_inc(xn_hi, 1)
                    nc.scalar.activation(xn[:, h], psX[h][:], ACT.Identity, bias=beta[:], scale=gamma[:]).then_inc(xn_ready, 1)

                def chunk(c, h):
                    act.wait_ge(transposed, c - 1)
                    normalise_u(c, h)
                    gain(c - 1, 1 - h)

                act.wait_ge(r2_ready, 1)
                normalise_u(0, 0)
                normalise_u(1, 1)
                gain(0, 0, first=True)
                act.wait_ge(r2_ready, 2)
                for h in range(2):
                    chunk(2 + h, h)
                act.wait_ge(w2_loaded, 16)
                nc.scalar.activation(w2h[:].rearrange("p e f d -> p (e f d)"), w232[:], ACT.Copy, scale=WS).then_inc(w2_hi, 1)
                with act.Fori(2, NCH // 2) as b:
                    act.wait_ge(r2_ready, b + 1)
                    for h in range(2):
                        chunk(2 * b + h, h)
                gain(NCH - 1, 1)
                act.wait_ge(w1_loaded, 16)
                for half in range(2):
                    cols = slice(half * NE * FF // 2, (half + 1) * NE * FF // 2)
                    nc.scalar.activation(w1h[:].rearrange("p e f -> p (e f)")[:, cols], w132[:, cols], ACT.Copy, scale=WS).then_inc(w1_hi, 1)
                    act.wait_ge(w1_hi, half + 1)
                    nc.scalar.activation(w132[:, cols], w132[:, cols], ACT.Copy, scale=WS).then_inc(w1_scaled, 1)
                    if half == 0:
                        act.wait_ge(rt, 3)
                        nc.scalar.activation(pr[:], L[:], ACT.Exp).then_inc(exp_ready, 1)

            @block.vector
            def _(dve):
                dve.sem_inc(xn_lo, 1)

                def stats_of(c, h):
                    for j in range(TPC):
                        nc.vector.bn_stats(stats[:, h, j, :], X[:, TPC * c + j, :]).then_inc(bn_done, 1)
                    dve.wait_ge(bn_done, TPC * c + TPC)
                    nc.vector.tensor_copy(seen[:], stats[:, h, TPC - 1, 0:1])
                    for j in range(TPC):
                        ins = nc.vector.bn_aggr(mvc[:, h, j, :], stats[:, h, j, :])
                    ins.then_inc(aggregated, 1)
                    dve.wait_ge(aggregated, c + 1)
                    nc.vector.tensor_copy(mv[:, ds(TPC * c, TPC), :], mvc[:, h]).then_inc(stats_ready, 1)

                def norm_x(c):
                    for j in range(TPC):
                        mean = mv[:, ds(TPC * c + j, 1), 0:1].rearrange("p t s -> p (t s)")
                        ins = nc.vector.tensor_scalar(u[:, TPC * c + j, :], X[:, TPC * c + j, :], mean,
                                                      r1[:, ds(TPC * c + j, 1)], ALU.subtract, ALU.mult)
                    ins.then_inc(u_ready, 1)

                def low(c, h):
                    dve.wait_ge(xn_ready, c + 1)
                    dve.wait_ge(xn_hi, c + 1)
                    nc.vector.tensor_tensor(xnl[:, ds(c * CH, CH)], xn[:, h], xnh[:, ds(c * CH, CH)], ALU.subtract).then_inc(xn_lo, 1)

                for c in range(4):
                    stats_of(c, c % 2)
                dve.wait_ge(r1_ready, 1)
                norm_x(0)
                norm_x(1)
                dve.wait_ge(loaded, LOADED)
                dve.wait_ge(wr_hi, 1)
                nc.vector.tensor_tensor(wrl[:], wr32[:], wrh[:], ALU.subtract).then_inc(wr_lo, 1)
                dve.wait_ge(b1_hi, 1)
                nc.vector.tensor_tensor(al[:], a32[:], ah[:], ALU.subtract).then_inc(b1_lo, 1)
                with dve.Fori(1, NCH // 2 - 1) as b:
                    for h in range(2):
                        stats_of(2 * b + 2 + h, h)
                    dve.wait_ge(r1_ready, b + 1)
                    for h in range(2):
                        norm_x(2 * b + h)
                    for h in range(2):
                        low(2 * b - 2 + h, h)
                dve.wait_ge(r1_ready, NCH // 2)
                norm_x(NCH - 2)
                norm_x(NCH - 1)
                dve.wait_ge(w2_hi, 1)

                def w2_low(half):
                    which, cols = slice(half * NE // 2, (half + 1) * NE // 2), slice(half * NE * FF // 2, (half + 1) * NE * FF // 2)
                    nc.vector.scalar_tensor_tensor(w2l[:, which].rearrange("p e f d -> p (e f d)"), w232[:, cols], WS,
                                                   w2h[:, which].rearrange("p e f d -> p (e f d)"), ALU.mult, ALU.subtract).then_inc(w2_lo, 1)

                low(NCH - 4, 0)
                w2_low(0)
                low(NCH - 3, 1)
                w2_low(1)
                low(NCH - 2, 0)
                low(NCH - 1, 1)

                step = [0]

                def then(ins, meanwhile=None):
                    step[0] += 1
                    ins.then_inc(rt, 1)
                    if meanwhile is not None:
                        meanwhile()
                    dve.wait_ge(rt, step[0])

                def k_sums():
                    dve.wait_ge(k_done, 1)
                    V.scalar_tensor_tensor(csum[:], b2[:], WS, psK[:, 0:NE], ALU.mult, ALU.add).then_inc(k_step, 1)

                def k_total():
                    dve.wait_ge(k_step, 1)
                    V.tensor_reduce(ctot[:], csum[:], AX_X, ALU.add).then_inc(k_step, 1)

                def k_of_expert():
                    dve.wait_ge(k_step, 2)
                    V.tensor_scalar(K[:], psK[:, 0:NE], -1.0, ctot[:], ALU.mult, ALU.add).then_inc(k_step, 1)

                def k_high():
                    dve.wait_ge(k_step, 3)
                    for i in (0, 1):
                        V.tensor_copy(K3c[:, i], K[:]).then_inc(k_step, 1)

                def k_low():
                    dve.wait_ge(k_step, 5)
                    V.tensor_tensor(K3c[:, 2], K[:], K3c[:, 0], ALU.subtract).then_inc(k_halves, 1)

                def k_store():
                    dve.wait_ge(k_turned, 1)
                    V.tensor_copy(K3[:], psK[0:3 * NE, 0:P]).then_inc(k_stored, 1)

                bc = lambda a: a[:, :, None].broadcast_to([P, NT, NE])
                rk = rank[:, None, :].broadcast_to([P, NT, NE])
                V = nc.vector
                dve.wait_ge(logits_done, NCH)
                then(V.tensor_tensor(L[:], lg, brb[:, None, :].broadcast_to([P, NT, NE]), ALU.add))
                then(V.tensor_reduce(m[:, 0], L[:], AX_X, ALU.max))
                then(V.tensor_tensor(L[:], L[:], bc(m[:, 0]), ALU.subtract))
                then(V.tensor_scalar(eq[:], L[:], 0.0, None, ALU.is_equal))
                then(V.tensor_tensor(eq[:], eq[:], rk, ALU.mult))
                then(V.tensor_reduce(m[:, 1], eq[:], AX_X, ALU.max))
                then(V.tensor_tensor(oh1[:], rk, bc(m[:, 1]), ALU.is_equal))
                then(V.scalar_tensor_tensor(oh2[:], oh1[:], -1e30, L[:], ALU.mult, ALU.add))
                then(V.tensor_reduce(m[:, 2], oh2[:], AX_X, ALU.max), k_sums)
                then(V.tensor_tensor(eq[:], oh2[:], bc(m[:, 2]), ALU.is_equal), k_total)
                then(V.tensor_tensor(eq[:], eq[:], rk, ALU.mult), k_of_expert)
                then(V.tensor_reduce(m[:, 3], eq[:], AX_X, ALU.max), k_high)
                then(V.tensor_tensor(oh2[:], rk, bc(m[:, 3]), ALU.is_equal), k_low)
                then(V.tensor_tensor(oh1[:], oh1[:], oh2[:], ALU.add))
                dve.wait_ge(exp_ready, 1)
                then(V.tensor_reduce(m[:, 4], pr[:], AX_X, ALU.add))
                then(V.reciprocal(m[:, 5], m[:, 4]), k_store)
                then(V.tensor_tensor(pr[:], pr[:], bc(m[:, 5]), ALU.mult))
                then(V.tensor_tensor(pr[:], pr[:], oh1[:], ALU.mult))
                V.tensor_scalar(Gs[:], pr[:], 1.0 / WS, None, ALU.mult).then_inc(gates_scaled, 1)
                V.tensor_copy(G3[:, :, 2], pr[:]).then_inc(gates_scaled, 1)
                then(V.tensor_copy(G3[:, :, 0], pr[:]))
                then(V.tensor_tensor(G3[:, :, 1], pr[:], G3[:, :, 0], ALU.subtract))
                dve.wait_ge(gates_scaled, 2)
                dve.wait_ge(k_stored, 1)

            @block.tensor
            def _(pe):
                def transposes(c, h):
                    pe.wait_ge(xhat_ready, c + 1)
                    for j in range(TPC):
                        ins = nc.tensor.transpose(psX[h][:, j * P:(j + 1) * P], xh[:, h, j, :], ident[:])
                    ins.then_inc(transposed, 1)

                def logits(c):
                    pe.wait_ge(xn_lo, 1 + c + 1)
                    for j in range(TPC):
                        t = TPC * c + j
                        o = psL[:, ds(t * NE, NE)]
                        nc.tensor.matmul(o, xnh[:, ds(t * P, P)], wrh[:], start=True, stop=False)
                        nc.tensor.matmul(o, xnh[:, ds(t * P, P)], wrl[:], start=False, stop=False)
                        ins = nc.tensor.matmul(o, xnl[:, ds(t * P, P)], wrh[:], start=False, stop=True)
                    ins.then_inc(logits_done, 1)

                pe.wait_ge(loaded, LOADED)
                transposes(0, 0)
                transposes(1, 1)
                pe.wait_ge(wr_lo, 1)
                with pe.Fori(1, NCH // 2) as b:
                    for h in range(2):
                        c = 2 * b + h
                        pe.wait_ge(xn_ready, c - 1)
                        transposes(c, h)
                        logits(c - 2)
                logits(NCH - 2)
                logits(NCH - 1)
                pe.wait_ge(w2_lo, 2)
                pe.wait_ge(b1_lo, 1)
                for e in range(NE):
                    for f in range(FC):
                        w, wl = w2h[:, e, f, :], w2l[:, e, f, :]
                        nc.tensor.matmul(psK[:, e:e + 1], w, ah[:, e, f:f + 1], start=(f == 0), stop=False)
                        nc.tensor.matmul(psK[:, e:e + 1], w, al[:, e, f:f + 1], start=False, stop=False)
                        ins = nc.tensor.matmul(psK[:, e:e + 1], wl, ah[:, e, f:f + 1], start=False, stop=(f == FC - 1))
                ins.then_inc(k_done, 1)
                pe.wait_ge(k_halves, 1)
                nc.tensor.matmul(psK[0:3 * NE, 0:P], K3c[:].rearrange("p a e -> p (a e)"), identh[:], start=True, stop=True).then_inc(k_turned, 1)


def mixture(nc, X, xnh, xnl, w1h, w1l, w2h, w2l, b1, K3, G3, Gs, identh, tag):
    with Stage(nc, tag) as st:
        sb, ps, sem = st.sb, st.ps, st.sem
        R = sb("R", [P, 2, FC, CH])
        Hh, Hl = sb("Hh", [P, 2, FC, CH], F16), sb("Hl", [P, 2, FC, CH], F16)
        GT = sb("GT", [3 * NE, CH], F16)
        ACT_HI = 2
        psZ = [ps(f"psZ{f}", [P, CH]) for f in range(FC)]
        psY = [ps(f"psY{j}", [P, TPC, D]) for j in range(2)]
        psG, psK = ps("psG", [P, CH]), ps("psK", [P, TPC, D])

        up_done, H_hi = sem("up_done"), sem("H_hi")
        relu_done = sem("relu_done")
        H_lo = sem("H_lo")
        down_done = sem("down_done")
        y_added = sem("y_added")
        gates_turned = sem("gates_turned")
        gates_stored = sem("gates_stored")
        k_done = sem("k_done")
        k_added = sem("k_added")

        with st.block() as block:

            @block.tensor
            def _(pe):
                pe.sem_inc(down_done, 2)
                pe.sem_inc(k_done, 1)

                def up(u, c, e):
                    for f in range(FC):
                        pe.wait_ge(relu_done, FC * u + f + 1)
                        x, xl = xnh[:, ds(c * CH, CH)], xnl[:, ds(c * CH, CH)]
                        w, wl = w1h[:, ds(e, 1), f * P:(f + 1) * P], w1l[:, ds(e, 1), f * P:(f + 1) * P]
                        nc.tensor.matmul(psZ[f][:], w, x, start=True, stop=False)
                        nc.tensor.matmul(psZ[f][:], w, xl, start=False, stop=False)
                        nc.tensor.matmul(psZ[f][:], wl, x, start=False, stop=True).then_inc(up_done, 1)

                def down(u, e, j):
                    pe.wait_ge(y_added, u + 1)
                    pe.wait_ge(H_lo, 2 * FC + FC * u + FC)
                    w = [(w2h[:, ds(e, 1), f, :], w2l[:, ds(e, 1), f, :]) for f in range(FC)]
                    for t in range(TPC):
                        tokens = slice(t * P, (t + 1) * P)
                        for f in range(FC):
                            h, hl = Hh[:, j, f, tokens], Hl[:, j, f, tokens]
                            nc.tensor.matmul(psY[j][:, t, :], h, w[f][0], start=(f == 0), stop=False)
                            nc.tensor.matmul(psY[j][:, t, :], h, w[f][1], start=False, stop=False)
                            ins = nc.tensor.matmul(psY[j][:, t, :], hl, w[f][0], start=False, stop=(f == FC - 1))
                    ins.then_inc(down_done, 1)

                def pair(c, ep, first=False):
                    for j in range(2):
                        if first and j == 1:
                            gated_k(c)
                        u = NE * c + 2 * ep + j
                        q = (NE // 2) * c + ep + j
                        up(u + 1, (q // (NE // 2)) % NCH, 2 * (q % (NE // 2)) + (1 - j))
                        down(u, 2 * ep + j, j)

                def turn_gates(c):
                    pe.wait_ge(gates_stored, c + 1)
                    for j in range(TPC):
                        ins = nc.tensor.matmul(psG[0:3 * NE, j * P:(j + 1) * P],
                                               G3[:, ds(TPC * c + j, 1)].rearrange("p t a e -> p (t a e)"), identh[:],
                                               start=True, stop=True)
                    ins.then_inc(gates_turned, 1)

                def gated_k(c):
                    pe.wait_ge(gates_stored, 1 + c + 1)
                    pe.wait_ge(k_added, c + 1)
                    for j in range(TPC):
                        ins = nc.tensor.matmul(psK[:, j, :], GT[:, j * P:(j + 1) * P], K3[:], start=True, stop=True)
                    ins.then_inc(k_done, 1)

                up(0, 0, 0)
                with pe.Fori(0, NCH) as c:
                    turn_gates(c)
                    pair(c, 0, first=True)
                    with pe.Fori(1, NE // 2) as ep:
                        pair(c, ep)

            @block.scalar
            def _(act):
                act.sem_inc(relu_done, FC)
                act.sem_inc(gates_stored, 1)

                def relu(u, e, j):
                    for f in range(FC):
                        act.wait_ge(up_done, FC * u + f + 1)
                        act.wait_ge(H_lo, FC * u + f + 1)
                        if f == FC - ACT_HI:
                            act.wait_ge(down_done, u + 1)
                        ins = nc.scalar.activation(R[:, j, f, :], psZ[f][:], ACT.Relu, bias=b1[:, ds(e, 1), f], scale=1.0 / WS)
                        if f >= FC - ACT_HI:
                            ins = nc.scalar.activation(Hh[:, j, f, :], psZ[f][:], ACT.Relu, bias=b1[:, ds(e, 1), f], scale=1.0 / WS)
                        ins.then_inc(relu_done, 1)

                relu(0, 0, 0)
                with act.Fori(0, NCH) as c:
                    act.wait_ge(gates_turned, c + 1)
                    act.wait_ge(k_done, c + 1)
                    nc.scalar.activation(GT[:], psG[0:3 * NE, :], ACT.Copy).then_inc(gates_stored, 1)
                    with act.Fori(0, NE // 2) as ep:
                        for j in range(2):
                            relu(NE * c + 2 * ep + j + 1, 2 * ((ep + j) % (NE // 2)) + (1 - j), 1 - j)

            @block.vector
            def _(dve):
                dve.sem_inc(H_lo, 2 * FC)
                dve.sem_inc(y_added, 2)
                dve.sem_inc(k_added, 1)

                def split(u, j):
                    dve.wait_ge(down_done, u + 1)
                    for f in range(FC):
                        dve.wait_ge(relu_done, FC + FC * u + f + 1)
                        if f < FC - ACT_HI:
                            nc.vector.tensor_copy(Hh[:, j, f, :], R[:, j, f, :]).then_inc(H_hi, 1)
                            dve.wait_ge(H_hi, (FC - ACT_HI) * u + f + 1)
                        nc.vector.tensor_tensor(Hl[:, j, f, :], R[:, j, f, :], Hh[:, j, f, :], ALU.subtract).then_inc(H_lo, 1)

                def gate(c, u, e, j):
                    dve.wait_ge(down_done, 2 + u + 1)
                    dve.wait_ge(y_added, 2 + u)
                    for t in range(TPC):
                        ins = nc.vector.scalar_tensor_tensor(X[:, ds(TPC * c + t, 1), :], psY[j][:, t:t + 1, :],
                                                             Gs[:, ds(TPC * c + t, 1), ds(e, 1)].rearrange("p t e -> p (t e)"),
                                                             X[:, ds(TPC * c + t, 1), :], ALU.mult, ALU.add)
                    ins.then_inc(y_added, 1)

                def pair(c, ep, first=False):
                    for j in range(2):
                        u = NE * c + 2 * ep + j
                        split(u + 1, 1 - j)
                        if first and j == 1:
                            add_k(c)
                        gate(c, u, 2 * ep + j, j)

                def add_k(c):
                    dve.wait_ge(k_done, 1 + c + 1)
                    dve.wait_ge(y_added, 2 + NE * c + 1)
                    nc.vector.scalar_tensor_tensor(X[:, ds(TPC * c, TPC), :], psK[:], 1.0 / WS, X[:, ds(TPC * c, TPC), :],
                                                   ALU.mult, ALU.add).then_inc(k_added, 1)
                    dve.wait_ge(k_added, 1 + c + 1)

                split(0, 0)
                with dve.Fori(0, NCH) as c:
                    pair(c, 0, first=True)
                    with dve.Fori(1, NE // 2) as ep:
                        pair(c, ep)


def full_attention(nc, X, io):
    with Stage(nc, "full") as st:
        sb = st.sb
        woh, wol = sb("woh", [P, HB // 2, D], F16), sb("wol", [P, HB // 2, D], F16)
        OTh, OTl = sb("OTh", [P, HB // 2, T], F16), sb("OTl", [P, HB // 2, T], F16)
        bob, gb, bb = sb("bob", [P, D]), sb("gb", [P, D]), sb("bb", [P, D])
        consts_loaded = st.sem("consts_loaded")
        with Stage(nc, "fullw") as st2:
            sb = st2.sb
            wTh, wTl = sb("wTh", [P, T], F16), sb("wTl", [P, T], F16)
            wq = sb("wqh", [P, HB, P], F16), sb("wql", [P, HB, P], F16)
            wk = sb("wkh", [P, HB, P], F16), sb("wkl", [P, HB, P], F16)
            wv = sb("wvh", [P, HB, DB], F16), sb("wvl", [P, HB, DB], F16)
            consts = (sb("identh", [P, P], F16), sb("bq", [P, 2 * HB]), sb("bk", [P, 2 * HB]), sb("bvb", [P, HB, DB]))
            full_prepare(nc, X, wTh, wTl, wq, wk, wv, (woh, wol), consts, (bob, gb, bb), consts_loaded, io)
            full_heads(nc, wTh, wTl, wq, wk, wv, OTh, OTl, consts, consts_loaded)
        full_output(nc, X, OTh, OTl, woh, wol, bob, gb, bb, consts_loaded)


CONSTS_LOADED = 9 * 16


def full_prepare(nc, X, wTh, wTl, wq, wk, wv, wo, consts, out_consts, consts_loaded, io):
    with Stage(nc, "bp") as st:
        sb, ps, sem = st.sb, st.ps, st.sem
        names = [("wqB", wq, HB * P), ("wkB", wk, HB * P), ("wvB", wv, HB * DB), ("woutB", wo, HB // 2 * D)]
        w32 = [sb(n, [P, size]) for n, _, size in names]
        ident = sb("ident", [P, P])
        seen = sb("seen", [P, 1])
        halfneg, epsc = sb("halfneg", [P, TPC]), sb("epsc", [P, TPC])
        stats, mv = sb("stats", [P, 2, TPC, 6]), sb("mv", [P, 2, TPC, 2])
        vare, rstd = sb("vare", [P, 2, TPC]), sb("rstd", [P, 2, TPC])
        w = sb("w", [P, 2, TPC, D])
        psX = [ps(f"psX{h}", [P, CH]) for h in range(2)]

        ident_loaded, loaded, set_up = sem("ident_loaded"), sem("loaded"), sem("set_up")
        w_hi, qk_lo, w_lo = sem("w_hi"), sem("qk_lo"), sem("w_lo")
        bn_done, stats_ready, eps_added, rstd_ready = sem("bn_done"), sem("stats_ready"), sem("eps_added"), sem("rstd_ready")
        w_ready, transposed, wT_hi, wT_lo, added = sem("w_ready"), sem("transposed"), sem("wT_hi"), sem("wT_lo"), sem("added")
        LOADED = 4 * 16
        identh, bq, bk, bvb = consts

        with st.block() as block:

            @block.sync
            def _(sp):
                sp.dma_start(ident[:], io["ident"]).then_inc(ident_loaded, 16)
                for (n, _, _), dst in zip(names, w32):
                    src = io[n]
                    if n == "wvB":
                        sp.dma_start(dst[:], src).then_inc(loaded, 16)
                    else:
                        sp.dma_start(dst[:], src.rearrange("p a b -> p (a b)")).then_inc(loaded, 16)
                sp.dma_start(identh[:], io["identh"]).then_inc(consts_loaded, 16)
                for a in range(2):
                    sp.dma_start(bq[:, a * HB:(a + 1) * HB], io["bqB"]).then_inc(consts_loaded, 16)
                    sp.dma_start(bk[:, a * HB:(a + 1) * HB], io["bkB"]).then_inc(consts_loaded, 16)
                sp.dma_start(bvb[:].rearrange("p a b -> p (a b)"),
                             io["bvB"].rearrange("(a n) -> a n", a=1).broadcast_to([P, HB * DB])).then_inc(consts_loaded, 16)
                for dst, n in zip(out_consts, ("boutB", "lngB", "lnbB")):
                    sp.dma_start(dst[:], io[n].rearrange("(a n) -> a n", a=1).broadcast_to([P, D])).then_inc(consts_loaded, 16)

            @block.gpsimd
            def _(pool):
                nc.gpsimd.memset(halfneg[:], -0.5).then_inc(set_up, 1)
                nc.gpsimd.memset(epsc[:], EPS).then_inc(set_up, 1)
                pool.wait_ge(set_up, 2)
                with pool.Fori(0, NCH // 2) as b:
                    for h in range(2):
                        c = 2 * b + h
                        pool.wait_ge(stats_ready, c + 1)
                        nc.gpsimd.tensor_tensor(vare[:, h], mv[:, h, :, 1], epsc[:], ALU.add).then_inc(eps_added, 1)
                        pool.wait_ge(eps_added, c + 1)
                        nc.gpsimd.tensor_tensor(rstd[:, h], vare[:, h], halfneg[:], ALU.pow).then_inc(rstd_ready, 1)
                for i, (_, (hi, lo), _) in enumerate(names[:2]):
                    pool.wait_ge(w_hi, i + 1)
                    nc.gpsimd.tensor_tensor(lo[:].rearrange("p a b -> p (a b)"), w32[i][:],
                                            hi[:].rearrange("p a b -> p (a b)"), ALU.subtract).then_inc(qk_lo, 1)

            @block.scalar
            def _(act):
                def wT_high(c, h):
                    act.wait_ge(transposed, c + 1)
                    nc.scalar.activation(wTh[:, ds(c * CH, CH)], psX[h][:], ACT.Copy).then_inc(wT_hi, 1)

                for h in range(2):
                    wT_high(h, h)
                act.wait_ge(loaded, LOADED)
                for i, (_, (hi, _), _) in enumerate(names):
                    nc.scalar.activation(hi[:].rearrange("p a b -> p (a b)"), w32[i][:], ACT.Copy).then_inc(w_hi, 1)
                with act.Fori(1, NCH // 2) as b:
                    for h in range(2):
                        wT_high(2 * b + h, h)

            @block.vector
            def _(dve):
                dve.sem_inc(wT_lo, 1)
                def stats_of(c, h):
                    for j in range(TPC):
                        nc.vector.bn_stats(stats[:, h, j, :], X[:, TPC * c + j, :]).then_inc(bn_done, 1)
                    dve.wait_ge(bn_done, TPC * c + TPC)
                    nc.vector.tensor_copy(seen[:], stats[:, h, TPC - 1, 0:1])
                    for j in range(TPC):
                        ins = nc.vector.bn_aggr(mv[:, h, j, :], stats[:, h, j, :])
                    ins.then_inc(stats_ready, 1)

                def normalise(c, h):
                    dve.wait_ge(rstd_ready, c + 1)
                    for j in range(TPC):
                        ins = nc.vector.tensor_scalar(w[:, h, j, :], X[:, TPC * c + j, :], mv[:, h, j, 0:1],
                                                      rstd[:, h, j:j + 1], ALU.subtract, ALU.mult)
                    ins.then_inc(w_ready, 1)

                def chunk(c, h, more):
                    if more:
                        stats_of(c + 2, h)
                    dve.wait_ge(w_ready, c + 1)
                    nc.vector.scalar_tensor_tensor(
                        X[:, ds(TPC * c, TPC), :], w[:, h], RSQRT2, X[:, ds(TPC * c, TPC), :],
                        ALU.mult, ALU.add).then_inc(added, 1)
                    if more or h == 0:
                        normalise(c + 1, 1 - h)
                    dve.wait_ge(wT_hi, c + 1)
                    nc.vector.tensor_tensor(wTl[:, ds(c * CH, CH)], psX[h][:], wTh[:, ds(c * CH, CH)], ALU.subtract).then_inc(wT_lo, 1)

                stats_of(0, 0)
                stats_of(1, 1)
                normalise(0, 0)
                with dve.Fori(0, NCH // 2 - 1) as b:
                    for h in range(2):
                        chunk(2 * b + h, h, True)
                for h in range(2):
                    chunk(NCH - 2 + h, h, False)
                for i, (_, (hi, lo), _) in enumerate(names[2:]):
                    dve.wait_ge(w_hi, 2 + i + 1)
                    nc.vector.tensor_tensor(lo[:].rearrange("p a b -> p (a b)"), w32[2 + i][:],
                                            hi[:].rearrange("p a b -> p (a b)"), ALU.subtract).then_inc(w_lo, 1)

            @block.tensor
            def _(pe):
                pe.wait_ge(ident_loaded, 16)
                with pe.Fori(0, NCH // 2) as b:
                    for h in range(2):
                        pe.wait_ge(w_ready, 2 * b + h + 1)
                        pe.wait_ge(wT_lo, 1 + 2 * b)
                        for j in range(TPC):
                            ins = nc.tensor.transpose(psX[h][:, j * P:(j + 1) * P], w[:, h, j, :], ident[:])
                        ins.then_inc(transposed, 1)


def full_heads(nc, wTh, wTl, wq, wk, wv, OTh, OTl, consts, consts_loaded):
    with Stage(nc, "bh") as st:
        sb, ps, sem = st.sb, st.ps, st.sem
        HALF = S // 2
        U = B * HB
        MROW = DB
        MROW2 = 96
        SUMS = KT - 1
        identh, bq, bk, bvb = consts
        ones = sb("ones", [P, DB])
        KH = sb("KH", [P, 2, S], F16)
        K1 = sb("K1", [P, 2, S], F16)
        QH = sb("QH", [P, 2, S], F16)
        QL = sb("QL", [P, 2, S], F16)
        Vb = sb("Vb", [P, 2 * KT, HB, DB])
        V = sb("V", [P, 2, KT, DB])
        Mx = sb("Mx", [P, KT, 2])
        Mn, Ml = sb("Mn", [P, KT]), sb("Ml", [P, KT, 2], F16)
        E = sb("E", [P, KT, S])
        Es = sb("Es", [P, S])
        rden = sb("rden", [P, HALF])
        O = sb("O", [P, S])
        psA = ps("psA", [P, 2, HALF])
        psS = [ps(f"psS{i}", [P, 2, HALF]) for i in range(2)]
        psO = [ps(f"psO{i}", [P, HALF]) for i in range(2)]

        first_v = [psS[i][:, a] for i in range(2) for a in range(2)]

        set_up = sem("set_up")
        k_done, v_done, q_done = sem("k_done"), sem("v_done"), sem("q_done")
        k_hi, k_split, k_copied, v_biased, v_copied, q_hi, q_split = (
            sem(n) for n in ("k_hi", "k_split", "k_copied", "v_biased", "v_copied", "q_hi", "q_split"))
        rows_done, max_done, max_hi, max_split, max_row_done, max_row = (
            sem("rows_done"), sem("max_done"), sem("max_hi"), sem("max_split"), sem("max_row_done"), sem("max_row"))
        scores_done = sem("scores_done")
        exp_done = sem("exp_done")
        value_done = sem("value_done")
        summed = sem("summed")
        den_done = sem("den_done")
        recip_done = sem("recip_done")
        normed = sem("normed")
        o_hi = sem("o_hi")
        o_lo = sem("o_lo")
        half_normed = sem("half_normed")

        batch = lambda u: u // HB
        head = lambda u: u % HB

        row_bank = lambda s, i: (psO[s][:], psA[:, 1], psA[:, 0])[i % 3]

        def add_tile(eng, engine, u, t):
            eng.wait_ge(exp_done, 2 + KT * u + t + 1)
            if t == 1:
                eng.wait_ge(den_done, 1 + u)
                engine.tensor_tensor(Es[:], E[:, 0, :], E[:, 1, :], ALU.add).then_inc(summed, 1)
            else:
                eng.wait_ge(summed, SUMS * (u + 1) + t - 1)
                engine.tensor_tensor(Es[:], Es[:], E[:, t, :], ALU.add).then_inc(summed, 1)

        with st.block() as block:

            @block.tensor
            def _(pe):
                pe.sem_inc(den_done, 1)
                def three(out, a, b, first=True, last=True):
                    nc.tensor.matmul(out, a[0], b[0], start=first, stop=False)
                    nc.tensor.matmul(out, a[0], b[1], start=False, stop=False)
                    return nc.tensor.matmul(out, a[1], b[0], start=False, stop=last)

                def tokens(u, at, n):
                    return wTh[:, ds(batch(u) * S + at, n)], wTl[:, ds(batch(u) * S + at, n)]

                def make_k(u, a):
                    three(psA[:, 1 - a], [x[:, ds(head(u), 1), :] for x in wk], tokens(u, a * HALF, HALF)).then_inc(k_done, 1)

                def make_v(i, out=psA[:, 1]):
                    token = [x[:, ds(i * P, P)] for x in (wTh, wTl)]
                    three(out, token, [x[:].rearrange("p a b -> p (a b)") for x in wv]).then_inc(v_done, 1)

                def make_q(u, a, first=False):
                    if a == 0:
                        pe.wait_ge(v_biased, KT + u)
                        if first:
                            pe.wait_ge(k_split, 2 * u + 1)
                    elif first:
                        pe.wait_ge(k_split, 2 * u + 2)
                    else:
                        pe.wait_ge(recip_done, u - 1)
                    three(psA[:, 1 - a], [x[:, ds(head(u), 1), :] for x in wq], tokens(u, a * HALF, HALF)).then_inc(q_done, 1)

                def rows(u, s, i):
                    t, a = i // 2, i % 2
                    if i == 0:
                        pe.wait_ge(q_hi, 2 * u + 1)
                        pe.wait_ge(normed, u + 1)
                    elif i < 3:
                        pe.wait_ge(q_split, 2 * u + i)
                    else:
                        pe.wait_ge(max_done, 2 * KT * u + i - 2)
                    nc.tensor.matmul(row_bank(s, i), QH[:, s, t * P:(t + 1) * P], KH[:, s, a * HALF:(a + 1) * HALF],
                                     start=True, stop=True).then_inc(rows_done, 1)

                def max_rows(u):
                    pe.wait_ge(max_split, u + 1)
                    for t in range(KT):
                        at = MROW if t < KT // 2 else MROW2
                        ins = nc.tensor.matmul(psA[at:at + 2, 0, t % 4 * P:(t % 4 + 1) * P], Ml[:, t, :], identh[:],
                                               start=True, stop=True)
                    ins.then_inc(max_row_done, 1)

                def scores(u, s, t, halves=(0, 1)):
                    if 0 in halves:
                        pe.wait_ge(exp_done, KT * u + t + 1)
                        if t == 0:
                            pe.wait_ge(k_copied, u + 1)
                            pe.wait_ge(max_row, 2 * u + 2)
                    keys = slice(t * P, (t + 1) * P)
                    for a in halves:
                        q = slice(a * HALF, (a + 1) * HALF)
                        nc.tensor.matmul(psS[t % 2][:, a], KH[:, s, keys], QH[:, s, q], start=True, stop=False)
                        ins = nc.tensor.matmul(psS[t % 2][:, a], K1[:, s, keys], QL[:, s, q], start=False, stop=True)
                    if 1 in halves:
                        ins.then_inc(scores_done, 1)

                def values(u, s, t):
                    pe.wait_ge(exp_done, 2 + KT * u + t + 1)
                    if t == 0:
                        pe.wait_ge(normed, u + 1)
                        pe.wait_ge(v_copied, u + 1)
                    for a in range(2):
                        ins = nc.tensor.matmul(psO[s][DB * a:DB * (a + 1), :], V[:, s, t, :], E[:, t, a * HALF:(a + 1) * HALF],
                                               start=(t == 0), stop=(t == KT - 1))
                    ins.then_inc(value_done, 1)

                def denominators(u):
                    pe.wait_ge(summed, SUMS * (u + 2))
                    for a in range(2):
                        ins = nc.tensor.matmul(psA[DB * a:DB * (a + 1), 0], ones[:], Es[:, a * HALF:(a + 1) * HALF],
                                               start=True, stop=True)
                    ins.then_inc(den_done, 1)

                def next_k(u, a, done, value):
                    pe.wait_ge(done, value)
                    make_k(u, a)

                def unit(u, s, first=False, more=2):
                    n, o = u + 1, 1 - s
                    if more:
                        make_q(n, 0)
                    if not first:
                        if more:
                            pe.wait_ge(k_split, 2 * n + 2)
                        denominators(u - 1)
                    scores(u, s, 1)
                    values(u, s, 0)
                    scores(u, s, 2)
                    values(u, s, 1)
                    scores(u, s, 3)
                    if more:
                        make_q(n, 1, first)
                    values(u, s, 2)
                    for t in range(4, KT):
                        if more:
                            rows(n, o, 4 * t - 16)
                        scores(u, s, t, (0,))
                        if more:
                            rows(n, o, 4 * t - 15)
                        scores(u, s, t, (1,))
                        if more:
                            rows(n, o, 4 * t - 14)
                        values(u, s, t - 1)
                        if more:
                            rows(n, o, 4 * t - 13)
                    if more == 2:
                        next_k(n + 1, 0, max_done, 2 * KT * (n + 1) - 2)
                    if more:
                        max_rows(n)
                    values(u, s, 7)
                    if more == 2:
                        pe.wait_ge(k_split, 2 * n + 3)
                        make_v((KT + 1 + u) % NT)
                        next_k(n + 1, 1, max_row, 2 * n + 2)
                    if more:
                        scores(n, o, 0)

                make_k(0, 0)
                make_k(0, 1)
                for t in range(KT):
                    if t >= len(first_v):
                        pe.wait_ge(v_biased, t - len(first_v) + 1)
                    make_v(t, first_v[t % len(first_v)])
                make_q(0, 0)
                make_q(0, 1, first=True)
                for i in range(2 * KT):
                    rows(0, 0, i)
                pe.wait_ge(consts_loaded, CONSTS_LOADED)
                next_k(1, 0, max_done, 2 * KT - 2)
                max_rows(0)
                pe.wait_ge(k_split, 3)
                make_v(KT)
                next_k(1, 1, max_row, 2)
                pe.wait_ge(set_up, 4)
                scores(0, 0, 0)
                unit(0, 0, first=True)
                unit(1, 1)
                with pe.Fori(1, U // 2 - 1) as pr:
                    for s in range(2):
                        unit(2 * pr + s, s)
                unit(U - 2, 0, more=1)
                unit(U - 1, 1, more=0)
                pe.wait_ge(recip_done, U - 1)
                denominators(U - 1)

            @block.scalar
            def _(act):
                act.sem_inc(exp_done, 2)

                def hi(u, s, a, dst, bias, done, signal):
                    act.wait_ge(done, 2 * u + a + 1)
                    nc.scalar.activation(dst[:, s, a * HALF:(a + 1) * HALF], psA[:, 1 - a], ACT.Identity,
                                         bias=bias[:, ds(a * HB + head(u), 1)]).then_inc(signal, 1)

                def row(u, s):
                    act.wait_ge(max_row_done, u + 1)
                    for a, at in enumerate((MROW, MROW2)):
                        nc.scalar.activation(QL[MROW:MROW + 2, s, a * HALF:(a + 1) * HALF], psA[at:at + 2, 0],
                                             ACT.Copy).then_inc(max_row, 1)

                def exp(u, s, t):
                    act.wait_ge(scores_done, KT * u + t + 1)
                    act.wait_ge(value_done, KT * u + t + 1)
                    act.wait_ge(summed, SUMS * u + max(t, 1))
                    nc.scalar.activation(E[:, t, :], psS[t % 2][:].rearrange("p a q -> p (a q)"), ACT.Exp,
                                         scale=SCALE_B).then_inc(exp_done, 1)

                def out_hi(u, s):
                    act.wait_ge(half_normed, 2 * u + 2)
                    rows_ = slice(DB * s, DB * (s + 1))
                    nc.scalar.activation(OTh[rows_, ds(head(u) // 2, 1), ds(batch(u) * S, S)], O[rows_, None, :],
                                         ACT.Copy).then_inc(o_hi, 1)

                def copy_v(u, s):
                    act.wait_ge(v_biased, KT * (batch(u) + 1))
                    act.wait_ge(value_done, KT * u)
                    nc.scalar.activation(V[:, s], Vb[:, ds(batch(u) % 2 * KT, KT), ds(head(u), 1), :], ACT.Copy).then_inc(v_copied, 1)

                def unit(u, s, first=False, more=2):
                    n, o = u + 1, 1 - s
                    exp(u, s, 0)
                    if more:
                        hi(n, o, 0, QH, bq, q_done, q_hi)
                    exp(u, s, 1)
                    exp(u, s, 2)
                    exp(u, s, 3)
                    if more:
                        hi(n, o, 1, QH, bq, q_done, q_hi)
                    exp(u, s, 4)
                    if not first:
                        out_hi(u - 1, o)
                    exp(u, s, 5)
                    if more:
                        copy_v(n, o)
                    exp(u, s, 6)
                    exp(u, s, 7)
                    if more == 2:
                        hi(n + 1, s, 0, KH, bk, k_done, k_hi)
                    if more:
                        row(n, o)
                    if more == 2:
                        hi(n + 1, s, 1, KH, bk, k_done, k_hi)

                act.wait_ge(consts_loaded, CONSTS_LOADED)
                for dst, bias, done, signal in ((KH, bk, k_done, k_hi), (QH, bq, q_done, q_hi)):
                    for a in range(2):
                        hi(0, 0, a, dst, bias, done, signal)
                copy_v(0, 0)
                act.wait_ge(set_up, 4)
                hi(1, 1, 0, KH, bk, k_done, k_hi)
                row(0, 0)
                hi(1, 1, 1, KH, bk, k_done, k_hi)
                unit(0, 0, first=True)
                unit(1, 1)
                with act.Fori(1, U // 2 - 1) as pr:
                    for s in range(2):
                        unit(2 * pr + s, s)
                unit(U - 2, 0, more=1)
                unit(U - 1, 1, more=0)
                out_hi(U - 1, 1)

            @block.vector
            def _(dve):
                dve.sem_inc(normed, 2)
                flat = lambda x: x.rearrange("p a q -> p (a q)")

                def k_low(u, s, a):
                    dve.wait_ge(k_hi, 2 * u + a + 1)
                    q = slice(a * HALF, (a + 1) * HALF)
                    nc.vector.scalar_tensor_tensor(KH[DB:P, s, q], psA[DB:P, 1 - a], bk[DB:P, ds(head(u), 1)], KH[DB:P, s, q],
                                                   ALU.add, ALU.subtract).then_inc(k_split, 1)

                def k_copy(u, s):
                    nc.vector.tensor_copy(K1[0:DB, s, :], KH[0:DB, s, :]).then_inc(k_copied, 1)

                def v_bias(i, src=psA[:, 1]):
                    dve.wait_ge(v_done, i + 1)
                    nc.vector.tensor_tensor(Vb[:, ds(i % (2 * KT), 1)], src.rearrange("p (h d) -> p h d", d=DB)[:, None],
                                            bvb[:, None], ALU.add).then_inc(v_biased, 1)

                def q_low(u, s, a):
                    dve.wait_ge(q_hi, 2 * u + a + 1)
                    q = slice(a * HALF, (a + 1) * HALF)
                    nc.vector.scalar_tensor_tensor(QL[0:DB, s, q], psA[0:DB, 1 - a], bq[0:DB, ds(head(u), 1)], QH[0:DB, s, q],
                                                   ALU.add, ALU.subtract).then_inc(q_split, 1)

                def row_max(u, s, i):
                    dve.wait_ge(rows_done, 2 * KT * u + i + 1)
                    nc.vector.tensor_reduce(Mx[:, i // 2, i % 2:i % 2 + 1], row_bank(s, i), AX_X, ALU.max).then_inc(max_done, 1)

                def max_halves(u):
                    dve.wait_ge(max_done, 2 * KT * (u + 1))
                    nc.vector.tensor_reduce(Mn[:], Mx[:], AX_X, ALU.max, negate=True).then_inc(max_hi, 1)
                    nc.vector.tensor_reduce(Ml[:, :, 0], Mx[:], AX_X, ALU.max, negate=True).then_inc(max_hi, 1)
                    dve.wait_ge(max_hi, 2 * u + 2)
                    nc.vector.tensor_tensor(Ml[:, :, 1], Mn[:], Ml[:, :, 0], ALU.subtract).then_inc(max_split, 1)

                def norm(u, s):
                    dve.wait_ge(den_done, 1 + u + 1)
                    nc.vector.reciprocal(rden[:], psA[:, 0]).then_inc(recip_done, 1)
                    dve.wait_ge(recip_done, u + 1)
                    dve.wait_ge(value_done, KT + KT * u + KT)
                    dve.wait_ge(o_lo, u + 1)
                    for a in range(2):
                        src = slice(DB * a, DB * (a + 1))
                        nc.vector.tensor_tensor(O[DB * s:DB * (s + 1), a * HALF:(a + 1) * HALF], psO[s][src, :], rden[src, :],
                                                ALU.mult).then_inc(half_normed, 1)
                    dve.wait_ge(half_normed, 2 * u + 2)
                    dve.sem_inc(normed, 1)

                def unit(u, s, first=False, more=2):
                    n, o = u + 1, 1 - s
                    if more:
                        q_low(n, o, 0)
                    if not first:
                        norm(u - 1, o)
                    if more:
                        q_low(n, o, 1)
                    for i in range(2 * KT):
                        if i == 3 and not first and more:
                            k_copy(n, o)
                        if more:
                            row_max(n, o, i)
                    if more:
                        max_halves(n)
                    if not more:
                        for t in range(1, KT):
                            add_tile(dve, nc.vector, u, t)
                    if more == 2:
                        k_low(n + 1, s, 0)
                        v_bias(KT + 1 + u)
                        k_low(n + 1, s, 1)

                dve.wait_ge(consts_loaded, CONSTS_LOADED)
                k_low(0, 0, 0)
                for t in range(KT):
                    v_bias(t, first_v[t % len(first_v)])
                k_low(0, 0, 1)
                k_copy(0, 0)
                q_low(0, 0, 0)
                q_low(0, 0, 1)
                for i in range(2 * KT):
                    row_max(0, 0, i)
                max_halves(0)
                k_low(1, 1, 0)
                v_bias(KT)
                k_low(1, 1, 1)
                k_copy(1, 1)
                unit(0, 0, first=True)
                unit(1, 1)
                with dve.Fori(1, U // 2 - 1) as pr:
                    for s in range(2):
                        unit(2 * pr + s, s)
                unit(U - 2, 0, more=1)
                unit(U - 1, 1, more=0)
                norm(U - 1, 1)

            @block.gpsimd
            def _(pool):
                pool.sem_inc(summed, SUMS)
                pool.sem_inc(value_done, KT)
                pool.sem_inc(o_lo, 2)
                def out_lo(u, s, sums_so_far):
                    pool.wait_ge(summed, SUMS + sums_so_far)
                    pool.wait_ge(o_hi, u + 1)
                    rows_ = slice(DB * s, DB * (s + 1))
                    nc.gpsimd.tensor_tensor(OTl[rows_, ds(head(u) // 2, 1), ds(batch(u) * S, S)], O[rows_, None, :],
                                            OTh[rows_, ds(head(u) // 2, 1), ds(batch(u) * S, S)], ALU.subtract).then_inc(o_lo, 1)

                def unit(u, s, first=False, last=False):
                    for t in range(1, 4):
                        add_tile(pool, nc.gpsimd, u, t)
                    if not first:
                        out_lo(u - 1, 1 - s, SUMS * u + 3)
                        pool.wait_ge(o_lo, 2 + u)
                    for t in range(4, KT):
                        add_tile(pool, nc.gpsimd, u, t)

                nc.gpsimd.memset(ones[:], 1.0).then_inc(set_up, 1)
                pool.wait_ge(set_up, 1)
                nc.gpsimd.memset(K1[DB:P, :, :], 0.0).then_inc(set_up, 1)
                nc.gpsimd.memset(QL[DB:P, :, :], 0.0).then_inc(set_up, 1)
                pool.wait_ge(set_up, 3)
                nc.gpsimd.memset(K1[DB:DB + 2, :, :], 1.0).then_inc(set_up, 1)
                pool.wait_ge(set_up, 4)
                unit(0, 0, first=True)
                unit(1, 1)
                with pool.Fori(1, U // 2 - 1) as pr:
                    for s in range(2):
                        unit(2 * pr + s, s)
                unit(U - 2, 0)
                out_lo(U - 2, 0, SUMS * (U - 1))
                out_lo(U - 1, 1, SUMS * U)
                pool.wait_ge(o_lo, 2 + U)


def full_output(nc, X, OTh, OTl, woh, wol, bob, gb, bb, consts_loaded):
    with Stage(nc, "bo") as st:
        sb, ps, sem = st.sb, st.ps, st.sem
        g2, b2 = sb("g2", [P, D]), sb("b2", [P, D])
        seen = sb("seen", [P, 1])
        halfneg, epsc = sb("halfneg", [P, TPC]), sb("epsc", [P, TPC])
        stats, mv = sb("stats", [P, 2, TPC, 6]), sb("mv", [P, 2, TPC, 2])
        vare, rstd = sb("vare", [P, 2, TPC]), sb("rstd", [P, 2, TPC])
        y, yn = sb("y", [P, 2, TPC, D]), sb("yn", [P, 2, TPC, D])
        psY = [ps(f"psY{h}", [P, TPC, D]) for h in range(2)]

        set_up, scaled = sem("set_up"), sem("scaled")
        projected, biased = sem("projected"), sem("biased")
        bn_done, stats_ready, eps_added, rstd_ready = sem("bn_done"), sem("stats_ready"), sem("eps_added"), sem("rstd_ready")
        normed, gained, shifted, added = sem("normed"), sem("gained"), sem("shifted"), sem("added")

        wide = lambda a: a[:, None, :].broadcast_to([P, TPC, D])

        with st.block() as block:

            @block.tensor
            def _(pe):
                with pe.Fori(0, NCH // 2) as b:
                    for h in range(2):
                        c = 2 * b + h
                        pe.wait_ge(biased, 1 + 2 * b)
                        for j in range(TPC):
                            for m in range(HB // 2):
                                o = psY[h][:, j, :]
                                oh, ol = OTh[:, m, ds(c * CH + j * P, P)], OTl[:, m, ds(c * CH + j * P, P)]
                                nc.tensor.matmul(o, oh, woh[:, m, :], start=(m == 0), stop=False)
                                nc.tensor.matmul(o, oh, wol[:, m, :], start=False, stop=False)
                                ins = nc.tensor.matmul(o, ol, woh[:, m, :], start=False, stop=(m == HB // 2 - 1))
                        ins.then_inc(projected, 1)

            @block.vector
            def _(dve):
                dve.sem_inc(biased, 1)
                dve.sem_inc(normed, 1)
                def stats_of(c, h, first=False):
                    dve.wait_ge(projected, c + 1)
                    if not first:
                        dve.wait_ge(normed, c)
                    nc.vector.tensor_tensor(y[:, h], psY[h][:], wide(bob), ALU.add).then_inc(biased, 1)
                    dve.wait_ge(biased, 1 + c + 1)
                    for j in range(TPC):
                        nc.vector.bn_stats(stats[:, h, j, :], y[:, h, j, :]).then_inc(bn_done, 1)
                    dve.wait_ge(bn_done, TPC * c + TPC)
                    nc.vector.tensor_copy(seen[:], stats[:, h, TPC - 1, 0:1])
                    for j in range(TPC):
                        ins = nc.vector.bn_aggr(mv[:, h, j, :], stats[:, h, j, :])
                    ins.then_inc(stats_ready, 1)

                def normalise(c, h):
                    dve.wait_ge(rstd_ready, c + 1)
                    dve.wait_ge(added, 1 + 2 * (c // 2))
                    for j in range(TPC):
                        ins = nc.vector.tensor_scalar(yn[:, h, j, :], y[:, h, j, :], mv[:, h, j, 0:1],
                                                      rstd[:, h, j:j + 1], ALU.subtract, ALU.mult)
                    ins.then_inc(normed, 1)

                dve.wait_ge(consts_loaded, CONSTS_LOADED)
                nc.vector.tensor_scalar(g2[:], gb[:], RSQRT2, None, ALU.mult).then_inc(scaled, 1)
                nc.vector.tensor_scalar(b2[:], bb[:], RSQRT2, None, ALU.mult).then_inc(scaled, 1)
                dve.wait_ge(scaled, 2)
                nc.vector.tensor_tensor(X[:], X[:], b2[:, None, :].broadcast_to([P, NT, D]), ALU.add).then_inc(shifted, 1)
                stats_of(0, 0, first=True)
                with dve.Fori(0, NCH // 2 - 1) as b:
                    for h in range(2):
                        stats_of(2 * b + h + 1, 1 - h)
                        normalise(2 * b + h, h)
                stats_of(NCH - 1, 1)
                normalise(NCH - 2, 0)
                normalise(NCH - 1, 1)
                dve.wait_ge(added, 1 + NCH)

            @block.gpsimd
            def _(pool):
                pool.sem_inc(added, 1)
                nc.gpsimd.memset(halfneg[:], -0.5).then_inc(set_up, 1)
                nc.gpsimd.memset(epsc[:], EPS).then_inc(set_up, 1)
                pool.wait_ge(set_up, 2)

                def rstd_of(c, h):
                    pool.wait_ge(stats_ready, c + 1)
                    nc.gpsimd.tensor_tensor(vare[:, h], mv[:, h, :, 1], epsc[:], ALU.add).then_inc(eps_added, 1)
                    pool.wait_ge(eps_added, c + 1)
                    nc.gpsimd.tensor_tensor(rstd[:, h], vare[:, h], halfneg[:], ALU.pow).then_inc(rstd_ready, 1)

                def add(c, h):
                    pool.wait_ge(normed, 1 + c + 1)
                    nc.gpsimd.tensor_tensor(yn[:, h], yn[:, h], wide(g2), ALU.mult).then_inc(gained, 1)
                    pool.wait_ge(gained, c + 1)
                    nc.gpsimd.tensor_tensor(X[:, ds(TPC * c, TPC), :], yn[:, h], X[:, ds(TPC * c, TPC), :], ALU.add).then_inc(added, 1)

                rstd_of(0, 0)
                pool.wait_ge(scaled, 2)
                pool.wait_ge(shifted, 1)
                with pool.Fori(0, NCH // 2 - 1) as b:
                    for h in range(2):
                        rstd_of(2 * b + h + 1, 1 - h)
                        add(2 * b + h, h)
                rstd_of(NCH - 1, 1)
                add(NCH - 2, 0)
                add(NCH - 1, 1)


def transformer_layer(nc, io, out):
    X_ctx = ExitStack()
    with X_ctx:
        X = X_ctx.enter_context(nc.sbuf_tensor("X", [P, NT, D], F32))
        with Stage(nc, "band") as st:
            Q4 = st.sb("Q4", [P, 4, T], F16)
            K4 = st.sb("K4", [P, 4, WIN + T], F16)
            V = st.sb("V", [P, NB, 2, HA, VW], F16)
            qk = {(n, part): st.sb(f"{n}{part}", [P, T], F16) for n in "qk" for part in "hl"}
            qk_hi, qk_lo, stacked, batch_stacked = (st.sem(n) for n in ("qk_hi", "qk_lo", "stacked", "batch_stacked"))
            late = SecondPart(st)
            band_project(nc, X, Q4, K4, V, qk, qk_hi, qk_lo, stacked, batch_stacked, late, io)
            band_attend(nc, X, Q4, K4, V, qk, qk_hi, qk_lo, stacked, batch_stacked, late)
        experts(nc, X, io, "f1")
        full_attention(nc, X, io)
        experts(nc, X, io, "f2")
        with Stage(nc, "out") as st:
            stored = st.sem("stored")
            with st.block() as block:
                @block.sync
                def _(sp):
                    sp.dma_start(out.rearrange("b (t p) d -> p (b t) d", p=P), X[:]).then_inc(stored, 16)
                    sp.wait_ge(stored, 16)


def shape_constants():
    half = D // 2
    inv = (np.float32(1.0) / np.power(10000.0, np.arange(half) / half).astype(np.float32)).astype(np.float32)
    ang = (np.arange(S, dtype=np.float32)[:, None] * inv[None, :]).T
    c, s = np.cos(ang), np.sin(ang)
    q, k = np.arange(P)[:, None] % WIN, np.arange(P)[None, :]
    band = (k >= q) & (k <= q + WIN)
    row = np.arange(P)
    fold = np.zeros((P, 2, P), np.float32)
    for j in range(2):
        fold[row, j, WIN * j + row % WIN] = 1.0
    return {
        "cos": np.concatenate([c, c]).astype(np.float32),
        "sin": np.concatenate([-s, s]).astype(np.float32),
        "ident": np.eye(P, dtype=np.float32),
        "identh": np.eye(P, dtype=np.float16),
        "bandm": np.where(np.stack([band & (k >= WIN), band], 1), 0.0, -1e30).astype(np.float32),
        "headm": ((row[:, None] % 32) // DA == np.arange(4)[None, :]).astype(np.float16),
        "parm": (row[:, None] // WIN == np.arange(2)[None, :]).astype(np.float32),
        "fold": fold,
        "rank": np.broadcast_to((NE - np.arange(NE)).astype(np.float32), (P, NE)).copy(),
    }


def laid_out(a):
    f = {k: np.asarray(v) for k, v in a.items()}
    wq, wk, wv = f["L0_attn_a_Wq"], f["L0_attn_a_Wk"], f["L0_attn_a_Wv"]
    bq, bk = f["L0_attn_a_bq"], f["L0_attn_a_bk"]
    half = D // 2
    roll = lambda x: np.concatenate([x[half:], x[:half]])
    wqk = f["L0_attn_b_W_qk"].reshape(D, HB, DB, 2)
    bqk = f["L0_attn_b_b_qk"].reshape(HB, DB, 2)
    dup = lambda x: np.concatenate([x, x], axis=-1)
    c = np.ascontiguousarray
    return {
        "x": f["L0_attn_a_hidden_state"],
        "wA": c(np.stack([wq.T, roll(wq).T, wk.T, roll(wk).T, wv.T], axis=1)),
        "biasA": c(np.stack([bq, roll(bq), bk, roll(bk)], axis=1)),
        "bv": f["L0_attn_a_bv"],
        "woT": c(f["L0_attn_a_Wo"].T),
        "bo": f["L0_attn_a_bo"],
        "wqB": c(dup(wqk[..., 0])), "wkB": c(dup(wqk[..., 1])),
        "bqB": c(dup(bqk[..., 0]).T), "bkB": c(dup(bqk[..., 1]).T),
        "wvB": f["L0_attn_b_W_v"], "bvB": f["L0_attn_b_b_v"],
        "woutB": c(f["L0_attn_b_W_out"].reshape(HB // 2, 2 * DB, D).transpose(1, 0, 2)),
        "boutB": f["L0_attn_b_b_out"],
        "lngB": f["L0_attn_b_ln_gamma"], "lnbB": f["L0_attn_b_ln_beta"],
        "gammaF": c(f["L0_ffn_gamma"][:, None]), "betaF": c(f["L0_ffn_beta"][:, None]),
        "wrF": f["L0_ffn_Wr"], "brF": f["L0_ffn_br"],
        "w1F": c(f["L0_ffn_W1"].transpose(1, 0, 2)),
        "b1F": c(f["L0_ffn_b1"].reshape(NE, FC, P).transpose(2, 0, 1)),
        "w2F": c(f["L0_ffn_W2"].reshape(NE, FC, P, D).transpose(2, 0, 1, 3)),
        "b2F": c(f["L0_ffn_b2"].T),
        **shape_constants(),
    }


def kernel(**inputs):
    import concourse.bacc as bacc
    from concourse.bass_utils import run_bass_kernel_spmd

    nc = bacc.Bacc("TRN2", target_bir_lowering=False, num_devices=1)
    arrays = laid_out(inputs)
    io = {n: nc.dram_tensor(f"in_{n}", a.shape, mybir.dt.from_np(a.dtype), kind="ExternalInput").ap()
          for n, a in arrays.items()}
    out = nc.dram_tensor("out", (B, S, D), F32, kind="ExternalOutput").ap()
    transformer_layer(nc, io, out)
    r = run_bass_kernel_spmd(nc, [{f"in_{n}": a for n, a in arrays.items()}], core_ids=[0])
    return r.results[0]["out"]
```
